# Optimizing a Trainium2 kernel written in Bass

```python
import numpy as np
import jax
import jax.numpy as jnp

def _softmax(x, axis=-1):
    return jax.nn.softmax(x, axis=axis)

def _gelu(x):
    return jax.nn.gelu(x, approximate=True)

def _silu(x):
    return jax.nn.silu(x)

def _sigmoid(x):
    return jax.nn.sigmoid(x)

def _layernorm(x, axis=-1, eps=1e-05):
    m = jnp.mean(x, axis=axis, keepdims=True)
    v = jnp.var(x, axis=axis, keepdims=True)
    return (x - m) / jnp.sqrt(v + eps)

def _scatter_add(tgt, idx, src, axis=0):
    return tgt.at[idx].add(src)

def _segment_sum(src, seg, n):
    return jax.ops.segment_sum(src, seg, n)
kernel_name = 'mk_gnn_preln_d2_gnn_r32_d388da'

def setup_inputs(seed: int=0):
    np.random.seed(seed)
    _w = jnp.asarray

    def _rec_inputs():
        import jax
        import jax.numpy as jnp
        _gk = jax.random.key(seed)
        x = -0.000202 + 1 * jax.random.normal(jax.random.fold_in(_gk, 1), (50000, 128), jnp.float32)
        src = jax.random.randint(jax.random.fold_in(_gk, 2), (50000,), 0, 50000, jnp.int32)
        dst = jnp.minimum((50000 * jax.random.uniform(jax.random.fold_in(_gk, 3), (50000,)) ** 2.0).astype(jnp.int32), 49999)
        _o = jnp.argsort(dst, stable=True)
        src = src[_o]
        dst = dst[_o]
        return (x, src, dst)
    x, src, dst = _rec_inputs()

    def _L0_gnn_setup():
        import jax, jax.numpy as jnp
        import numpy as np
        N, E, F_IN, H, C = (50000, 25000, 128, 4, 32)
        NEG_SLOPE = 0.2
        key = jax.random.key(seed)
        k1, k2, k3, k4, k5, k6, k7 = jax.random.split(key, 7)
        nodes = jax.random.normal(k1, (N, F_IN), dtype=jnp.float32)
        senders = jax.random.randint(k2, (E,), 0, N, dtype=jnp.int32)
        receivers = jax.random.randint(k3, (E,), 0, N, dtype=jnp.int32)
        W = jax.random.normal(k4, (F_IN, H * C), dtype=jnp.float32) / np.sqrt(F_IN)
        b_lin = jnp.zeros((H * C,), dtype=jnp.float32)
        alpha = jax.random.normal(k5, (1, H, 2 * C), dtype=jnp.float32)
        bias = jnp.zeros((H * C,), dtype=jnp.float32)
        return {'nodes': nodes, 'senders': senders, 'receivers': receivers, 'W': W, 'b_lin': b_lin, 'alpha': alpha, 'bias': bias}
    _L0_gnn_all = _L0_gnn_setup()
    _L0_gnn_in = {k: v for k, v in _L0_gnn_all.items() if k in ('W', 'b_lin', 'alpha', 'bias')}
    del _L0_gnn_all

    def _L1_gnn_setup():
        import jax, jax.numpy as jnp
        import numpy as np
        N_NODES = 50000
        N_EDGES = 25000
        DIM = 128
        BN_EPS = 1e-05
        key = jax.random.key(seed)
        ks = jax.random.split(key, 12)
        d = DIM
        s = 1.0 / np.sqrt(d)
        x = jax.random.normal(ks[0], (N_NODES, d), dtype=jnp.float32)
        edge_index = jax.random.randint(ks[1], (2, N_EDGES), 0, N_NODES, dtype=jnp.int64)
        W_msg = jax.random.uniform(ks[2], (d, d), jnp.float32, -s, s)
        b_msg = jax.random.uniform(ks[3], (d,), jnp.float32, -s, s)
        sa = 1.0 / np.sqrt(2 * d)
        W_att = jax.random.uniform(ks[4], (2 * d, 1), jnp.float32, -sa, sa)
        b_att = jax.random.uniform(ks[5], (1,), jnp.float32, -sa, sa)
        W_ih = jax.random.uniform(ks[6], (3 * d, d), jnp.float32, -s, s)
        b_ih = jax.random.uniform(ks[7], (3 * d,), jnp.float32, -s, s)
        W_hh = jax.random.uniform(ks[8], (3 * d, d), jnp.float32, -s, s)
        b_hh = jax.random.uniform(ks[9], (3 * d,), jnp.float32, -s, s)
        gamma = jnp.ones((d,), jnp.float32)
        beta = jnp.zeros((d,), jnp.float32)
        return {'x': x, 'edge_index': edge_index, 'W_msg': W_msg, 'b_msg': b_msg, 'W_att': W_att, 'b_att': b_att, 'W_ih': W_ih, 'b_ih': b_ih, 'W_hh': W_hh, 'b_hh': b_hh, 'gamma': gamma, 'beta': beta}
    _L1_gnn_all = _L1_gnn_setup()
    _L1_gnn_in = {k: v for k, v in _L1_gnn_all.items() if k in ('W_msg', 'b_msg', 'W_att', 'b_att', 'W_ih', 'b_ih', 'W_hh', 'b_hh', 'gamma', 'beta')}
    del _L1_gnn_all
    return {'x': x, 'src': src, 'dst': dst, 'L0_gnn_W': _L0_gnn_in['W'], 'L0_gnn_b_lin': _L0_gnn_in['b_lin'], 'L0_gnn_alpha': _L0_gnn_in['alpha'], 'L0_gnn_bias': _L0_gnn_in['bias'], 'L1_gnn_W_msg': _L1_gnn_in['W_msg'], 'L1_gnn_b_msg': _L1_gnn_in['b_msg'], 'L1_gnn_W_att': _L1_gnn_in['W_att'], 'L1_gnn_b_att': _L1_gnn_in['b_att'], 'L1_gnn_W_ih': _L1_gnn_in['W_ih'], 'L1_gnn_b_ih': _L1_gnn_in['b_ih'], 'L1_gnn_W_hh': _L1_gnn_in['W_hh'], 'L1_gnn_b_hh': _L1_gnn_in['b_hh'], 'L1_gnn_gamma': _L1_gnn_in['gamma'], 'L1_gnn_beta': _L1_gnn_in['beta']}

def reference(x, src, dst, L0_gnn_W, L0_gnn_b_lin, L0_gnn_alpha, L0_gnn_bias, L1_gnn_W_msg, L1_gnn_b_msg, L1_gnn_W_att, L1_gnn_b_att, L1_gnn_W_ih, L1_gnn_b_ih, L1_gnn_W_hh, L1_gnn_b_hh, L1_gnn_gamma, L1_gnn_beta):
    import jax
    import jax.numpy as jnp

    def _L0_gnn_ref(nodes, senders, receivers, W, b_lin, alpha, bias):
        import jax, jax.numpy as jnp
        import numpy as np
        N, E, F_IN, H, C = (50000, 25000, 128, 4, 32)
        NEG_SLOPE = 0.2
        n = nodes.shape[0]
        x = nodes @ W + b_lin
        loop = jnp.arange(n, dtype=senders.dtype)
        snd = jnp.concatenate([senders, loop])
        rcv = jnp.concatenate([receivers, loop])
        sent = x[snd]
        recvd = x[rcv]
        feat = jnp.concatenate([sent, recvd], axis=1).reshape(-1, H, 2 * C)
        logits = jnp.sum(feat * alpha, axis=-1)
        logits = jax.nn.leaky_relu(logits, negative_slope=NEG_SLOPE)
        seg_max = jax.ops.segment_max(logits, rcv, num_segments=n)
        e = jnp.exp(logits - seg_max[rcv])
        denom = jax.ops.segment_sum(e, rcv, num_segments=n)
        att = e / denom[rcv]
        msgs = att[:, :, None] * sent.reshape(-1, H, C)
        out = jax.ops.segment_sum(msgs, rcv, num_segments=n)
        out = out.reshape(-1, H * C)
        out = out + bias
        return out

    def _L1_gnn_ref(x, edge_index, W_msg, b_msg, W_att, b_att, W_ih, b_ih, W_hh, b_hh, gamma, beta):
        import jax, jax.numpy as jnp
        import numpy as np
        N_NODES = 50000
        N_EDGES = 25000
        DIM = 128
        BN_EPS = 1e-05
        num_nodes, d = x.shape
        src = edge_index[0]
        dst = edge_index[1]
        xs = x[src]
        xd = x[dst]
        att = jax.nn.sigmoid(xs @ W_att[:d] + xd @ W_att[d:] + b_att)
        messages = (xs @ W_msg + b_msg) * att
        aggregated = jax.ops.segment_sum(messages, dst, num_segments=num_nodes)
        gi = aggregated @ W_ih.T + b_ih
        gh = x @ W_hh.T + b_hh
        i_r, i_z, i_n = jnp.split(gi, 3, axis=1)
        h_r, h_z, h_n = jnp.split(gh, 3, axis=1)
        r = jax.nn.sigmoid(i_r + h_r)
        z = jax.nn.sigmoid(i_z + h_z)
        n = jnp.tanh(i_n + r * h_n)
        h_new = (1.0 - z) * n + z * x
        mean = jnp.mean(h_new, axis=0)
        var = jnp.var(h_new, axis=0)
        return gamma * (h_new - mean) * jax.lax.rsqrt(var + BN_EPS) + beta
    edge_index = jnp.stack([src, dst])
    h = jnp.maximum(_layernorm(x, axis=-1), 0.0)
    x = x + _L0_gnn_ref(h, src, dst, L0_gnn_W, L0_gnn_b_lin, L0_gnn_alpha, L0_gnn_bias)
    h = jnp.maximum(_layernorm(x, axis=-1), 0.0)
    x = x + _L1_gnn_ref(h, edge_index, L1_gnn_W_msg, L1_gnn_b_msg, L1_gnn_W_att, L1_gnn_b_att, L1_gnn_W_ih, L1_gnn_b_ih, L1_gnn_W_hh, L1_gnn_b_hh, L1_gnn_gamma, L1_gnn_beta)
    return x

_drawn_inputs = setup_inputs


def setup_inputs(seed=0):
    import zlib

    import numpy as np

    out = dict(_drawn_inputs(seed))
    spreads = {'L0_gnn_b_lin': (0.0, 0.1),
     'L0_gnn_bias': (0.0, 0.1),
     'L1_gnn_gamma': (1.0, 0.2),
     'L1_gnn_beta': (0.0, 0.1)}
    factors = {'L1_gnn_b_msg': 3.284, 'L1_gnn_W_att': 2.893, 'L1_gnn_b_ih': 4.665, 'L1_gnn_b_hh': 5.158}
    for name, (base, spread) in spreads.items():
        noise = np.random.default_rng([zlib.crc32(name.encode()), seed]).standard_normal(out[name].shape)
        drawn = base * np.exp(spread * noise) if base else spread * noise
        out[name] = jnp.asarray(drawn.astype(out[name].dtype))
    for name, factor in factors.items():
        out[name] = (out[name] * factor).astype(out[name].dtype)
    return out
```

```python
import concourse.bass as bass
from concourse import mybir
from contextlib import ExitStack

P = 128
N = 50000
E = 50000
T = 512
K = T // P
NG = -(-E // T)
NT = NG * K
CH = 4
CT = NT // CH
H = 4
ROW = P + 2 * H
LAST = N - T
FRESH = (NG * T - N) // K
PAD = 70000.0
NOWHERE = 60000.0
BIG = 1e30
EPS = 1e-5
SLOPE = 0.2


def wait(eng, sem, count):
    if not (isinstance(count, int) and count <= 0):
        eng.wait_ge(sem, count)


def staged(eng, depth, body):
    head = depth + 2 + depth % 2
    for i in range(head):
        body(i, i % 2)
    end = NG - 2
    with eng.Fori(0, (end - head) // 2) as turn:
        body(turn * 2 + head, 0)
        body(turn * 2 + (head + 1), 1)
    for i in range(end, NG + depth):
        body(i, i % 2)


def live(g):
    return not isinstance(g, int) or 0 <= g < NG


def node_rows(g):
    if isinstance(g, int):
        return min(g * T, LAST)
    return g * T


class Shared:
    pass


def build(nc, io, scratch):
    v = Shared()
    v.io = io
    v.f32, v.i32, v.bf16 = mybir.dt.float32, mybir.dt.int32, mybir.dt.bfloat16
    v.ACT, v.ALU, v.AX = mybir.ActivationFunctionType, mybir.AluOpType, mybir.AxisListType
    v.acc0, v.acc1, v.x1_d, v.h1_d, v.s2_d, v.same_d, v.start_d, v.hn_d = (
        scratch[n] for n in ("acc0", "acc1", "x1", "h1", "s2", "same", "start", "hnew"))
    v.x_d, v.out_d = io["x"], io["out"]
    v.src_s, v.dst_s = scratch["src_s"], scratch["dst_s"]
    v.src_sorted, v.dst_sorted = (a[:, :].rearrange("n a -> (n a)") for a in (v.src_s, v.dst_s))

    with ExitStack() as whole:
        def keep(name, shape, dt=v.f32):
            return whole.enter_context(nc.sbuf_tensor(name, shape, dt))

        v.ident = keep("ident", [P, P])
        v.ones = keep("ones", [1, P])
        v.zeros = keep("zeros", [P, 2125])
        v.ones16 = keep("ones16", [1, P], v.bf16)
        v.w_ext = keep("w_ext", [P, P + H])
        v.b_ext = keep("b_ext", [1, P + H])
        v.alpha = keep("alpha", [P, H])
        v.alpha_all = keep("alpha_all", [P, P])
        v.b_lin = keep("b_lin", [P, 1])
        v.bias_all = keep("bias_all", [P, P])
        v.w_msg = keep("w_msg", [P, P])
        v.b_msg = keep("b_msg", [P, 1])
        v.w_att1 = keep("w_att1", [P, 1])
        v.w_att2_all = keep("w_att2_all", [P, P])
        v.b_att = keep("b_att", [P, 1])
        v.minus_b_att = keep("minus_b_att", [P, 1])
        v.w_ihT = keep("w_ihT", [P, 3 * P])
        v.w_hhT = keep("w_hhT", [P, 3 * P])
        v.b_ih = keep("b_ih", [P, 3])
        v.b_hh = keep("b_hh", [P, 3])
        v.b_gate = keep("b_gate", [P, 2])
        v.gamma = keep("gamma", [P, 1])
        v.beta = keep("beta", [P, 1])
        v.eps = keep("eps", [P, 1])
        v.src_idx = keep("src_idx", [P, NT], v.i32)
        v.dst_idx = keep("dst_idx", [P, NT], v.i32)
        v.put_idx = keep("put_idx", [P, NT], v.i32)
        v.stats = keep("stats", [P, NG, 6])

        v.tick = whole.enter_context(nc.semaphore("tick"))

        order(nc, v)
        prepare(nc, v)
        edges0(nc, v)
        nodes0(nc, v)
        edges1(nc, v)
        nodes1(nc, v)
        finish(nc, v)


def order(nc, v):
    f32, i32, ALU, AX = v.f32, v.i32, v.ALU, v.AX
    src, dst = v.io["src"], v.io["dst"]
    with ExitStack() as ctx:
        def sb(name, shape, dt=f32):
            return ctx.enter_context(nc.sbuf_tensor(name, shape, dt))

        def sem(name):
            return ctx.enter_context(nc.semaphore(name))

        W = 390
        B = NT * P // 8
        near = sb("o_near", [P, 2, 2, W], i32)
        falls = sb("o_falls", [P, 2, W])
        fell = sb("o_fell", [P, 1])
        fell_all = sb("o_fell_all", [1, 1], i32)
        ones_col = sb("o_ones", [P, 1])
        ps = ctx.enter_context(nc.psum_tensor("o_ps", [1, 512], f32))
        cols = sb("o_cols", [P, 2, NT], i32)
        key = sb("o_key", [P, 2, NT])
        one = sb("o_one", [P, 2])
        number = sb("o_number", [P, NT], i32)
        along = sb("o_along", [P, B], i32)
        alongf = sb("o_alongf", [P, B])
        rowi = sb("o_rowi", [P, B], i32)
        rowf = sb("o_rowf", [P, B])
        before = sb("o_before", [P, B])
        count = sb("o_count", [P, 1])
        rank = sb("o_rank", [P, NT])
        ranki = sb("o_ranki", [P, NT], i32)
        at = sb("o_at", [P, 3], i32)
        copied, near_in, fell_done, summed, told = (sem(f"o_{n}") for n in (
            "copied", "near_in", "fell_done", "summed", "told"))
        blank, cols_in, numbers, row_in, row_used, ranked, picked, placed = (sem(f"o_{n}") for n in (
            "blank", "cols_in", "numbers", "row_in", "row_used", "ranked", "picked", "placed"))
        block = ctx.enter_context(nc.Block())

        @block.sync
        def _(sp):
            for first in (0, E - 1 - P * W):
                for shift in range(2):
                    a = first + shift
                    sp.dma_start(near[:, min(first, 1), shift, :], dst[a:a + P * W].rearrange("(p w) -> p w", p=P))\
                      .then_inc(near_in, 16)
            for out, array in ((v.src_s, src), (v.dst_s, dst)):
                sp.dma_start(out[:, :].rearrange("(p w) a -> p (w a)", p=80), array.rearrange("(p w) -> p w", p=80))\
                  .then_inc(copied, 16)
            sp.wait_ge(copied, 32)
            sp.wait_ge(told, 1)
            wrong = sp.value_load(fell_all[0:1, 0:1], min_val=0, max_val=E)
            with sp.If(wrong > 0):
                sp.wait_ge(blank, 1)
                for a, array in enumerate((dst, src)):
                    whole = E // P
                    with nc.allow_non_contiguous_dma(reason="only for edges that come unordered"):
                        sp.dma_start(cols[:, a, 0:whole], array[0:whole * P].rearrange("(t p) -> p t", p=P))\
                          .then_inc(cols_in, 16)
                        sp.dma_start(cols[0:E % P, a, whole:whole + 1],
                                     array[whole * P:E].rearrange("(p t) -> p t", t=1)).then_inc(cols_in, 16)

                def row(b, width):
                    sp.dma_start(rowi[:, 0:width], dst[bass.ds(b * B, width)].rearrange("(a n) -> a n", a=1)
                                 .broadcast_to([P, width])).then_inc(row_in, 16)

                row(0, B)
                with sp.Fori(0, 6) as b:
                    sp.wait_ge(row_used, b + 1)
                    row(b + 1, B)
                sp.wait_ge(row_used, 8)
                row(7, E - 7 * B)

        @block.vector
        def _(dve):
            dve.memset(ones_col[:, :], 1.0).then_inc(fell_done, 1)
            dve.wait_ge(near_in, 64)
            dve.tensor_tensor(falls[:, :, :], near[:, :, 0, :], near[:, :, 1, :], ALU.is_gt)
            dve.drain()
            dve.tensor_reduce(out=fell[:, :], in_=falls[:, :, :].rearrange("p a w -> p (a w)"), axis=AX.X, op=ALU.add)\
               .then_inc(fell_done, 1)
            dve.wait_ge(summed, 1)
            dve.tensor_scalar(fell_all[0:1, 0:1], ps[0:1, 0:1], float(E), None, ALU.min).then_inc(told, 1)
            dve.wait_ge(told, 1)
            wrong = dve.value_load(fell_all[0:1, 0:1], min_val=0, max_val=E)
            with dve.If(wrong > 0):
                dve.memset(cols[:, 0, :], int(PAD))
                dve.memset(cols[:, 1, :], 0).then_inc(blank, 1)
                dve.memset(rank[:, :], 0.0)
                dve.wait_ge(numbers, 2)
                dve.wait_ge(cols_in, 64)
                dve.tensor_copy(alongf[:, :], along[:, :])
                dve.tensor_copy(key[:, 1, :], number[:, :])
                dve.tensor_scalar(key[:, 0, :], cols[:, 0, :], 65536.0, None, ALU.mult)

                def block_of_edges(b):
                    dve.wait_ge(row_in, b * 16 + 16)
                    dve.tensor_scalar(rowf[:, :], rowi[:, :], 65536.0, None, ALU.mult)
                    dve.drain()
                    dve.sem_inc(row_used, 1)
                    with dve.Fori(0, NT) as t:
                        dve.tensor_copy(one[:, :], key[:, :, bass.ds(t, 1)].rearrange("p a t -> p (a t)"))
                        dve.drain()
                        dve.scalar_tensor_tensor(out=before[:, :], in0=rowf[:, :], scalar=one[:, 0:1], in1=alongf[:, :],
                                                 op0=ALU.subtract, op1=ALU.add)
                        dve.drain()
                        dve.tensor_scalar(before[:, :], before[:, :], one[:, 1:2], 0.0, ALU.is_lt, ALU.add,
                                          accum_out=count[:, :])
                        dve.drain()
                        dve.tensor_tensor(rank[:, bass.ds(t, 1)], rank[:, bass.ds(t, 1)], count[:, :], ALU.add)
                    dve.drain()
                    dve.tensor_scalar(key[:, 1, :], key[:, 1, :], float(B), None, ALU.subtract)
                    dve.drain()

                dve.drain()
                with dve.Fori(0, 7) as b:
                    block_of_edges(b)
                dve.memset(rowi[:, E - 7 * B:B], int(PAD)).then_inc(row_used, 1)
                dve.wait_ge(row_used, 8)
                block_of_edges(7)
                dve.tensor_copy(ranki[:, :], rank[:, :]).then_inc(ranked, 1)

        @block.tensor
        def _(pe):
            pe.wait_ge(fell_done, 2)
            pe.matmul(ps[0:1, 0:1], fell[:, :], ones_col[:, :], start=True, stop=True).then_inc(summed, 1)

        @block.gpsimd
        def _(pool):
            pool.wait_ge(told, 1)
            wrong = pool.value_load(fell_all[0:1, 0:1], min_val=0, max_val=E)
            with pool.If(wrong > 0):
                pool.iota(along[:, :], pattern=[[1, B]], base=0, channel_multiplier=0).then_inc(numbers, 1)
                pool.iota(number[:, :], pattern=[[P, NT]], base=0, channel_multiplier=1).then_inc(numbers, 1)
                bound = pool.to_reg(E - 1)
                pool.wait_ge(copied, 32)
                pool.wait_ge(cols_in, 64)
                pool.wait_ge(ranked, 1)
                pool.sem_inc(v.tick, 1)
                with pool.Fori(0, NT) as t:
                    pool.tensor_copy(at[:, 0:1], ranki[:, bass.ds(t, 1)])
                    pool.tensor_copy(at[:, 1:3], cols[:, :, bass.ds(t, 1)].rearrange("p a t -> p (a t)"))\
                        .then_inc(picked, 1)
                    pool.wait_ge(picked, t + 1)
                    pool.sem_inc(v.tick, 1)
                    for a, out in ((1, v.dst_s), (2, v.src_s)):
                        pool.indirect_dma_start(out=out[:, :], out_offset=bass.IndirectOffsetOnAxis(ap=at[:, 0:1], axis=0),
                                                in_=at[:, a:a + 1], in_offset=None, bounds_check=bound, oob_is_err=False)\
                            .then_inc(placed, 16)
                    pool.wait_ge(placed, t * 32 + 32)
                    pool.sem_inc(v.tick, 1)


def prepare(nc, v):
    f32, i32, ALU = v.f32, v.i32, v.ALU
    io = v.io
    with ExitStack() as ctx:
        def sb(name, shape, dt=f32):
            return ctx.enter_context(nc.sbuf_tensor(name, shape, dt))

        def sem(name):
            return ctx.enter_context(nc.semaphore(name))

        raw = [sb(f"raw_{n}", [CT, CH, P], i32) for n in ("src", "dst", "prev", "next")]
        flt = [sb(f"flt_{n}", [CT, CH, P]) for n in ("src", "dst", "prev", "next")]
        same = sb("same", [CT, CH, P])
        same16 = sb("same16", [CT, CH, P], v.bf16)
        start = sb("start", [CT, CH, P], v.bf16)
        ends = sb("ends", [CT, CH, P])
        put = sb("put", [CT, CH, P])
        inside = sb("inside", [CT, CH, P])
        w_ih = sb("w_ih", [P, 3, P])
        w_hh = sb("w_hh", [P, 3, P])
        wT = sb("wT", [P, P])
        ps_t = ctx.enter_context(nc.psum_tensor("ps_t", [P, 3, 512], f32))
        ps_w = ctx.enter_context(nc.psum_tensor("ps_w", [P, 2, 512], f32))
        ps_a = ctx.enter_context(nc.psum_tensor("ps_a", [P, 3, 512], f32))

        weights_in, edges_in, filled, cleared = sem("weights_in"), sem("edges_in"), sem("filled"), sem("cleared")
        zeros_set, raw_set, consts, consts2, flt_ready = sem("zeros_set"), sem("raw_set"), sem("consts"), sem("consts2"), sem("flt_ready")
        chain, tables, tables_out = sem("chain"), sem("tables"), sem("tables_out")
        edges_T, weights_T, wT_ready, folded, bfold = (sem(n) for n in ("edges_T", "weights_T", "wT_ready", "folded", "bfold"))
        idx_done, alpha_zero, alpha_in, w_in, gates = (sem(n) for n in ("idx_done", "alpha_zero", "alpha_in", "w_in", "gates"))
        block = ctx.enter_context(nc.Block())
        full = (E // P) - (CH - 1) * CT
        rest = E % P
        weight_loads = [0]

        @block.sync
        def _(sp):
            sp.wait_ge(raw_set, 1)
            n = 0

            def load(dst, src):
                sp.dma_start(dst, src).then_inc(edges_in, 16)

            def rows(a, lo, count):
                return a[lo:lo + count * P].rearrange("(t p) -> t p", p=P)

            for a, (buf, array) in enumerate(((raw[0], v.src_sorted), (raw[1], v.dst_sorted))):
                for c in range(CH - 1):
                    load(buf[:, c, :], rows(array, c * CT * P, CT))
                load(buf[0:full, CH - 1, :], rows(array, (CH - 1) * CT * P, full))
                load(buf[full:full + 1, CH - 1, 0:rest], array[E - rest:E].rearrange("(a n) -> a n", a=1))
            load(raw[2][0:1, 0, 1:P], v.dst_sorted[0:P - 1].rearrange("(a n) -> a n", a=1))
            load(raw[2][1:CT, 0, :], rows(v.dst_sorted, P - 1, CT - 1))
            for c in range(1, CH - 1):
                load(raw[2][:, c, :], rows(v.dst_sorted, c * CT * P - 1, CT))
            load(raw[2][0:full, CH - 1, :], rows(v.dst_sorted, (CH - 1) * CT * P - 1, full))
            load(raw[2][full:full + 1, CH - 1, 0:rest], v.dst_sorted[E - rest - 1:E - 1].rearrange("(a n) -> a n", a=1))
            for c in range(CH - 1):
                load(raw[3][:, c, :], rows(v.dst_sorted, c * CT * P + 1, CT))
            load(raw[3][0:full, CH - 1, :], rows(v.dst_sorted, (CH - 1) * CT * P + 1, full))
            load(raw[3][full:full + 1, CH - 1, 0:rest - 1], v.dst_sorted[E - rest + 1:E].rearrange("(a n) -> a n", a=1))
            sp.wait_ge(tables, 2)
            for table, t in ((v.same_d, same16), (v.start_d, start)):
                sp.dma_start(table[:].rearrange("(c t p) -> t c p", c=CH, t=CT), t[:, :, :]).then_inc(tables_out, 16)
            sp.wait_ge(tables_out, 32)
            sp.wait_ge(cleared, 16 * 25)

        @block.scalar
        def _(act):
            def load(dst, src):
                weight_loads[0] += 1
                act.dma_start(dst, src).then_inc(weights_in, 16)

            def column(a):
                return a.rearrange("(p a) -> p a", a=1)

            load(v.w_ext[:, 0:P], io["L0_gnn_W"])
            load(v.b_lin[:, :], column(io["L0_gnn_b_lin"]))
            load(v.b_ext[:, 0:P], io["L0_gnn_b_lin"].rearrange("(a n) -> a n", a=1))
            load(v.bias_all[:, :], io["L0_gnn_bias"].rearrange("(a n) -> a n", a=1).broadcast_to([P, P]))
            load(v.w_msg[:, :], io["L1_gnn_W_msg"])
            load(v.b_msg[:, :], column(io["L1_gnn_b_msg"]))
            load(v.w_att1[:, :], io["L1_gnn_W_att"][0:P, :])
            load(v.w_att2_all[:, :], io["L1_gnn_W_att"][P:2 * P, :].rearrange("n a -> a n").broadcast_to([P, P]))
            load(v.b_att[:, :], io["L1_gnn_b_att"].rearrange("(a n) -> a n", a=1).broadcast_to([P, 1]))
            load(w_ih[:, :, :], io["L1_gnn_W_ih"].rearrange("(c r) k -> r c k", c=3))
            load(w_hh[:, :, :], io["L1_gnn_W_hh"].rearrange("(c r) k -> r c k", c=3))
            for c in range(3):
                load(v.b_ih[:, c:c + 1], column(io["L1_gnn_b_ih"][c * P:(c + 1) * P]))
                load(v.b_hh[:, c:c + 1], column(io["L1_gnn_b_hh"][c * P:(c + 1) * P]))
            load(v.gamma[:, :], column(io["L1_gnn_gamma"]))
            load(v.beta[:, :], column(io["L1_gnn_beta"]))
            act.wait_ge(alpha_zero, 1)
            for h in range(2):
                load(v.alpha[64 * h:64 * h + 64, h:h + 1], io["L0_gnn_alpha"][0, h, :].rearrange("(p a) -> p a", a=1))
            act.wait_ge(zeros_set, 1)
            clear = v.acc0[:, :].rearrange("n d -> (n d)").rearrange("(p c) -> p c", p=P)
            for j in range(25):
                act.dma_start(clear[:, j * 2125:(j + 1) * 2125], v.zeros[:, :]).then_inc(cleared, 16)

        @block.gpsimd
        def _(pool):
            pool.memset(v.ident[:, :], 0.0).then_inc(consts, 1)
            pool.wait_ge(consts, 1)
            pool.affine_select(out=v.ident[:, :], in_=v.ident[:, :], compare_op=ALU.not_equal, fill=1.0, base=0,
                               pattern=[[-1, P]], channel_multiplier=1).then_inc(consts2, 1)

        @block.vector
        def _(dve):
            links = [0]

            def link(ins):
                links[0] += 1
                ins.then_inc(chain, 1)
                dve.wait_ge(chain, links[0])

            dve.memset(raw[0][:, :, :], 0)
            dve.memset(raw[1][:, :, :], int(PAD))
            dve.memset(raw[3][:, :, :], int(PAD))
            link(dve.memset(raw[2][:, :, :], int(PAD)))
            dve.memset(raw[2][0:1, 0, 0:1], -1).then_inc(raw_set, 1)
            dve.memset(v.alpha[:, :], 0.0).then_inc(alpha_zero, 1)
            dve.memset(v.zeros[:, :], 0.0).then_inc(zeros_set, 1)
            dve.memset(v.ones[:, :], 1.0)
            dve.memset(v.ones16[:, :], 1.0)
            dve.memset(v.alpha_all[:, :], 0.0)
            dve.memset(v.eps[:, :], EPS)
            dve.wait_ge(edges_in, 16 * (2 * (CH + 1) + (CH + 2) + (CH + 1)))
            dve.tensor_copy(flt[3][:, :, :], raw[3][:, :, :])
            dve.tensor_copy(flt[2][:, :, :], raw[2][:, :, :])
            dve.tensor_copy(flt[0][:, :, :], raw[0][:, :, :])
            link(dve.tensor_copy(flt[1][:, :, :], raw[1][:, :, :]))
            link(dve.tensor_tensor(same[:, :, :], flt[1][:, :, :], flt[2][:, :, :], ALU.is_equal))
            dve.tensor_copy(same16[:, :, :], same[:, :, :])
            dve.tensor_scalar(start[:, :, :], same[:, :, :], 1.0, BIG, ALU.subtract, ALU.mult).then_inc(tables, 2)
            dve.tensor_tensor(ends[:, :, :], flt[1][:, :, :], flt[3][:, :, :], ALU.not_equal)
            link(dve.tensor_scalar(put[:, :, :], flt[1][:, :, :], NOWHERE, None, ALU.subtract))
            link(dve.tensor_tensor(put[:, :, :], put[:, :, :], ends[:, :, :], ALU.mult))
            dve.tensor_scalar(put[:, :, :], put[:, :, :], NOWHERE, None, ALU.add)
            dve.tensor_scalar(inside[:, :, :], flt[1][:, :, :], float(N - 1), None, ALU.min).then_inc(flt_ready, 1)
            dve.wait_ge(weights_in, 16 * weight_loads[0])
            dve.tensor_tensor(v.b_gate[:, :], v.b_ih[:, 0:2], v.b_hh[:, 0:2], ALU.add)
            dve.tensor_scalar(v.minus_b_att[:, :], v.b_att[:, :], -1.0, None, ALU.mult)
            for h in range(2):
                dve.tensor_copy(v.alpha_all[:, h * (P // H):(h + 1) * (P // H)],
                                v.alpha[:, h:h + 1].broadcast_to([P, P // H]))
            dve.wait_ge(edges_T, 1)
            for a, t in enumerate((v.src_idx, v.dst_idx, v.put_idx)):
                dve.tensor_copy(t[:, :], ps_t[:, a, 0:NT])
            dve.wait_ge(weights_T, 1)
            dve.tensor_copy(v.w_ihT[:, :], ps_w[:, 0, 0:3 * P])
            dve.tensor_copy(v.w_hhT[:, :], ps_w[:, 1, 0:3 * P])
            dve.tensor_copy(wT[:, :], ps_a[:, 0, 0:P]).then_inc(wT_ready, 1)
            dve.wait_ge(folded, 1)
            dve.tensor_copy(v.w_ext[:, P:P + H], ps_a[:, 1, 0:H])
            dve.tensor_copy(v.b_ext[:, P:P + H], ps_a[0:1, 2, 0:H])

        @block.tensor
        def _(pe):
            pe.wait_ge(consts2, 1)
            pe.wait_ge(flt_ready, 1)
            for a, t in enumerate((flt[0], inside, put)):
                for c in range(CH):
                    last = pe.transpose(ps_t[:, a, c * CT:(c + 1) * CT], t[:, c, :], v.ident[0:CT, 0:CT])
            last.then_inc(edges_T, 1)
            pe.wait_ge(weights_in, 16 * weight_loads[0])
            for c in range(3):
                pe.transpose(ps_w[:, 0, c * P:(c + 1) * P], w_ih[:, c, :], v.ident[:, :])
                pe.transpose(ps_w[:, 1, c * P:(c + 1) * P], w_hh[:, c, :], v.ident[:, :])
            pe.transpose(ps_a[:, 0, 0:P], v.w_ext[:, 0:P], v.ident[:, :]).then_inc(weights_T, 1)
            pe.wait_ge(wT_ready, 1)
            pe.matmul(ps_a[:, 1, 0:H], wT[:, :], v.alpha[:, :], start=True, stop=True)
            pe.matmul(ps_a[0:1, 2, 0:H], v.b_lin[:, :], v.alpha[:, :], start=True, stop=True).then_inc(folded, 1)


def edges0(nc, v):
    f32, i32, ALU, ACT = v.f32, v.i32, v.ALU, v.ACT
    with ExitStack() as ctx:
        def sb(name, shape, dt=f32):
            return ctx.enter_context(nc.sbuf_tensor(name, shape, dt))

        def pb(name, shape):
            return ctx.enter_context(nc.psum_tensor(name, shape, f32))

        def sem(name):
            return ctx.enter_context(nc.semaphore(name))

        gi = sb("e0_gi", [P, 2, K], i32)
        si = sb("e0_si", [P, 2, K], i32)
        xg = sb("e0_xg", [P, 2, K, P])
        bst = sb("e0_bst", [P, K, 6])
        mv = sb("e0_mv", [P, K, 2])
        lnv = sb("e0_lnv", [P, K])
        rstd = sb("e0_rstd", [P, K])
        z = sb("e0_z", [P, 2, K, P])
        hT = sb("e0_hT", [P, T])
        xw = sb("e0_xw", [P, 2, T])
        raw_l = sb("e0_raw_l", [P, T])
        L = sb("e0_L", [P, T])
        start = sb("e0_start", [1, 2, T], v.bf16)
        M = sb("e0_M", [P, 2, T + 1])
        keepf = sb("e0_keepf", [P, T])
        y = sb("e0_y", [P, T])
        S = sb("e0_S", [P, 2, T])
        D = sb("e0_D", [P, 2, T])
        row = sb("e0_row", [P, 2, K, ROW])
        ps_z, ps_x, ps_l, ps_a, ps_b = (pb(f"e0_ps{n}", [P, T]) for n in "zxlab")
        ps_S, ps_D, ps_M = (pb(f"e0_ps{n}", [P, K, P]) for n in "SDM")

        idx_copied = sem("e0_idx_copied")
        got = [sem("e0_got0"), sem("e0_got1")]
        start_in = [sem("e0_start_in0"), sem("e0_start_in1")]
        put = [sem("e0_put0"), sem("e0_put1")]
        stats_done, aggr_done, ln_done, rstd_done, z_done = (sem(f"e0_{n}") for n in ("stats", "aggr", "ln", "rstd", "z"))
        zT_done, relu_done, w_done, xw_done, l_done, L_done, M_done = (sem(f"e0_{n}") for n in ("zT", "relu", "w", "xw", "l", "L", "M"))
        arg_done, exp_done, y_done, S_done, D_done, back_done, row_done = (sem(f"e0_{n}") for n in ("arg", "exp", "y", "S", "D", "back", "row"))
        put_copied, acc1_clear, raw_done = sem("e0_put_copied"), sem("e0_acc1_clear"), sem("e0_raw")
        start_done, u_done = sem("e0_start"), sem("e0_u")
        block = ctx.enter_context(nc.Block())
        DEPTH = 4

        @block.gpsimd
        def _(pool):
            bound = pool.to_reg(N - 1)

            def body(i, par):
                g = i
                if live(g):
                    s = par
                    wait(pool, z_done, g - 1)
                    pool.tensor_copy(gi[:, s, :], v.src_idx[:, bass.ds(g * K, K)]).then_inc(idx_copied, 1)
                    pool.wait_ge(idx_copied, g + 1)
                    pool.sem_inc(v.tick, 1)
                    for k in range(K):
                        pool.indirect_dma_start(out=xg[:, s, k, :], out_offset=None, in_=v.x_d[:, :],
                                                in_offset=bass.IndirectOffsetOnAxis(ap=gi[:, s, k:k + 1], axis=0),
                                                bounds_check=bound, oob_is_err=False).then_inc(got[s], 16)
                g = i - 4
                if live(g):
                    s = par
                    wait(pool, put[s], (g - s) * (8 * K))
                    pool.tensor_copy(si[:, s, :], v.put_idx[:, bass.ds(g * K, K)]).then_inc(put_copied, 1)
                    pool.wait_ge(put_copied, g + 1)
                    pool.sem_inc(v.tick, 1)
                    pool.wait_ge(row_done, g + 1)
                    pool.sem_inc(v.tick, 1)
                    for k in range(K):
                        pool.indirect_dma_start(out=v.acc0[:, :],
                                                out_offset=bass.IndirectOffsetOnAxis(ap=si[:, s, k:k + 1], axis=0),
                                                in_=row[:, s, k, :], in_offset=None,
                                                bounds_check=bound, oob_is_err=False).then_inc(put[s], 16)

            staged(pool, DEPTH, body)
            for s in range(2):
                pool.wait_ge(put[s], NG // 2 * 16 * K)

        @block.sync
        def _(sp):
            def body(i, par):
                g = i - 2
                if live(g):
                    s = par
                    wait(sp, start_done, g - 1)
                    src = v.start_d[bass.ds(g * T, T)].rearrange("(a n) -> a n", a=1)
                    sp.dma_start(start[:, s, :], src).then_inc(start_in[s], 16)
                    if isinstance(g, int) and g == NG - 1:
                        rest = N - g * T
                        sp.dma_start(v.acc1[g * T:N, :].rearrange("(p k) d -> p (k d)", k=3),
                                     v.zeros[0:rest // 3, 0:3 * P]).then_inc(acc1_clear, 16)
                    else:
                        sp.dma_start(v.acc1[bass.ds(g * T, T), :].rearrange("(p k) d -> p (k d)", k=K),
                                     v.zeros[:, 0:T]).then_inc(acc1_clear, 16)

            staged(sp, 2, body)
            sp.wait_ge(acc1_clear, 16 * NG)

        @block.vector
        def _(dve):
            dve.memset(M[:, 1, T:T + 1], -BIG)
            dve.memset(S[:, 1, T - 1:T], 0.0)
            dve.memset(D[:, 1, T - 1:T], 0.0)
            dve.drain()

            def body(i, par):
                g = i - 1
                if live(g):
                    s = (par - 1) % 2
                    wait(dve, got[s], (g - s) * (8 * K) + 16 * K)
                    for k in range(K):
                        dve.bn_stats(bst[:, k, :], xg[:, s, k, :]).then_inc(stats_done, 1)
                    dve.wait_ge(stats_done, (g + 1) * K)
                    wait(dve, z_done, g)
                    dve.sem_inc(v.tick, 1)
                    for k in range(K):
                        dve.bn_aggr(mv[:, k, :], bst[:, k, :]).then_inc(aggr_done, 1)
                g = i - 3
                if live(g):
                    s = (par - 3) % 2
                    dve.wait_ge(exp_done, g + 1)
                    dve.tensor_tensor(y[:, :], xw[:, s, :], ps_b[:, :], ALU.mult).then_inc(y_done, 1)
                    wait(dve, back_done, g - 1)
                    dve.wait_ge(y_done, g + 1)
                    dve.tensor_tensor_scan(S[:, s, :], keepf[:, :], y[:, :], S[:, 1 - s, T - 1:T],
                                           ALU.mult, ALU.add).then_inc(S_done, 1)
                    dve.tensor_tensor_scan(D[:, s, :], keepf[:, :], ps_b[:, :], D[:, 1 - s, T - 1:T],
                                           ALU.mult, ALU.add).then_inc(D_done, 1)
                g = i - 1
                if live(g):
                    s = (par - 1) % 2
                    dve.wait_ge(rstd_done, g + 1)
                    wait(dve, zT_done, g - 1)
                    for k in range(K):
                        last = dve.tensor_scalar(z[:, s, k, :], xg[:, s, k, :], mv[:, k, 0:1], rstd[:, k:k + 1],
                                                 ALU.subtract, ALU.mult)
                    last.then_inc(z_done, 1)
                g = i - 2
                if live(g):
                    s = (par - 2) % 2
                    dve.wait_ge(raw_done, g + 1)
                    dve.scalar_tensor_tensor(out=L[:, :], in0=ps_l[:, :], scalar=SLOPE, in1=raw_l[:, :],
                                             op0=ALU.mult, op1=ALU.max).then_inc(L_done, 1)
                    wait(dve, back_done, g - 1)
                    dve.tensor_copy(M[:, s, 0:1], M[:, 1 - s, T:T + 1])
                    dve.wait_ge(start_done, g + 1)
                    dve.wait_ge(L_done, g + 1)
                    dve.tensor_tensor_scan(M[:, s, 1:T + 1], ps_a[:, :], L[:, :], M[:, 1 - s, T:T + 1],
                                           ALU.add, ALU.max).then_inc(M_done, 1)
                    dve.wait_ge(M_done, g + 1)
                    dve.tensor_tensor(ps_a[:, :], M[:, s, 0:T], ps_a[:, :], ALU.add).then_inc(u_done, 1)
                    wait(dve, exp_done, g)
                    dve.tensor_tensor(ps_b[:, :], L[:, :], M[:, s, 1:T + 1], ALU.subtract)
                    dve.wait_ge(u_done, g + 1)
                    dve.tensor_tensor(ps_a[:, :], ps_a[:, :], M[:, s, 1:T + 1], ALU.subtract).then_inc(arg_done, 1)

            staged(dve, 3, body)

        @block.scalar
        def _(act):
            act.preload_act_table_set("natural_log_exp_and_others")
            def body(i, par):
                g = i - 2
                if live(g):
                    act.wait_ge(zT_done, g + 1)
                    wait(act, w_done, g)
                    act.activation(hT[:, :], ps_z[:, :], ACT.Relu).then_inc(relu_done, 1)
                g = i - 3
                if live(g):
                    act.wait_ge(arg_done, g + 1)
                    wait(act, D_done, g)
                    act.activation(ps_b[:, :], ps_b[:, :], ACT.Exp)
                    act.activation(keepf[:, :], ps_a[:, :], ACT.Exp).then_inc(exp_done, 1)
                g = i - 1
                if live(g):
                    act.wait_ge(aggr_done, (g + 1) * K)
                    wait(act, z_done, g)
                    act.activation(lnv[:, :], mv[:, :, 1], ACT.Ln, bias=v.eps[:, :]).then_inc(ln_done, 1)
                    act.wait_ge(ln_done, g + 1)
                    act.activation(rstd[:, :], lnv[:, :], ACT.Exp, scale=-0.5).then_inc(rstd_done, 1)
                g = i - 2
                if live(g):
                    s = (par - 2) % 2
                    act.wait_ge(w_done, g + 1)
                    wait(act, y_done, g - 1)
                    act.activation(xw[:, s, :], ps_x[:, :], ACT.Identity, bias=v.b_lin[:, :]).then_inc(xw_done, 1)
                    act.wait_ge(l_done, g + 1)
                    wait(act, L_done, g)
                    act.activation(raw_l[:, :], ps_l[:, :], ACT.Copy).then_inc(raw_done, 1)
                g = i - 3
                if live(g):
                    s = (par - 3) % 2
                    act.wait_ge(back_done, g + 1)
                    wait(act, put[s], (g - s) * (8 * K))
                    act.activation(row[:, s, :, 0:P], ps_S[:, :, :], ACT.Copy)
                    act.activation(row[:, s, :, P:P + H], ps_D[:, :, 0:P:P // H], ACT.Copy)
                    act.activation(row[:, s, :, P + H:ROW], ps_M[:, :, 0:P:P // H], ACT.Copy).then_inc(row_done, 1)

            staged(act, 3, body)

        @block.tensor
        def _(pe):
            def body(i, par):
                g = i - 2
                if live(g):
                    s = (par - 2) % 2
                    pe.wait_ge(z_done, g + 1)
                    wait(pe, relu_done, g)
                    for k in range(K):
                        last = pe.transpose(ps_z[:, k * P:(k + 1) * P], z[:, s, k, :], v.ident[:, :])
                    last.then_inc(zT_done, 1)
                g = i - 2
                if live(g):
                    s = (par - 2) % 2
                    pe.wait_ge(relu_done, g + 1)
                    wait(pe, xw_done, g)
                    pe.matmul(ps_x[:, :], v.w_ext[:, 0:P], hT[:, :], start=True, stop=True).then_inc(w_done, 1)
                    pe.wait_ge(start_in[s], (g - s) * 8 + 16)
                    wait(pe, exp_done, g)
                    pe.matmul(ps_a[:, :], v.ones16[:, :], start[:, s, :], start=True, stop=True).then_inc(start_done, 1)
                    pe.wait_ge(xw_done, g + 1)
                    wait(pe, L_done, g)
                    pe.matmul(ps_l[:, :], v.alpha_all[:, :], xw[:, s, :], start=True, stop=True).then_inc(l_done, 1)
                g = i - 3
                if live(g):
                    s = (par - 3) % 2
                    pe.wait_ge(S_done, g + 1)
                    wait(pe, row_done, g)
                    for k in range(K):
                        pe.transpose(ps_S[:, k, :], S[:, s, k * P:(k + 1) * P], v.ident[:, :])
                        pe.transpose(ps_M[:, k, :], M[:, s, k * P + 1:(k + 1) * P + 1], v.ident[:, :])
                    pe.wait_ge(D_done, g + 1)
                    for k in range(K):
                        last = pe.transpose(ps_D[:, k, :], D[:, s, k * P:(k + 1) * P], v.ident[:, :])
                    last.then_inc(back_done, 1)

            staged(pe, 3, body)


def nodes0(nc, v):
    f32, ALU, ACT, AX = v.f32, v.ALU, v.ACT, v.AX
    with ExitStack() as ctx:
        def sb(name, shape, dt=f32):
            return ctx.enter_context(nc.sbuf_tensor(name, shape, dt))

        def pb(name, shape):
            return ctx.enter_context(nc.psum_tensor(name, shape, f32))

        def sem(name):
            return ctx.enter_context(nc.semaphore(name))

        x = sb("n0_x", [P, 4, K, P])
        ac = sb("n0_ac", [P, 4, K, ROW])
        bst = sb("n0_bst", [P, K, 6])
        mv = sb("n0_mv", [P, K, 2])
        lnv = sb("n0_lnv", [P, K])
        rstd = sb("n0_rstd", [P, K])
        z = sb("n0_z", [P, K, P])
        hT = sb("n0_hT", [P, T])
        raw_l = sb("n0_raw_l", [P, K, H])
        L = sb("n0_L", [P, K, H])
        empty = sb("n0_empty", [P, K, H])
        me = sb("n0_me", [P, K, H])
        top = sb("n0_top", [P, K, H])
        arg = sb("n0_arg", [P, 2, K, H])
        ex = sb("n0_ex", [P, 2, K, H])
        den = sb("n0_den", [P, K, H])
        rden = sb("n0_rden", [P, K, H])
        w = sb("n0_w", [P, 2, 2, K, H])
        own = sb("n0_own", [P, K, P])
        fe = sb("n0_fe", [P, K, P])
        base = sb("n0_base", [P, K, P])
        rest = sb("n0_rest", [P, K, P])
        x1 = sb("n0_x1", [P, 2, K, P])
        bst1 = sb("n0_bst1", [P, K, 6])
        mv1 = sb("n0_mv1", [P, 2, K, 2])
        lnv1 = sb("n0_lnv1", [P, K])
        rstd1 = sb("n0_rstd1", [P, 2, K])
        z1 = sb("n0_z1", [P, K, P])
        h1 = sb("n0_h1", [P, 2, K, P])
        prod = sb("n0_prod", [P, 2, K, P])
        s2 = sb("n0_s2", [P, 2, K])
        ps_z = pb("n0_psz", [P, T])
        ps_x = pb("n0_psx", [P, 2, K, 256])

        names = ("stats", "aggr", "ln", "rstd", "z", "zT", "relu", "xw", "L", "soft", "arg", "ex", "w", "own", "fe",
                 "rest", "x1", "stats1", "aggr1", "ln1", "rstd1", "z1", "h1", "prod", "s2", "raw", "top")
        sems = {n: sem(f"n0_{n}") for n in names}
        q = sems
        x_in = [sem(f"n0_x_in{s}") for s in range(4)]
        x_out = [sem("n0_x_out0"), sem("n0_x_out1")]
        h_out = [sem("n0_h_out0"), sem("n0_h_out1")]
        s_out = [sem("n0_s_out0"), sem("n0_s_out1")]
        block = ctx.enter_context(nc.Block())

        def group(dram, g, width=None):
            return dram[bass.ds(node_rows(g), T), :].rearrange("(p k) d -> p k d", k=K)

        def staged4(eng, depth, body):
            head = -(-(depth + 3) // 4) * 4
            for i in range(head):
                body(i, i % 4)
            end = head + (NG - 1 - head) // 4 * 4
            with eng.Fori(0, (end - head) // 4) as turn:
                for j in range(4):
                    body(turn * 4 + (head + j), j)
            for i in range(end, NG + depth):
                body(i, i % 4)

        def half(g, par, off):
            return (par - off) % 2

        @block.sync
        def _(sp):
            def body(i, par):
                g = i
                if live(g):
                    s4 = par
                    wait(sp, q["x1"], g - 3)
                    wait(sp, q["rest"], g - 3)
                    sp.dma_start(x[:, s4, :, :], group(v.x_d, g)).then_inc(x_in[s4], 16)
                    sp.dma_start(ac[:, s4, :, :], group(v.acc0, g)).then_inc(x_in[s4], 16)

            staged4(sp, 0, body)

        @block.scalar
        def _(act):
            act.preload_act_table_set("natural_log_exp_and_others")
            def body(i, par):
                g = i - 2
                if live(g):
                    act.wait_ge(q["zT"], g + 1)
                    wait(act, q["xw"], g)
                    act.activation(hT[:, :], ps_z[:, :], ACT.Relu).then_inc(q["relu"], 1)
                g = i - 1
                if live(g):
                    act.wait_ge(q["aggr"], (g + 1) * K)
                    wait(act, q["z"], g)
                    act.activation(lnv[:, :], mv[:, :, 1], ACT.Ln, bias=v.eps[:, :]).then_inc(q["ln"], 1)
                    act.wait_ge(q["ln"], g + 1)
                    act.activation(rstd[:, :], lnv[:, :], ACT.Exp, scale=-0.5).then_inc(q["rstd"], 1)
                g = i - 2
                if live(g):
                    s = half(g, par, 2)
                    act.wait_ge(q["xw"], g + 1)
                    wait(act, q["L"], g)
                    act.activation(raw_l[:, :, :], ps_x[:, s, :, P:P + H], ACT.Copy).then_inc(q["raw"], 1)
                g = i - 4
                if live(g):
                    s = half(g, par, 4)
                    act.wait_ge(q["z1"], g + 1)
                    wait(act, h_out[s], (g - s) * 8)
                    wait(act, q["prod"], g - 1)
                    act.activation(h1[:, s, :, :], z1[:, :, :], ACT.Relu).then_inc(q["h1"], 1)
                g = i - 2
                if live(g):
                    act.wait_ge(q["arg"], g + 1)
                    wait(act, q["w"], g)
                    act.activation(ex[:, :, :, :], arg[:, :, :, :], ACT.Exp).then_inc(q["ex"], 1)
                g = i - 3
                if live(g):
                    s = half(g, par, 3)
                    act.wait_ge(q["aggr1"], (g + 1) * K)
                    act.activation(lnv1[:, :], mv1[:, s, :, 1], ACT.Ln, bias=v.eps[:, :]).then_inc(q["ln1"], 1)
                    act.wait_ge(q["ln1"], g + 1)
                    wait(act, q["z1"], g - 1)
                    act.activation(rstd1[:, s, :], lnv1[:, :], ACT.Exp, scale=-0.5).then_inc(q["rstd1"], 1)
                g = i - 4
                if live(g):
                    s = half(g, par, 4)
                    at = FRESH if isinstance(g, int) and g == NG - 1 else 0
                    act.wait_ge(q["h1"], g + 1)
                    act.dma_start(group(v.x1_d, g)[at:P], x1[at:P, s, :, :]).then_inc(x_out[s], 16)
                    act.dma_start(group(v.h1_d, g)[at:P], h1[at:P, s, :, :]).then_inc(h_out[s], 16)
                    act.wait_ge(q["s2"], g + 1)
                    sdst = v.s2_d[bass.ds(node_rows(g), T), :].rearrange("(p k) d -> p (k d)", k=K)
                    act.dma_start(sdst[at:P], s2[at:P, s, :]).then_inc(s_out[s], 16)

            staged4(act, 4, body)
            for s in range(2):
                act.wait_ge(x_out[s], NG // 2 * 16)
                act.wait_ge(h_out[s], NG // 2 * 16)
                act.wait_ge(s_out[s], NG // 2 * 16)

        @block.gpsimd
        def _(pool):
            def body(i, par):
                g = i - 4
                if live(g):
                    s = half(g, par, 4)
                    w2 = v.w_att2_all[:, :].rearrange("p (a d) -> p a d", a=1).broadcast_to([P, K, P])
                    wait(pool, q["s2"], g - 1)
                    pool.wait_ge(q["h1"], g + 1)
                    pool.tensor_tensor(prod[:, s, :, :], h1[:, s, :, :], w2, ALU.mult).then_inc(q["prod"], 1)
                g = i - 2
                if live(g):
                    s, s4 = half(g, par, 2), (par - 2) % 4
                    b = v.bias_all[:, :].rearrange("p (a d) -> p a d", a=1).broadcast_to([P, K, P])
                    pool.wait_ge(x_in[s4], (g - s4) * 8 + 32)
                    pool.tensor_tensor(base[:, :, :], x[:, s4, :, :], b, ALU.add)
                    pool.wait_ge(q["w"], g + 1)
                    pool.tensor_tensor(fe[:, :, :].rearrange("p k (h c) -> p k h c", h=H),
                                       ac[:, s4, :, 0:P].rearrange("p k (h c) -> p k h c", h=H),
                                       w[:, s, 0, :, :].rearrange("p k (h a) -> p k h a", a=1)
                                       .broadcast_to([P, K, H, P // H]), ALU.mult).then_inc(q["fe"], 1)
                    wait(pool, q["x1"], g)
                    pool.wait_ge(q["fe"], g + 1)
                    pool.tensor_tensor(rest[:, :, :], fe[:, :, :], base[:, :, :], ALU.add).then_inc(q["rest"], 1)
                    pool.wait_ge(q["rest"], g + 1)
                    pool.sem_inc(v.tick, 1)

            staged4(pool, 4, body)

        @block.vector
        def _(dve):
            def body(i, par):
                g = i - 1
                if live(g):
                    s4 = (par - 1) % 4
                    dve.wait_ge(x_in[s4], (g - s4) * 8 + 32)
                    for k in range(K):
                        dve.bn_stats(bst[:, k, :], x[:, s4, k, :]).then_inc(q["stats"], 1)
                    dve.wait_ge(q["stats"], (g + 1) * K)
                    wait(dve, q["z"], g)
                    dve.sem_inc(v.tick, 1)
                    for k in range(K):
                        dve.bn_aggr(mv[:, k, :], bst[:, k, :]).then_inc(q["aggr"], 1)
                g = i - 3
                if live(g):
                    s = half(g, par, 3)
                    dve.tensor_tensor(own[:, :, :].rearrange("p k (h c) -> p k h c", h=H),
                                      ps_x[:, s, :, 0:P].rearrange("p k (h c) -> p k h c", h=H),
                                      w[:, s, 1, :, :].rearrange("p k (h a) -> p k h a", a=1)
                                      .broadcast_to([P, K, H, P // H]), ALU.mult).then_inc(q["own"], 1)
                    dve.wait_ge(q["rest"], g + 1)
                    wait(dve, x_out[s], (g - s) * 8)
                    dve.wait_ge(q["own"], g + 1)
                    dve.tensor_tensor(x1[:, s, :, :], own[:, :, :], rest[:, :, :], ALU.add).then_inc(q["x1"], 1)
                    dve.wait_ge(q["x1"], g + 1)
                    for k in range(K):
                        dve.bn_stats(bst1[:, k, :], x1[:, s, k, :]).then_inc(q["stats1"], 1)
                g = i - 1
                if live(g):
                    s4 = (par - 1) % 4
                    dve.wait_ge(q["rstd"], g + 1)
                    wait(dve, q["zT"], g)
                    for k in range(K):
                        last = dve.tensor_scalar(z[:, k, :], x[:, s4, k, :], mv[:, k, 0:1], rstd[:, k:k + 1],
                                                 ALU.subtract, ALU.mult)
                    last.then_inc(q["z"], 1)
                g = i - 3
                if live(g):
                    s = half(g, par, 3)
                    dve.wait_ge(q["stats1"], (g + 1) * K)
                    wait(dve, q["z1"], g - 1)
                    dve.sem_inc(v.tick, 1)
                    for k in range(K):
                        dve.bn_aggr(mv1[:, s, k, :], bst1[:, k, :]).then_inc(q["aggr1"], 1)
                g = i - 4
                if live(g):
                    s = half(g, par, 4)
                    dve.wait_ge(q["rstd1"], g + 1)
                    wait(dve, q["h1"], g)
                    for k in range(K):
                        last = dve.tensor_scalar(z1[:, k, :], x1[:, s, k, :], mv1[:, s, k, 0:1], rstd1[:, s, k:k + 1],
                                                 ALU.subtract, ALU.mult)
                    last.then_inc(q["z1"], 1)
                g = i - 2
                if live(g):
                    s, s4 = half(g, par, 2), (par - 2) % 4
                    dn = ac[:, s4, :, P:P + H]
                    mx = ac[:, s4, :, P + H:ROW]
                    dve.tensor_scalar(empty[:, :, :], dn, 0.0, -BIG, ALU.is_equal, ALU.mult).then_inc(q["soft"], 1)
                    dve.wait_ge(q["soft"], g * 5 + 1)
                    dve.tensor_tensor(me[:, :, :], mx, empty[:, :, :], ALU.add).then_inc(q["soft"], 1)
                    dve.wait_ge(q["soft"], g * 5 + 2)
                    dve.wait_ge(q["raw"], g + 1)
                    dve.scalar_tensor_tensor(out=L[:, :, :], in0=raw_l[:, :, :], scalar=SLOPE, in1=raw_l[:, :, :],
                                             op0=ALU.mult, op1=ALU.max).then_inc(q["L"], 1)
                    dve.wait_ge(q["L"], g + 1)
                    dve.tensor_tensor(top[:, :, :], me[:, :, :], L[:, :, :], ALU.max).then_inc(q["top"], 1)
                    dve.wait_ge(q["top"], g + 1)
                    dve.tensor_tensor(arg[:, 0, :, :], me[:, :, :], top[:, :, :], ALU.subtract)
                    dve.tensor_tensor(arg[:, 1, :, :], L[:, :, :], top[:, :, :], ALU.subtract).then_inc(q["arg"], 1)
                    dve.wait_ge(q["ex"], g + 1)
                    dve.tensor_tensor(den[:, :, :], ex[:, 0, :, :], dn, ALU.mult).then_inc(q["soft"], 1)
                    dve.wait_ge(q["soft"], g * 5 + 3)
                    dve.tensor_tensor(den[:, :, :], den[:, :, :], ex[:, 1, :, :], ALU.add).then_inc(q["soft"], 1)
                    dve.wait_ge(q["soft"], g * 5 + 4)
                    dve.reciprocal(rden[:, :, :], den[:, :, :]).then_inc(q["soft"], 1)
                    dve.wait_ge(q["soft"], g * 5 + 5)
                    wait(dve, q["own"], g - 1)
                    wait(dve, q["fe"], g - 1)
                    dve.tensor_tensor(w[:, s, :, :, :].rearrange("p a k h -> p a (k h)"),
                                      ex[:, :, :, :].rearrange("p a k h -> p a (k h)"),
                                      rden[:, :, :].rearrange("p (a k) h -> p a (k h)", a=1).broadcast_to([P, 2, K * H]),
                                      ALU.mult).then_inc(q["w"], 1)
                    dve.wait_ge(q["w"], g + 1)
                g = i - 4
                if live(g):
                    s = half(g, par, 4)
                    dve.wait_ge(q["prod"], g + 1)
                    wait(dve, s_out[s], (g - s) * 8)
                    dve.tensor_reduce(out=s2[:, s, :], in_=prod[:, s, :, :], axis=AX.X, op=ALU.add).then_inc(q["s2"], 1)

            staged4(dve, 4, body)

        @block.tensor
        def _(pe):
            def body(i, par):
                g = i - 2
                if live(g):
                    s = half(g, par, 2)
                    pe.wait_ge(q["z"], g + 1)
                    wait(pe, q["relu"], g)
                    for k in range(K):
                        last = pe.transpose(ps_z[:, k * P:(k + 1) * P], z[:, k, :], v.ident[:, :])
                    last.then_inc(q["zT"], 1)
                    pe.wait_ge(q["relu"], g + 1)
                    wait(pe, q["own"], g - 1)
                    wait(pe, q["raw"], g - 1)
                    for k in range(K):
                        pe.matmul(ps_x[:, s, k, 0:P + H], hT[:, k * P:(k + 1) * P], v.w_ext[:, :], start=True, stop=False)
                        last = pe.matmul(ps_x[:, s, k, 0:P + H], v.ones[:, :], v.b_ext[:, :], start=False, stop=True)
                    last.then_inc(q["xw"], 1)

            staged4(pe, 2, body)


def edges1(nc, v):
    f32, i32, ALU, ACT = v.f32, v.i32, v.ALU, v.ACT
    with ExitStack() as ctx:
        def sb(name, shape, dt=f32):
            return ctx.enter_context(nc.sbuf_tensor(name, shape, dt))

        def pb(name, shape):
            return ctx.enter_context(nc.psum_tensor(name, shape, f32))

        def sem(name):
            return ctx.enter_context(nc.semaphore(name))

        gi = sb("e1_gi", [P, 2, 2, K], i32)
        si = sb("e1_si", [P, 2, K], i32)
        hg = sb("e1_hg", [P, 2, K, P])
        sg = sb("e1_sg", [P, 2, K])
        hT = sb("e1_hT", [P, 2, T])
        lin = sb("e1_lin", [P, 2, T])
        arg = sb("e1_arg", [P, K])
        ex = sb("e1_ex", [P, K])
        ex1 = sb("e1_ex1", [P, K])
        att = sb("e1_att", [P, 2, K])
        same = sb("e1_same", [1, 2, T], v.bf16)
        y = sb("e1_y", [P, T])
        S = sb("e1_S", [P, 2, T])
        row = sb("e1_row", [P, 2, K, P])
        ps_h, ps_m, ps_s, ps_c, ps_t, ps_r = (pb(f"e1_ps{n}", [P, T]) for n in "hmsctr")

        names = ("idx", "sidx", "hT", "hTs", "s1", "msg", "lin", "arg", "ex", "ex1", "att", "bc", "y", "S", "back", "row")
        q = {n: sem(f"e1_{n}") for n in names}
        got = [sem("e1_got0"), sem("e1_got1")]
        same_in = [sem("e1_same_in0"), sem("e1_same_in1")]
        put = [sem("e1_put0"), sem("e1_put1")]
        block = ctx.enter_context(nc.Block())

        @block.gpsimd
        def _(pool):
            bound = pool.to_reg(N - 1)

            def body(i, par):
                g = i
                if live(g):
                    s = par
                    wait(pool, q["hT"], g - 1)
                    wait(pool, q["arg"], g - 1)
                    pool.tensor_copy(gi[:, s, 0, :], v.src_idx[:, bass.ds(g * K, K)])
                    pool.tensor_copy(gi[:, s, 1, :], v.dst_idx[:, bass.ds(g * K, K)]).then_inc(q["idx"], 1)
                    pool.wait_ge(q["idx"], g + 1)
                    pool.sem_inc(v.tick, 1)
                    for k in range(K):
                        for a, (out, table) in enumerate(((hg[:, s, k, :], v.h1_d), (sg[:, s, k:k + 1], v.s2_d))):
                            pool.indirect_dma_start(out=out, out_offset=None, in_=table[:, :],
                                                    in_offset=bass.IndirectOffsetOnAxis(ap=gi[:, s, a, k:k + 1], axis=0),
                                                    bounds_check=bound, oob_is_err=False).then_inc(got[s], 16)
                g = i - 3
                if live(g):
                    s = (par - 3) % 2
                    wait(pool, put[s], (g - s) * (8 * K))
                    pool.tensor_copy(si[:, s, :], v.put_idx[:, bass.ds(g * K, K)]).then_inc(q["sidx"], 1)
                    pool.wait_ge(q["sidx"], g + 1)
                    pool.sem_inc(v.tick, 1)
                    pool.wait_ge(q["row"], g + 1)
                    pool.sem_inc(v.tick, 1)
                    for k in range(K):
                        pool.indirect_dma_start(out=v.acc1[:, :],
                                                out_offset=bass.IndirectOffsetOnAxis(ap=si[:, s, k:k + 1], axis=0),
                                                in_=row[:, s, k, :], in_offset=None,
                                                bounds_check=bound, oob_is_err=False).then_inc(put[s], 16)

            staged(pool, 3, body)
            for s in range(2):
                pool.wait_ge(put[s], NG // 2 * 16 * K)

        @block.sync
        def _(sp):
            def body(i, par):
                g = i
                if live(g):
                    s = par
                    wait(sp, q["bc"], g - 1)
                    sp.dma_start(same[:, s, :], v.same_d[bass.ds(g * T, T)].rearrange("(a n) -> a n", a=1))\
                      .then_inc(same_in[s], 16)

            staged(sp, 0, body)

        @block.vector
        def _(dve):
            dve.memset(S[:, 1, T - 1:T], 0.0)
            dve.drain()

            def body(i, par):
                g = i - 1
                if live(g):
                    s = (par - 1) % 2
                    dve.wait_ge(q["s1"], g + 1)
                    wait(dve, q["ex"], g)
                    dve.tensor_tensor(arg[:, :], ps_s[:, 0:K], sg[:, s, :], ALU.add).then_inc(q["arg"], 1)
                    dve.wait_ge(q["ex"], g + 1)
                    dve.tensor_scalar(ex1[:, :], ex[:, :], 1.0, None, ALU.add).then_inc(q["ex1"], 1)
                    wait(dve, q["bc"], g - 1)
                    dve.wait_ge(q["ex1"], g + 1)
                    dve.reciprocal(att[:, s, :], ex1[:, :]).then_inc(q["att"], 1)
                    dve.wait_ge(q["att"], g + 1)
                g = i - 2
                if live(g):
                    s = (par - 2) % 2
                    dve.wait_ge(q["bc"], g + 1)
                    dve.wait_ge(q["lin"], g + 1)
                    dve.tensor_tensor(y[:, :], lin[:, s, :], ps_t[:, :], ALU.mult).then_inc(q["y"], 1)
                    wait(dve, q["back"], g - 1)
                    dve.wait_ge(q["y"], g + 1)
                    dve.tensor_tensor_scan(S[:, s, :], ps_c[:, :], y[:, :], S[:, 1 - s, T - 1:T],
                                           ALU.mult, ALU.add).then_inc(q["S"], 1)
                    dve.wait_ge(q["S"], g + 1)

            staged(dve, 2, body)

        @block.scalar
        def _(act):
            act.preload_act_table_set("natural_log_exp_and_others")
            def body(i, par):
                g = i - 1
                if live(g):
                    s = (par - 1) % 2
                    act.wait_ge(q["hT"], g + 1)
                    wait(act, q["msg"], g - 1)
                    act.activation(hT[:, s, :], ps_h[:, :], ACT.Copy).then_inc(q["hTs"], 1)
                    act.wait_ge(q["arg"], g + 1)
                    wait(act, q["ex1"], g)
                    act.activation(ex[:, :], arg[:, :], ACT.Exp, scale=-1.0, bias=v.minus_b_att[:, :]).then_inc(q["ex"], 1)
                    act.wait_ge(q["msg"], g + 1)
                    wait(act, q["y"], g - 1)
                    act.activation(lin[:, s, :], ps_m[:, :], ACT.Identity, bias=v.b_msg[:, :]).then_inc(q["lin"], 1)
                g = i - 2
                if live(g):
                    s = (par - 2) % 2
                    act.wait_ge(q["back"], g + 1)
                    wait(act, put[s], (g - s) * (8 * K))
                    act.activation(row[:, s, :, :].rearrange("p k d -> p (k d)"), ps_r[:, :], ACT.Copy).then_inc(q["row"], 1)

            staged(act, 2, body)

        @block.tensor
        def _(pe):
            def body(i, par):
                g = i - 1
                if live(g):
                    s = (par - 1) % 2
                    pe.wait_ge(got[s], (g - s) * (16 * K) + 32 * K)
                    wait(pe, q["hTs"], g)
                    for k in range(K):
                        last = pe.transpose(ps_h[:, k * P:(k + 1) * P], hg[:, s, k, :], v.ident[:, :])
                    last.then_inc(q["hT"], 1)
                g = i - 2
                if live(g):
                    s = (par - 2) % 2
                    pe.wait_ge(q["att"], g + 1)
                    pe.wait_ge(same_in[s], (g - s) * 8 + 16)
                    wait(pe, q["S"], g)
                    pe.matmul(ps_c[:, :], v.ones16[:, :], same[:, s, :], start=True, stop=True)
                    for k in range(K):
                        last = pe.matmul(ps_t[:, k * P:(k + 1) * P], att[:, s, k:k + 1].broadcast_to([P, P]),
                                         v.ident[:, :], start=True, stop=True)
                    last.then_inc(q["bc"], 1)
                g = i - 1
                if live(g):
                    s = (par - 1) % 2
                    pe.wait_ge(q["hTs"], g + 1)
                    wait(pe, q["arg"], g)
                    for k in range(K):
                        last = pe.matmul(ps_s[:, k:k + 1], hT[:, s, k * P:(k + 1) * P], v.w_att1[:, :], start=True, stop=True)
                    last.then_inc(q["s1"], 1)
                    wait(pe, q["lin"], g)
                    pe.matmul(ps_m[:, :], v.w_msg[:, :], hT[:, s, :], start=True, stop=True).then_inc(q["msg"], 1)
                g = i - 2
                if live(g):
                    s = (par - 2) % 2
                    pe.wait_ge(q["S"], g + 1)
                    wait(pe, q["row"], g)
                    for k in range(K):
                        last = pe.transpose(ps_r[:, k * P:(k + 1) * P], S[:, s, k * P:(k + 1) * P], v.ident[:, :])
                    last.then_inc(q["back"], 1)

            staged(pe, 2, body)


def nodes1(nc, v):
    f32, ALU, ACT = v.f32, v.ALU, v.ACT
    with ExitStack() as ctx:
        def sb(name, shape, dt=f32):
            return ctx.enter_context(nc.sbuf_tensor(name, shape, dt))

        def pb(name, shape):
            return ctx.enter_context(nc.psum_tensor(name, shape, f32))

        def sem(name):
            return ctx.enter_context(nc.semaphore(name))

        h = sb("n1_h", [P, 2, K, P])
        a = sb("n1_a", [P, 2, K, P])
        hT = sb("n1_hT", [P, 2, T])
        aT = sb("n1_aT", [P, 2, T])
        r = sb("n1_r", [P, T])
        zg = sb("n1_zg", [P, 2, T])
        t1 = sb("n1_t1", [P, T])
        t2 = sb("n1_t2", [P, T])
        n = sb("n1_n", [P, 2, T])
        d = sb("n1_d", [P, T])
        e = sb("n1_e", [P, 2, T])
        hn = sb("n1_hn", [P, 2, T])
        ps_h, ps_a = pb("n1_psh", [P, T]), pb("n1_psa", [P, T])
        ps_r, ps_z, ps_i, ps_n = (pb(f"n1_ps{c}", [P, T]) for c in "rzin")
        names = ("T", "hT", "aT", "gr", "gz", "gn", "r", "z", "t1", "t2", "n", "d", "e", "hn", "st")
        q = {c: sem(f"n1_{c}") for c in names}
        rows_in = [sem("n1_in0"), sem("n1_in1")]
        out = [sem("n1_out0"), sem("n1_out1")]
        block = ctx.enter_context(nc.Block())

        def group(dram, g):
            return dram[bass.ds(node_rows(g), T), :].rearrange("(p k) d -> p k d", k=K)

        @block.sync
        def _(sp):
            def body(i, par):
                g = i
                if live(g):
                    s = par
                    wait(sp, q["T"], g - 1)
                    sp.dma_start(h[:, s, :, :], group(v.h1_d, g)).then_inc(rows_in[s], 16)
                    sp.dma_start(a[:, s, :, :], group(v.acc1, g)).then_inc(rows_in[s], 16)
                g = i - 3
                if live(g):
                    s = (par - 3) % 2
                    sp.wait_ge(q["hn"], g + 1)
                    sp.dma_start(v.hn_d[:, bass.ds(g * T, T)], hn[:, s, :]).then_inc(out[s], 16)

            staged(sp, 3, body)
            for s in range(2):
                sp.wait_ge(out[s], NG // 2 * 16)

        @block.tensor
        def _(pe):
            def body(i, par):
                g = i - 1
                if live(g):
                    s = (par - 1) % 2
                    pe.wait_ge(rows_in[s], (g - s) * 16 + 32)
                    wait(pe, q["aT"], g)
                    for k in range(K):
                        pe.transpose(ps_h[:, k * P:(k + 1) * P], h[:, s, k, :], v.ident[:, :])
                    for k in range(K):
                        last = pe.transpose(ps_a[:, k * P:(k + 1) * P], a[:, s, k, :], v.ident[:, :])
                    last.then_inc(q["T"], 1)
                g = i - 2
                if live(g):
                    s = (par - 2) % 2
                    pe.wait_ge(q["aT"], g + 1)
                    wait(pe, q["r"], g)
                    pe.matmul(ps_r[:, :], v.w_hhT[:, 0:P], hT[:, s, :], start=True, stop=False)
                    pe.matmul(ps_r[:, :], v.w_ihT[:, 0:P], aT[:, s, :], start=False, stop=True).then_inc(q["gr"], 1)
                    wait(pe, q["t2"], g)
                    pe.matmul(ps_n[:, :], v.w_hhT[:, 2 * P:3 * P], hT[:, s, :], start=True, stop=True)
                    pe.matmul(ps_i[:, :], v.w_ihT[:, 2 * P:3 * P], aT[:, s, :], start=True, stop=True).then_inc(q["gn"], 1)
                    wait(pe, q["z"], g)
                    pe.matmul(ps_z[:, :], v.w_hhT[:, P:2 * P], hT[:, s, :], start=True, stop=False)
                    pe.matmul(ps_z[:, :], v.w_ihT[:, P:2 * P], aT[:, s, :], start=False, stop=True).then_inc(q["gz"], 1)

            staged(pe, 2, body)

        @block.scalar
        def _(act):
            act.preload_act_table_set("sigmoid_and_others")
            def body(i, par):
                g = i - 1
                if live(g):
                    s = (par - 1) % 2
                    act.wait_ge(q["T"], g + 1)
                    wait(act, q["gz"], g - 1)
                    wait(act, q["d"], g - 1)
                    act.activation(hT[:, s, :], ps_h[:, :], ACT.Copy)
                    act.activation(aT[:, s, :], ps_a[:, :], ACT.Copy).then_inc(q["aT"], 1)
                g = i - 2
                if live(g):
                    s = (par - 2) % 2
                    act.wait_ge(q["gr"], g + 1)
                    wait(act, q["t1"], g)
                    act.activation(r[:, :], ps_r[:, :], ACT.Sigmoid, bias=v.b_gate[:, 0:1]).then_inc(q["r"], 1)
                    act.wait_ge(q["gz"], g + 1)
                    wait(act, q["e"], g - 1)
                    act.activation(zg[:, s, :], ps_z[:, :], ACT.Sigmoid, bias=v.b_gate[:, 1:2]).then_inc(q["z"], 1)
                    act.wait_ge(q["t2"], g + 1)
                    wait(act, q["hn"], g - 1)
                    act.activation(n[:, s, :], t2[:, :], ACT.Tanh, bias=v.b_ih[:, 2:3]).then_inc(q["n"], 1)

            staged(act, 2, body)

        @block.vector
        def _(dve):
            def body(i, par):
                g = i - 2
                if live(g):
                    dve.wait_ge(q["gn"], g + 1)
                    dve.wait_ge(q["r"], g + 1)
                    dve.scalar_tensor_tensor(out=t1[:, :], in0=ps_n[:, :], scalar=v.b_hh[:, 2:3], in1=r[:, :],
                                             op0=ALU.add, op1=ALU.mult).then_inc(q["t1"], 1)
                    dve.wait_ge(q["t1"], g + 1)
                    wait(dve, q["n"], g)
                    dve.tensor_tensor(t2[:, :], t1[:, :], ps_i[:, :], ALU.add).then_inc(q["t2"], 1)
                g = i - 3
                if live(g):
                    s = (par - 3) % 2
                    dve.wait_ge(q["hn"], g + 1)
                    lo = FRESH if isinstance(g, int) and g == NG - 1 else 0
                    part = hn[:, s, :].rearrange("p (k n) -> p k n", k=K)[:, :, lo:P]
                    dve.bn_stats(v.stats[:, bass.ds(g, 1), :], part).then_inc(q["st"], 1)
                g = i - 2
                if live(g):
                    s = (par - 2) % 2
                    dve.wait_ge(q["n"], g + 1)
                    dve.tensor_tensor(d[:, :], hT[:, s, :], n[:, s, :], ALU.subtract).then_inc(q["d"], 1)
                    wait(dve, q["hn"], g - 1)
                    dve.wait_ge(q["z"], g + 1)
                    dve.wait_ge(q["d"], g + 1)
                    dve.tensor_tensor(e[:, s, :], d[:, :], zg[:, s, :], ALU.mult).then_inc(q["e"], 1)
                    dve.wait_ge(q["e"], g + 1)

            staged(dve, 3, body)

        @block.gpsimd
        def _(pool):
            def body(i, par):
                g = i - 2
                if live(g):
                    s = (par - 2) % 2
                    wait(pool, out[s], (g - s) * 8)
                    wait(pool, q["st"], g - 1)
                    pool.wait_ge(q["e"], g + 1)
                    pool.tensor_tensor(hn[:, s, :], e[:, s, :], n[:, s, :], ALU.add).then_inc(q["hn"], 1)

            staged(pool, 2, body)


def finish(nc, v):
    f32, ALU, ACT = v.f32, v.ALU, v.ACT
    with ExitStack() as ctx:
        def sb(name, shape, dt=f32):
            return ctx.enter_context(nc.sbuf_tensor(name, shape, dt))

        def sem(name):
            return ctx.enter_context(nc.semaphore(name))

        mv = sb("f_mv", [P, 2])
        sd = sb("f_sd", [P, 1])
        rs = sb("f_rs", [P, 1])
        scale = sb("f_scale", [P, 1])
        ms = sb("f_ms", [P, 1])
        shift = sb("f_shift", [P, 1])
        hn = sb("f_hn", [P, 2, T])
        x1 = sb("f_x1", [P, 2, K, P])
        bn = sb("f_bn", [P, 2, T])
        o = sb("f_o", [P, 2, K, P])
        ps = [ctx.enter_context(nc.psum_tensor(f"f_ps{s}", [P, T], f32)) for s in range(2)]
        chain, ready = sem("f_chain"), sem("f_ready")
        bn_done, T_done, o_done, sd_done, sd_in = sem("f_bn_done"), sem("f_T_done"), sem("f_o_done"), sem("f_sd_done"), sem("f_sd_in")
        rows_in = [sem("f_in0"), sem("f_in1")]
        out = [sem("f_out0"), sem("f_out1")]
        block = ctx.enter_context(nc.Block())

        def group(dram, g):
            return dram[bass.ds(node_rows(g), T), :].rearrange("(p k) d -> p k d", k=K)

        @block.sync
        def _(sp):
            def body(i, par):
                g = i
                if live(g):
                    s = par
                    wait(sp, bn_done, g - 1)
                    wait(sp, o_done, g - 1)
                    sp.dma_start(hn[:, s, :], v.hn_d[:, bass.ds(g * T, T)]).then_inc(rows_in[s], 16)
                    sp.dma_start(x1[:, s, :, :], group(v.x1_d, g)).then_inc(rows_in[s], 16)

            staged(sp, 0, body)

        @block.scalar
        def _(act):
            act.wait_ge(sd_in, 1)
            act.activation(sd[:, :], mv[:, 1:2], ACT.Sqrt, bias=v.eps[:, :]).then_inc(sd_done, 1)
            act.wait_ge(ready, 1)

            def body(i, par):
                g = i - 1
                if live(g):
                    s = (par - 1) % 2
                    act.wait_ge(rows_in[s], (g - s) * 16 + 32)
                    wait(act, T_done, g - 1)
                    act.activation(bn[:, s, :], hn[:, s, :], ACT.Identity, bias=shift[:, :], scale=scale[:, :])\
                       .then_inc(bn_done, 1)
                g = i - 2
                if live(g):
                    s = (par - 2) % 2
                    at = FRESH if isinstance(g, int) and g == NG - 1 else 0
                    act.wait_ge(o_done, g + 1)
                    act.dma_start(group(v.out_d, g)[at:P], o[at:P, s, :, :]).then_inc(out[s], 16)

            staged(act, 2, body)
            for s in range(2):
                act.wait_ge(out[s], NG // 2 * 16)

        @block.vector
        def _(dve):
            links = [0]

            def link(ins):
                links[0] += 1
                ins.then_inc(chain, 1)
                dve.wait_ge(chain, links[0])

            dve.bn_aggr(mv[:, :], v.stats[:, :, :].rearrange("p g s -> p (g s)")).then_inc(sd_in, 1)
            dve.wait_ge(sd_in, 1)
            dve.wait_ge(sd_done, 1)
            link(dve.reciprocal(rs[:, :], sd[:, :]))
            link(dve.tensor_tensor(scale[:, :], rs[:, :], v.gamma[:, :], ALU.mult))
            link(dve.tensor_tensor(ms[:, :], mv[:, 0:1], scale[:, :], ALU.mult))
            dve.tensor_tensor(shift[:, :], v.beta[:, :], ms[:, :], ALU.subtract).then_inc(ready, 1)

            def body(i, par):
                g = i - 2
                if live(g):
                    s = (par - 2) % 2
                    dve.wait_ge(T_done, g + 1)
                    wait(dve, out[s], (g - s) * 8)
                    dve.tensor_tensor(o[:, s, :, :].rearrange("p k d -> p (k d)"), ps[s][:, :],
                                      x1[:, s, :, :].rearrange("p k d -> p (k d)"), ALU.add).then_inc(o_done, 1)

            staged(dve, 2, body)

        @block.tensor
        def _(pe):
            def body(i, par):
                g = i - 2
                if live(g):
                    s = (par - 2) % 2
                    pe.wait_ge(bn_done, g + 1)
                    wait(pe, o_done, g - 1)
                    for k in range(K):
                        last = pe.transpose(ps[s][:, k * P:(k + 1) * P], bn[:, s, k * P:(k + 1) * P], v.ident[:, :])
                    last.then_inc(T_done, 1)

            staged(pe, 2, body)


_INS = ["x", "src", "dst", "L0_gnn_W", "L0_gnn_b_lin", "L0_gnn_alpha", "L0_gnn_bias", "L1_gnn_W_msg", "L1_gnn_b_msg",
        "L1_gnn_W_att", "L1_gnn_b_att", "L1_gnn_W_ih", "L1_gnn_b_ih", "L1_gnn_W_hh", "L1_gnn_b_hh", "L1_gnn_gamma",
        "L1_gnn_beta"]
_SCRATCH = {"acc0": (N, ROW), "acc1": (N, P), "x1": (N, P), "h1": (N, P), "s2": (N, 1), "same": (NT * P,),
            "start": (NT * P,), "hnew": (P, NG * T)}
DEBUG = False


def kernel(**inputs):
    import numpy as np
    import concourse.bacc as bacc
    from concourse.bass_utils import run_bass_kernel_spmd

    nc = bacc.Bacc("TRN2", target_bir_lowering=False, num_devices=1)
    arrays, io = {}, {}
    for name in _INS:
        a = np.ascontiguousarray(inputs[name])
        arrays[f"in_{name}"] = a
        io[name] = nc.dram_tensor(f"in_{name}", a.shape, mybir.dt.from_np(a.dtype), kind="ExternalInput").ap()
    io["out"] = nc.dram_tensor("out", (N, P), mybir.dt.float32, kind="ExternalOutput").ap()
    kind = "ExternalOutput" if DEBUG else "Internal"
    scratch = {n: nc.dram_tensor(f"scratch_{n}", (E, 1), mybir.dt.int32, kind="Internal").ap() for n in ("src_s", "dst_s")}
    scratch |= {n: nc.dram_tensor(f"scratch_{n}", s, mybir.dt.bfloat16 if n in ("same", "start") else mybir.dt.float32,
                                  kind=kind).ap() for n, s in _SCRATCH.items()}
    build(nc, io, scratch)
    r = run_bass_kernel_spmd(nc, [arrays], core_ids=[0])
    return r.results[0]["out"]
```

```python
import concourse.bass as bass
from concourse import mybir
from contextlib import ExitStack

P = 128
N = 50000
E = 50000
T = 512
K = T // P
NG = -(-E // T)
NT = NG * K
CH = 4
CT = NT // CH
H = 4
ROW = P + 2 * H
EMPTY = NG * T
LAST = N - T
FRESH = (NG * T - N) // K
PAD = 70000.0
NOWHERE = 60000.0
BIG = 1e30
EPS = 1e-5
SLOPE = 0.2


def wait(eng, sem, count):
    if not (isinstance(count, int) and count <= 0):
        eng.wait_ge(sem, count)


def staged(eng, depth, body):
    head = depth + 2 + depth % 2
    for i in range(head):
        body(i, i % 2)
    end = NG - 2
    with eng.Fori(0, (end - head) // 2) as turn:
        body(turn * 2 + head, 0)
        body(turn * 2 + (head + 1), 1)
    for i in range(end, NG + depth):
        body(i, i % 2)


def staged4(eng, depth, body):
    head = -(-(depth + 3) // 4) * 4
    for i in range(head):
        body(i, i % 4)
    end = head + (NG - 1 - head) // 4 * 4
    with eng.Fori(0, (end - head) // 4) as turn:
        for j in range(4):
            body(turn * 4 + (head + j), j)
    for i in range(end, NG + depth):
        body(i, i % 4)


def half(par, off):
    return (par - off) % 2


def live(g):
    return not isinstance(g, int) or 0 <= g < NG


def node_rows(g):
    if isinstance(g, int):
        return min(g * T, LAST)
    return g * T


class Shared:
    pass


def build(nc, io, scratch):
    v = Shared()
    v.io = io
    v.used = []
    v.f32, v.i32, v.bf16 = mybir.dt.float32, mybir.dt.int32, mybir.dt.bfloat16
    v.ACT, v.ALU, v.AX = mybir.ActivationFunctionType, mybir.AluOpType, mybir.AxisListType
    v.sums0, v.sums1, v.x1_d, v.h1_d, v.s2_d, v.same_d, v.start_d, v.hn_d = (
        scratch[n] for n in ("sums0", "sums1", "x1", "h1", "s2", "same", "start", "hnew"))
    v.x_d, v.out_d = io["x"], io["out"]
    v.src_s, v.dst_s, v.place_d = scratch["src_s"], scratch["dst_s"], scratch["place"]
    v.src_sorted, v.dst_sorted = (a[:, :].rearrange("n a -> (n a)") for a in (v.src_s, v.dst_s))

    with ExitStack() as whole:
        def keep(name, shape, dt=v.f32):
            return whole.enter_context(nc.sbuf_tensor(name, shape, dt))

        v.ident = keep("ident", [P, P])
        v.ones = keep("ones", [1, P])
        v.ones16 = keep("ones16", [1, P], v.bf16)
        v.w_ext = keep("w_ext", [P, P + H])
        v.b_ext = keep("b_ext", [1, P + H])
        v.alpha = keep("alpha", [P, H])
        v.alpha_all = keep("alpha_all", [P, P])
        v.b_lin = keep("b_lin", [P, 1])
        v.bias = keep("bias", [P, 1])
        v.w_msg = keep("w_msg", [P, P])
        v.b_msg = keep("b_msg", [P, 1])
        v.w_att1 = keep("w_att1", [P, 1])
        v.w_att2_all = keep("w_att2_all", [P, P])
        v.b_att = keep("b_att", [P, 1])
        v.minus_b_att = keep("minus_b_att", [P, 1])
        v.w_ihT = keep("w_ihT", [P, 3 * P])
        v.w_hhT = keep("w_hhT", [P, 3 * P])
        v.b_ih = keep("b_ih", [P, 3])
        v.b_hh = keep("b_hh", [P, 3])
        v.b_gate = keep("b_gate", [P, 2])
        v.gamma = keep("gamma", [P, 1])
        v.beta = keep("beta", [P, 1])
        v.eps = keep("eps", [P, 1])
        v.ends_idx = keep("ends_idx", [P, NT, 2], v.i32)
        v.place_idx = keep("place_idx", [P, NT, 3], v.i32)
        v.stats = keep("stats", [P, NG, 6])

        v.tick = whole.enter_context(nc.semaphore("tick"))

        order(nc, v)
        prepare(nc, v)
        edges0(nc, v)
        nc.clear_and_free_semaphores(v.used)
        nc.all_engine_barrier()
        v.used = []
        nodes0(nc, v)
        edges1(nc, v)
        nodes1(nc, v)
        finish(nc, v)


def order(nc, v):
    f32, i32, ALU, AX = v.f32, v.i32, v.ALU, v.AX
    src, dst = v.io["src"], v.io["dst"]
    with ExitStack() as ctx:
        def sb(name, shape, dt=f32):
            return ctx.enter_context(nc.sbuf_tensor(name, shape, dt))

        def sem(name):
            v.used.append(nc.alloc_semaphore(name))
            return v.used[-1]

        W = 390
        B = NT * P // 8
        near = sb("o_near", [P, 2, 2, W], i32)
        falls = sb("o_falls", [P, 2, W])
        fell = sb("o_fell", [P, 1])
        fell_all = sb("o_fell_all", [1, 1], i32)
        ones_col = sb("o_ones", [P, 1])
        ps = ctx.enter_context(nc.psum_tensor("o_ps", [1, 512], f32))
        cols = sb("o_cols", [P, 2, NT], i32)
        key = sb("o_key", [P, 2, NT])
        one = sb("o_one", [P, 2])
        number = sb("o_number", [P, NT], i32)
        along = sb("o_along", [P, B], i32)
        alongf = sb("o_alongf", [P, B])
        rowi = sb("o_rowi", [P, B], i32)
        rowf = sb("o_rowf", [P, B])
        before = sb("o_before", [P, B])
        count = sb("o_count", [P, 1])
        rank = sb("o_rank", [P, NT])
        ranki = sb("o_ranki", [P, NT], i32)
        at = sb("o_at", [P, 3], i32)
        copied, near_in, fell_done, summed, told = (sem(f"o_{n}") for n in (
            "copied", "near_in", "fell_done", "summed", "told"))
        blank, cols_in, numbers, row_in, row_used, ranked, picked, placed = (sem(f"o_{n}") for n in (
            "blank", "cols_in", "numbers", "row_in", "row_used", "ranked", "picked", "placed"))
        block = ctx.enter_context(nc.Block())

        @block.sync
        def _(sp):
            for first in (0, E - 1 - P * W):
                for shift in range(2):
                    a = first + shift
                    sp.dma_start(near[:, min(first, 1), shift, :], dst[a:a + P * W].rearrange("(p w) -> p w", p=P))\
                      .then_inc(near_in, 16)
            for out, array in ((v.src_s, src), (v.dst_s, dst)):
                sp.dma_start(out[:, :].rearrange("(p w) a -> p (w a)", p=80), array.rearrange("(p w) -> p w", p=80))\
                  .then_inc(copied, 16)
            sp.wait_ge(copied, 32)
            sp.wait_ge(told, 1)
            wrong = sp.value_load(fell_all[0:1, 0:1], min_val=0, max_val=E)
            with sp.If(wrong > 0):
                sp.wait_ge(blank, 1)
                for a, array in enumerate((dst, src)):
                    whole = E // P
                    with nc.allow_non_contiguous_dma(reason="only for edges that come unordered"):
                        sp.dma_start(cols[:, a, 0:whole], array[0:whole * P].rearrange("(t p) -> p t", p=P))\
                          .then_inc(cols_in, 16)
                        sp.dma_start(cols[0:E % P, a, whole:whole + 1],
                                     array[whole * P:E].rearrange("(p t) -> p t", t=1)).then_inc(cols_in, 16)

                def row(b, width):
                    sp.dma_start(rowi[:, 0:width], dst[bass.ds(b * B, width)].rearrange("(a n) -> a n", a=1)
                                 .broadcast_to([P, width])).then_inc(row_in, 16)

                row(0, B)
                with sp.Fori(0, 6) as b:
                    sp.wait_ge(row_used, b + 1)
                    row(b + 1, B)
                sp.wait_ge(row_used, 8)
                row(7, E - 7 * B)

        @block.vector
        def _(dve):
            dve.memset(ones_col[:, :], 1.0).then_inc(fell_done, 1)
            dve.wait_ge(near_in, 64)
            dve.tensor_tensor(falls[:, :, :], near[:, :, 0, :], near[:, :, 1, :], ALU.is_gt)
            dve.drain()
            dve.tensor_reduce(out=fell[:, :], in_=falls[:, :, :].rearrange("p a w -> p (a w)"), axis=AX.X, op=ALU.add)\
               .then_inc(fell_done, 1)
            dve.wait_ge(summed, 1)
            dve.tensor_scalar(fell_all[0:1, 0:1], ps[0:1, 0:1], float(E), None, ALU.min).then_inc(told, 1)
            dve.wait_ge(told, 1)
            wrong = dve.value_load(fell_all[0:1, 0:1], min_val=0, max_val=E)
            with dve.If(wrong > 0):
                dve.memset(cols[:, 0, :], int(PAD))
                dve.memset(cols[:, 1, :], 0).then_inc(blank, 1)
                dve.memset(rank[:, :], 0.0)
                dve.wait_ge(numbers, 2)
                dve.wait_ge(cols_in, 64)
                dve.tensor_copy(alongf[:, :], along[:, :])
                dve.tensor_copy(key[:, 1, :], number[:, :])
                dve.tensor_scalar(key[:, 0, :], cols[:, 0, :], 65536.0, None, ALU.mult)

                def block_of_edges(b):
                    dve.wait_ge(row_in, b * 16 + 16)
                    dve.tensor_scalar(rowf[:, :], rowi[:, :], 65536.0, None, ALU.mult)
                    dve.drain()
                    dve.sem_inc(row_used, 1)
                    with dve.Fori(0, NT) as t:
                        dve.tensor_copy(one[:, :], key[:, :, bass.ds(t, 1)].rearrange("p a t -> p (a t)"))
                        dve.drain()
                        dve.scalar_tensor_tensor(out=before[:, :], in0=rowf[:, :], scalar=one[:, 0:1], in1=alongf[:, :],
                                                 op0=ALU.subtract, op1=ALU.add)
                        dve.drain()
                        dve.tensor_scalar(before[:, :], before[:, :], one[:, 1:2], 0.0, ALU.is_lt, ALU.add,
                                          accum_out=count[:, :])
                        dve.drain()
                        dve.tensor_tensor(rank[:, bass.ds(t, 1)], rank[:, bass.ds(t, 1)], count[:, :], ALU.add)
                    dve.drain()
                    dve.tensor_scalar(key[:, 1, :], key[:, 1, :], float(B), None, ALU.subtract)
                    dve.drain()

                dve.drain()
                with dve.Fori(0, 7) as b:
                    block_of_edges(b)
                dve.memset(rowi[:, E - 7 * B:B], int(PAD)).then_inc(row_used, 1)
                dve.wait_ge(row_used, 8)
                block_of_edges(7)
                dve.tensor_copy(ranki[:, :], rank[:, :]).then_inc(ranked, 1)

        @block.tensor
        def _(pe):
            pe.wait_ge(fell_done, 2)
            pe.matmul(ps[0:1, 0:1], fell[:, :], ones_col[:, :], start=True, stop=True).then_inc(summed, 1)

        @block.gpsimd
        def _(pool):
            pool.wait_ge(told, 1)
            wrong = pool.value_load(fell_all[0:1, 0:1], min_val=0, max_val=E)
            with pool.If(wrong > 0):
                pool.iota(along[:, :], pattern=[[1, B]], base=0, channel_multiplier=0).then_inc(numbers, 1)
                pool.iota(number[:, :], pattern=[[P, NT]], base=0, channel_multiplier=1).then_inc(numbers, 1)
                bound = pool.to_reg(E - 1)
                pool.wait_ge(copied, 32)
                pool.wait_ge(cols_in, 64)
                pool.wait_ge(ranked, 1)
                pool.sem_inc(v.tick, 1)
                with pool.Fori(0, NT) as t:
                    pool.tensor_copy(at[:, 0:1], ranki[:, bass.ds(t, 1)])
                    pool.tensor_copy(at[:, 1:3], cols[:, :, bass.ds(t, 1)].rearrange("p a t -> p (a t)"))\
                        .then_inc(picked, 1)
                    pool.wait_ge(picked, t + 1)
                    pool.sem_inc(v.tick, 1)
                    for a, out in ((1, v.dst_s), (2, v.src_s)):
                        pool.indirect_dma_start(out=out[:, :], out_offset=bass.IndirectOffsetOnAxis(ap=at[:, 0:1], axis=0),
                                                in_=at[:, a:a + 1], in_offset=None, bounds_check=bound, oob_is_err=False)\
                            .then_inc(placed, 16)
                    pool.wait_ge(placed, t * 32 + 32)
                    pool.sem_inc(v.tick, 1)


def prepare(nc, v):
    f32, i32, ALU = v.f32, v.i32, v.ALU
    io = v.io
    with ExitStack() as ctx:
        def sb(name, shape, dt=f32):
            return ctx.enter_context(nc.sbuf_tensor(name, shape, dt))

        def sem(name):
            v.used.append(nc.alloc_semaphore(name))
            return v.used[-1]

        raw = [sb(f"raw_{n}", [CT, CH, P], i32) for n in ("src", "dst", "prev", "next")]
        flt = [sb(f"flt_{n}", [CT, CH, P]) for n in ("src", "dst", "prev", "next")]
        same = sb("same", [CT, CH, P])
        same16 = sb("same16", [CT, CH, P], v.bf16)
        start = sb("start", [CT, CH, P], v.bf16)
        ends = sb("ends", [CT, CH, P])
        put = sb("put", [CT, CH, P])
        place = sb("place", [P, NT], i32)
        inside = sb("inside", [CT, CH, P])
        w_ih = sb("w_ih", [P, 3, P])
        w_hh = sb("w_hh", [P, 3, P])
        wT = sb("wT", [P, P])
        zeros = sb("zeros", [1, ROW])
        bias_row = sb("bias_row", [1, P])
        nowhere = sb("nowhere", [80, N // 80], i32)
        ps_t = ctx.enter_context(nc.psum_tensor("ps_t", [P, 3, 512], f32))
        ps_w = ctx.enter_context(nc.psum_tensor("ps_w", [P, 2, 512], f32))
        ps_a = ctx.enter_context(nc.psum_tensor("ps_a", [P, 3, 512], f32))

        weights_in, edges_in, filled, cleared = sem("weights_in"), sem("edges_in"), sem("filled"), sem("cleared")
        zeros_set, raw_set, consts, consts2, flt_ready = sem("zeros_set"), sem("raw_set"), sem("consts"), sem("consts2"), sem("flt_ready")
        chain, tables, tables_out = sem("chain"), sem("tables"), sem("tables_out")
        edges_T, weights_T, wT_ready, folded, bfold = (sem(n) for n in ("edges_T", "weights_T", "wT_ready", "folded", "bfold"))
        idx_done, alpha_zero, alpha_in, w_in, gates = (sem(n) for n in ("idx_done", "alpha_zero", "alpha_in", "w_in", "gates"))
        block = ctx.enter_context(nc.Block())
        full = (E // P) - (CH - 1) * CT
        rest = E % P
        weight_loads = [0]

        @block.sync
        def _(sp):
            sp.wait_ge(raw_set, 1)
            n = 0

            def load(dst, src):
                sp.dma_start(dst, src).then_inc(edges_in, 16)

            def rows(a, lo, count):
                return a[lo:lo + count * P].rearrange("(t p) -> t p", p=P)

            for a, (buf, array) in enumerate(((raw[0], v.src_sorted), (raw[1], v.dst_sorted))):
                for c in range(CH - 1):
                    load(buf[:, c, :], rows(array, c * CT * P, CT))
                load(buf[0:full, CH - 1, :], rows(array, (CH - 1) * CT * P, full))
                load(buf[full:full + 1, CH - 1, 0:rest], array[E - rest:E].rearrange("(a n) -> a n", a=1))
            load(raw[2][0:1, 0, 1:P], v.dst_sorted[0:P - 1].rearrange("(a n) -> a n", a=1))
            load(raw[2][1:CT, 0, :], rows(v.dst_sorted, P - 1, CT - 1))
            for c in range(1, CH - 1):
                load(raw[2][:, c, :], rows(v.dst_sorted, c * CT * P - 1, CT))
            load(raw[2][0:full, CH - 1, :], rows(v.dst_sorted, (CH - 1) * CT * P - 1, full))
            load(raw[2][full:full + 1, CH - 1, 0:rest], v.dst_sorted[E - rest - 1:E - 1].rearrange("(a n) -> a n", a=1))
            for c in range(CH - 1):
                load(raw[3][:, c, :], rows(v.dst_sorted, c * CT * P + 1, CT))
            load(raw[3][0:full, CH - 1, :], rows(v.dst_sorted, (CH - 1) * CT * P + 1, full))
            load(raw[3][full:full + 1, CH - 1, 0:rest - 1], v.dst_sorted[E - rest + 1:E].rearrange("(a n) -> a n", a=1))
            sp.wait_ge(tables, 2)
            for table, t in ((v.same_d, same16), (v.start_d, start)):
                sp.dma_start(table[:].rearrange("(c t p) -> t c p", c=CH, t=CT), t[:, :, :]).then_inc(tables_out, 16)
            sp.wait_ge(tables_out, 32)

        @block.scalar
        def _(act):
            def load(dst, src):
                weight_loads[0] += 1
                act.dma_start(dst, src).then_inc(weights_in, 16)

            def column(a):
                return a.rearrange("(p a) -> p a", a=1)

            load(v.w_ext[:, 0:P], io["L0_gnn_W"])
            load(v.b_lin[:, :], column(io["L0_gnn_b_lin"]))
            load(v.b_ext[:, 0:P], io["L0_gnn_b_lin"].rearrange("(a n) -> a n", a=1))
            load(v.bias[:, :], column(io["L0_gnn_bias"]))
            load(bias_row[:, :], io["L0_gnn_bias"].rearrange("(a n) -> a n", a=1))
            load(v.w_msg[:, :], io["L1_gnn_W_msg"])
            load(v.b_msg[:, :], column(io["L1_gnn_b_msg"]))
            load(v.w_att1[:, :], io["L1_gnn_W_att"][0:P, :])
            load(v.w_att2_all[:, :], io["L1_gnn_W_att"][P:2 * P, :].rearrange("n a -> a n").broadcast_to([P, P]))
            load(v.b_att[:, :], io["L1_gnn_b_att"].rearrange("(a n) -> a n", a=1).broadcast_to([P, 1]))
            load(w_ih[:, :, :], io["L1_gnn_W_ih"].rearrange("(c r) k -> r c k", c=3))
            load(w_hh[:, :, :], io["L1_gnn_W_hh"].rearrange("(c r) k -> r c k", c=3))
            for c in range(3):
                load(v.b_ih[:, c:c + 1], column(io["L1_gnn_b_ih"][c * P:(c + 1) * P]))
                load(v.b_hh[:, c:c + 1], column(io["L1_gnn_b_hh"][c * P:(c + 1) * P]))
            load(v.gamma[:, :], column(io["L1_gnn_gamma"]))
            load(v.beta[:, :], column(io["L1_gnn_beta"]))
            act.wait_ge(alpha_zero, 1)
            for h in range(2):
                load(v.alpha[64 * h:64 * h + 64, h:h + 1], io["L0_gnn_alpha"][0, h, :].rearrange("(p a) -> p a", a=1))
            act.wait_ge(zeros_set, 1)
            act.dma_start(v.sums0[EMPTY:EMPTY + 1, :], zeros[:, 0:ROW]).then_inc(cleared, 16)
            act.dma_start(v.sums1[EMPTY:EMPTY + 1, :], zeros[:, 0:P]).then_inc(cleared, 16)
            act.dma_start(v.place_d.rearrange("(p w) a -> p (w a)", p=80), nowhere[:, :]).then_inc(cleared, 16)
            act.wait_ge(cleared, 48)

        @block.gpsimd
        def _(pool):
            pool.memset(v.ident[:, :], 0.0).then_inc(consts, 1)
            pool.wait_ge(consts, 1)
            pool.affine_select(out=v.ident[:, :], in_=v.ident[:, :], compare_op=ALU.not_equal, fill=1.0, base=0,
                               pattern=[[-1, P]], channel_multiplier=1).then_inc(consts2, 1)
            pool.iota(place[:, :], pattern=[[T, NG], [1, K]], base=0, channel_multiplier=K).then_inc(consts2, 1)

        @block.vector
        def _(dve):
            links = [0]

            def link(ins):
                links[0] += 1
                ins.then_inc(chain, 1)
                dve.wait_ge(chain, links[0])

            dve.memset(raw[0][:, :, :], 0)
            dve.memset(raw[1][:, :, :], int(PAD))
            dve.memset(raw[3][:, :, :], int(PAD))
            link(dve.memset(raw[2][:, :, :], int(PAD)))
            dve.memset(raw[2][0:1, 0, 0:1], -1).then_inc(raw_set, 1)
            dve.memset(v.alpha[:, :], 0.0).then_inc(alpha_zero, 1)
            dve.memset(nowhere[:, :], EMPTY)
            dve.memset(zeros[:, :], 0.0).then_inc(zeros_set, 1)
            dve.memset(v.ones[:, :], 1.0)
            dve.memset(v.ones16[:, :], 1.0)
            dve.memset(v.alpha_all[:, :], 0.0)
            dve.memset(v.eps[:, :], EPS)
            dve.wait_ge(edges_in, 16 * (2 * (CH + 1) + (CH + 2) + (CH + 1)))
            dve.tensor_copy(flt[3][:, :, :], raw[3][:, :, :])
            dve.tensor_copy(flt[2][:, :, :], raw[2][:, :, :])
            dve.tensor_copy(flt[0][:, :, :], raw[0][:, :, :])
            link(dve.tensor_copy(flt[1][:, :, :], raw[1][:, :, :]))
            link(dve.tensor_tensor(same[:, :, :], flt[1][:, :, :], flt[2][:, :, :], ALU.is_equal))
            dve.tensor_copy(same16[:, :, :], same[:, :, :])
            dve.tensor_scalar(start[:, :, :], same[:, :, :], 1.0, BIG, ALU.subtract, ALU.mult).then_inc(tables, 2)
            dve.tensor_tensor(ends[:, :, :], flt[1][:, :, :], flt[3][:, :, :], ALU.not_equal)
            link(dve.tensor_scalar(put[:, :, :], flt[1][:, :, :], NOWHERE, None, ALU.subtract))
            link(dve.tensor_tensor(put[:, :, :], put[:, :, :], ends[:, :, :], ALU.mult))
            dve.tensor_scalar(put[:, :, :], put[:, :, :], NOWHERE, None, ALU.add)
            dve.tensor_scalar(inside[:, :, :], flt[1][:, :, :], float(N - 1), None, ALU.min).then_inc(flt_ready, 1)
            dve.wait_ge(weights_in, 16 * weight_loads[0])
            dve.tensor_tensor(v.b_gate[:, :], v.b_ih[:, 0:2], v.b_hh[:, 0:2], ALU.add)
            dve.tensor_tensor(v.b_ext[:, 0:P], v.b_ext[:, 0:P], bias_row[:, :], ALU.add)
            dve.tensor_scalar(v.minus_b_att[:, :], v.b_att[:, :], -1.0, None, ALU.mult)
            for h in range(2):
                dve.tensor_copy(v.alpha_all[:, h * (P // H):(h + 1) * (P // H)],
                                v.alpha[:, h:h + 1].broadcast_to([P, P // H]))
            dve.wait_ge(edges_T, 1)
            for a, t in enumerate((v.ends_idx[:, :, 0], v.ends_idx[:, :, 1], v.place_idx[:, :, 1])):
                dve.tensor_copy(t, ps_t[:, a, 0:NT])
            dve.tensor_copy(v.place_idx[:, :, 0], ps_t[:, 0, 0:NT])
            dve.wait_ge(consts2, 2)
            dve.tensor_copy(v.place_idx[:, :, 2], place[:, :])
            dve.wait_ge(weights_T, 1)
            dve.tensor_copy(v.w_ihT[:, :], ps_w[:, 0, 0:3 * P])
            dve.tensor_copy(v.w_hhT[:, :], ps_w[:, 1, 0:3 * P])
            dve.tensor_copy(wT[:, :], ps_a[:, 0, 0:P]).then_inc(wT_ready, 1)
            dve.wait_ge(folded, 1)
            dve.tensor_copy(v.w_ext[:, P:P + H], ps_a[:, 1, 0:H])
            dve.tensor_copy(v.b_ext[:, P:P + H], ps_a[0:1, 2, 0:H])

        @block.tensor
        def _(pe):
            pe.wait_ge(consts2, 1)
            pe.wait_ge(flt_ready, 1)
            for a, t in enumerate((flt[0], inside, put)):
                for c in range(CH):
                    last = pe.transpose(ps_t[:, a, c * CT:(c + 1) * CT], t[:, c, :], v.ident[0:CT, 0:CT])
            last.then_inc(edges_T, 1)
            pe.wait_ge(weights_in, 16 * weight_loads[0])
            for c in range(3):
                pe.transpose(ps_w[:, 0, c * P:(c + 1) * P], w_ih[:, c, :], v.ident[:, :])
                pe.transpose(ps_w[:, 1, c * P:(c + 1) * P], w_hh[:, c, :], v.ident[:, :])
            pe.transpose(ps_a[:, 0, 0:P], v.w_ext[:, 0:P], v.ident[:, :]).then_inc(weights_T, 1)
            pe.wait_ge(wT_ready, 1)
            pe.matmul(ps_a[:, 1, 0:H], wT[:, :], v.alpha[:, :], start=True, stop=True)
            pe.matmul(ps_a[0:1, 2, 0:H], v.b_lin[:, :], v.alpha[:, :], start=True, stop=True).then_inc(folded, 1)


def edges0(nc, v):
    f32, i32, ALU, ACT = v.f32, v.i32, v.ALU, v.ACT
    with ExitStack() as ctx:
        def sb(name, shape, dt=f32):
            return ctx.enter_context(nc.sbuf_tensor(name, shape, dt))

        def pb(name, shape):
            return ctx.enter_context(nc.psum_tensor(name, shape, f32))

        def sem(name):
            v.used.append(nc.alloc_semaphore(name))
            return v.used[-1]

        gi = sb("e0_gi", [P, 2, K, 3], i32)
        xg = sb("e0_xg", [P, 2, K, P])
        bst = sb("e0_bst", [P, K, 6])
        mv = sb("e0_mv", [P, K, 2])
        lnv = sb("e0_lnv", [P, K])
        rstd = sb("e0_rstd", [P, K])
        z = sb("e0_z", [P, 2, K, P])
        hT = sb("e0_hT", [P, T])
        xw = sb("e0_xw", [P, 2, T])
        raw_l = sb("e0_raw_l", [P, T])
        L = sb("e0_L", [P, T])
        start = sb("e0_start", [1, 2, T], v.bf16)
        M = sb("e0_M", [P, 2, T + 1])
        keepf = sb("e0_keepf", [P, T])
        y = sb("e0_y", [P, T])
        S = sb("e0_S", [P, 2, T])
        D = sb("e0_D", [P, 2, T])
        row = sb("e0_row", [P, 2, K, ROW])
        ps_z, ps_x, ps_l, ps_a, ps_b = (pb(f"e0_ps{n}", [P, T]) for n in "zxlab")
        ps_S, ps_D, ps_M = (pb(f"e0_ps{n}", [P, K, P]) for n in "SDM")

        idx_copied = sem("e0_idx_copied")
        got = [sem("e0_got0"), sem("e0_got1")]
        start_in = [sem("e0_start_in0"), sem("e0_start_in1")]
        put = [sem("e0_put0"), sem("e0_put1")]
        stats_done, aggr_done, ln_done, rstd_done, z_done = (sem(f"e0_{n}") for n in ("stats", "aggr", "ln", "rstd", "z"))
        zT_done, relu_done, w_done, xw_done, l_done, L_done, M_done = (sem(f"e0_{n}") for n in ("zT", "relu", "w", "xw", "l", "L", "M"))
        arg_done, exp_done, y_done, S_done, D_done, back_done, row_done = (sem(f"e0_{n}") for n in ("arg", "exp", "y", "S", "D", "back", "row"))
        raw_done = sem("e0_raw")
        row_out = [sem("e0_row_out0"), sem("e0_row_out1")]
        start_done, u_done = sem("e0_start"), sem("e0_u")
        block = ctx.enter_context(nc.Block())

        @block.gpsimd
        def _(pool):
            bound = pool.to_reg(N - 1)

            def body(i, par):
                g = i
                if live(g):
                    s = par
                    wait(pool, z_done, g - 1)
                    wait(pool, put[s], (g - s) * (8 * K))
                    pool.tensor_copy(gi[:, s, :, :], v.place_idx[:, bass.ds(g * K, K), :]).then_inc(idx_copied, 1)
                    pool.wait_ge(idx_copied, g + 1)
                    pool.sem_inc(v.tick, 1)
                    for k in range(K):
                        pool.indirect_dma_start(out=xg[:, s, k, :], out_offset=None, in_=v.x_d[:, :],
                                                in_offset=bass.IndirectOffsetOnAxis(ap=gi[:, s, k, 0:1], axis=0),
                                                bounds_check=bound, oob_is_err=False).then_inc(got[s], 16)
                    for k in range(K):
                        pool.indirect_dma_start(out=v.place_d[:, :],
                                                out_offset=bass.IndirectOffsetOnAxis(ap=gi[:, s, k, 1:2], axis=0),
                                                in_=gi[:, s, k, 2:3], in_offset=None,
                                                bounds_check=bound, oob_is_err=False).then_inc(put[s], 16)

            staged(pool, 0, body)
            for s in range(2):
                pool.wait_ge(put[s], NG // 2 * 16 * K)

        @block.sync
        def _(sp):
            def body(i, par):
                g = i - 2
                if live(g):
                    s = par
                    wait(sp, start_done, g - 1)
                    src = v.start_d[bass.ds(g * T, T)].rearrange("(a n) -> a n", a=1)
                    sp.dma_start(start[:, s, :], src).then_inc(start_in[s], 16)
                g = i - 4
                if live(g):
                    s = par
                    sp.wait_ge(row_done, g + 1)
                    sp.dma_start(v.sums0[bass.ds(g * T, T), :].rearrange("(p k) d -> p k d", k=K), row[:, s, :, :])\
                      .then_inc(row_out[s], 16)

            staged(sp, 4, body)
            for s in range(2):
                sp.wait_ge(row_out[s], NG // 2 * 16)

        @block.vector
        def _(dve):
            dve.memset(M[:, 1, T:T + 1], -BIG)
            dve.memset(S[:, 1, T - 1:T], 0.0)
            dve.memset(D[:, 1, T - 1:T], 0.0)
            dve.drain()

            def body(i, par):
                g = i - 1
                if live(g):
                    s = (par - 1) % 2
                    wait(dve, got[s], (g - s) * (8 * K) + 16 * K)
                    for k in range(K):
                        dve.bn_stats(bst[:, k, :], xg[:, s, k, :]).then_inc(stats_done, 1)
                    dve.wait_ge(stats_done, (g + 1) * K)
                    wait(dve, z_done, g)
                    dve.sem_inc(v.tick, 1)
                    for k in range(K):
                        dve.bn_aggr(mv[:, k, :], bst[:, k, :]).then_inc(aggr_done, 1)
                g = i - 3
                if live(g):
                    s = (par - 3) % 2
                    dve.wait_ge(exp_done, g + 1)
                    dve.scalar_tensor_tensor(out=y[:, :], in0=xw[:, s, :], scalar=v.bias[:, :], in1=ps_b[:, :],
                                             op0=ALU.add, op1=ALU.mult).then_inc(y_done, 1)
                    wait(dve, back_done, g - 1)
                    dve.wait_ge(y_done, g + 1)
                    dve.tensor_tensor_scan(S[:, s, :], keepf[:, :], y[:, :], S[:, 1 - s, T - 1:T],
                                           ALU.mult, ALU.add).then_inc(S_done, 1)
                    dve.tensor_tensor_scan(D[:, s, :], keepf[:, :], ps_b[:, :], D[:, 1 - s, T - 1:T],
                                           ALU.mult, ALU.add).then_inc(D_done, 1)
                g = i - 1
                if live(g):
                    s = (par - 1) % 2
                    dve.wait_ge(rstd_done, g + 1)
                    wait(dve, zT_done, g - 1)
                    for k in range(K):
                        last = dve.tensor_scalar(z[:, s, k, :], xg[:, s, k, :], mv[:, k, 0:1], rstd[:, k:k + 1],
                                                 ALU.subtract, ALU.mult)
                    last.then_inc(z_done, 1)
                g = i - 2
                if live(g):
                    s = (par - 2) % 2
                    dve.wait_ge(raw_done, g + 1)
                    dve.scalar_tensor_tensor(out=L[:, :], in0=ps_l[:, :], scalar=SLOPE, in1=raw_l[:, :],
                                             op0=ALU.mult, op1=ALU.max).then_inc(L_done, 1)
                    wait(dve, back_done, g - 1)
                    dve.tensor_copy(M[:, s, 0:1], M[:, 1 - s, T:T + 1])
                    dve.wait_ge(start_done, g + 1)
                    dve.wait_ge(L_done, g + 1)
                    dve.tensor_tensor_scan(M[:, s, 1:T + 1], ps_a[:, :], L[:, :], M[:, 1 - s, T:T + 1],
                                           ALU.add, ALU.max).then_inc(M_done, 1)
                    dve.wait_ge(M_done, g + 1)
                    dve.tensor_tensor(ps_a[:, :], M[:, s, 0:T], ps_a[:, :], ALU.add).then_inc(u_done, 1)
                    wait(dve, exp_done, g)
                    dve.tensor_tensor(ps_b[:, :], L[:, :], M[:, s, 1:T + 1], ALU.subtract)
                    dve.wait_ge(u_done, g + 1)
                    dve.tensor_tensor(ps_a[:, :], ps_a[:, :], M[:, s, 1:T + 1], ALU.subtract).then_inc(arg_done, 1)

            staged(dve, 3, body)

        @block.scalar
        def _(act):
            act.preload_act_table_set("natural_log_exp_and_others")
            def body(i, par):
                g = i - 2
                if live(g):
                    act.wait_ge(zT_done, g + 1)
                    wait(act, w_done, g)
                    act.activation(hT[:, :], ps_z[:, :], ACT.Relu).then_inc(relu_done, 1)
                g = i - 3
                if live(g):
                    act.wait_ge(arg_done, g + 1)
                    wait(act, D_done, g)
                    act.activation(ps_b[:, :], ps_b[:, :], ACT.Exp)
                    act.activation(keepf[:, :], ps_a[:, :], ACT.Exp).then_inc(exp_done, 1)
                g = i - 1
                if live(g):
                    act.wait_ge(aggr_done, (g + 1) * K)
                    wait(act, z_done, g)
                    act.activation(lnv[:, :], mv[:, :, 1], ACT.Ln, bias=v.eps[:, :]).then_inc(ln_done, 1)
                    act.wait_ge(ln_done, g + 1)
                    act.activation(rstd[:, :], lnv[:, :], ACT.Exp, scale=-0.5).then_inc(rstd_done, 1)
                g = i - 2
                if live(g):
                    s = (par - 2) % 2
                    act.wait_ge(w_done, g + 1)
                    wait(act, y_done, g - 1)
                    act.activation(xw[:, s, :], ps_x[:, :], ACT.Identity, bias=v.b_lin[:, :]).then_inc(xw_done, 1)
                    act.wait_ge(l_done, g + 1)
                    wait(act, L_done, g)
                    act.activation(raw_l[:, :], ps_l[:, :], ACT.Copy).then_inc(raw_done, 1)
                g = i - 3
                if live(g):
                    s = (par - 3) % 2
                    act.wait_ge(back_done, g + 1)
                    wait(act, row_out[s], (g - s) * 8)
                    act.activation(row[:, s, :, 0:P], ps_S[:, :, :], ACT.Copy)
                    act.activation(row[:, s, :, P:P + H], ps_D[:, :, 0:P:P // H], ACT.Copy)
                    act.activation(row[:, s, :, P + H:ROW], ps_M[:, :, 0:P:P // H], ACT.Copy).then_inc(row_done, 1)

            staged(act, 3, body)

        @block.tensor
        def _(pe):
            def body(i, par):
                g = i - 2
                if live(g):
                    s = (par - 2) % 2
                    pe.wait_ge(z_done, g + 1)
                    wait(pe, relu_done, g)
                    for k in range(K):
                        last = pe.transpose(ps_z[:, k * P:(k + 1) * P], z[:, s, k, :], v.ident[:, :])
                    last.then_inc(zT_done, 1)
                g = i - 2
                if live(g):
                    s = (par - 2) % 2
                    pe.wait_ge(relu_done, g + 1)
                    wait(pe, xw_done, g)
                    pe.matmul(ps_x[:, :], v.w_ext[:, 0:P], hT[:, :], start=True, stop=True).then_inc(w_done, 1)
                    pe.wait_ge(start_in[s], (g - s) * 8 + 16)
                    wait(pe, exp_done, g)
                    pe.matmul(ps_a[:, :], v.ones16[:, :], start[:, s, :], start=True, stop=True).then_inc(start_done, 1)
                    pe.wait_ge(xw_done, g + 1)
                    wait(pe, L_done, g)
                    pe.matmul(ps_l[:, :], v.alpha_all[:, :], xw[:, s, :], start=True, stop=True).then_inc(l_done, 1)
                g = i - 3
                if live(g):
                    s = (par - 3) % 2
                    pe.wait_ge(S_done, g + 1)
                    wait(pe, row_done, g)
                    for k in range(K):
                        pe.transpose(ps_S[:, k, :], S[:, s, k * P:(k + 1) * P], v.ident[:, :])
                        pe.transpose(ps_M[:, k, :], M[:, s, k * P + 1:(k + 1) * P + 1], v.ident[:, :])
                    pe.wait_ge(D_done, g + 1)
                    for k in range(K):
                        last = pe.transpose(ps_D[:, k, :], D[:, s, k * P:(k + 1) * P], v.ident[:, :])
                    last.then_inc(back_done, 1)

            staged(pe, 3, body)


def nodes0(nc, v):
    f32, ALU, ACT, AX = v.f32, v.ALU, v.ACT, v.AX
    with ExitStack() as ctx:
        def sb(name, shape, dt=f32):
            return ctx.enter_context(nc.sbuf_tensor(name, shape, dt))

        def pb(name, shape):
            return ctx.enter_context(nc.psum_tensor(name, shape, f32))

        def sem(name):
            v.used.append(nc.alloc_semaphore(name))
            return v.used[-1]

        x = sb("n0_x", [P, 4, K, P])
        place = sb("n0_place", [P, 4, K], v.i32)
        sums = sb("n0_sums", [P, 4, K, ROW])
        bst = sb("n0_bst", [P, K, 6])
        mv = sb("n0_mv", [P, K, 2])
        lnv = sb("n0_lnv", [P, K])
        rstd = sb("n0_rstd", [P, K])
        off = sb("n0_off", [P, K])
        h = sb("n0_h", [P, K, P])
        hT = sb("n0_hT", [P, T])
        raw_l = sb("n0_raw_l", [P, K, H])
        L = sb("n0_L", [P, K, H])
        empty = sb("n0_empty", [P, K, H])
        me = sb("n0_me", [P, K, H])
        top = sb("n0_top", [P, K, H])
        arg = sb("n0_arg", [P, 2, K, H])
        ex = sb("n0_ex", [P, 2, K, H])
        den = sb("n0_den", [P, K, H])
        rden = sb("n0_rden", [P, K, H])
        w = sb("n0_w", [P, 2, 2, K, H])
        own = sb("n0_own", [P, 2, K, P])
        fe = sb("n0_fe", [P, K, P])
        rest = sb("n0_rest", [P, 2, K, P])
        x1 = sb("n0_x1", [P, 2, K, P])
        bst1 = sb("n0_bst1", [P, K, 6])
        mv1 = sb("n0_mv1", [P, 2, K, 2])
        lnv1 = sb("n0_lnv1", [P, K])
        rstd1 = sb("n0_rstd1", [P, 2, K])
        off1 = sb("n0_off1", [P, 2, K])
        h1 = sb("n0_h1", [P, 2, K, P])
        prod = sb("n0_prod", [P, K, P])
        s2 = sb("n0_s2", [P, 2, K])
        ps_z = pb("n0_psz", [P, T])
        ps_x = pb("n0_psx", [P, 2, K, 256])

        names = ("stats", "aggr", "ln", "rstd", "off", "h", "zT", "relu", "xw", "raw", "L", "soft", "top", "arg", "ex",
                 "w", "own", "fe", "rest", "x1", "stats1", "aggr1", "ln1", "rstd1", "off1", "h1", "prod", "s2")
        q = {n: sem(f"n0_{n}") for n in names}
        x_in = [sem(f"n0_x_in{s}") for s in range(4)]
        got = [sem(f"n0_got{s}") for s in range(4)]
        place_in = [sem(f"n0_place_in{s}") for s in range(4)]
        x_out = [sem("n0_x_out0"), sem("n0_x_out1")]
        h_out = [sem("n0_h_out0"), sem("n0_h_out1")]
        s_out = [sem("n0_s_out0"), sem("n0_s_out1")]
        block = ctx.enter_context(nc.Block())

        def group(dram, g):
            return dram[bass.ds(node_rows(g), T), :].rearrange("(p k) d -> p k d", k=K)

        def by_head(a):
            return a.rearrange("p k (h c) -> p k h c", h=H)

        def spread(a):
            return a.rearrange("p k (h a) -> p k h a", a=1).broadcast_to([P, K, H, P // H])

        @block.sync
        def _(sp):
            def body(i, par):
                g = i - 7
                if live(g):
                    s = half(par, 7)
                    at = FRESH if isinstance(g, int) and g == NG - 1 else 0
                    sp.wait_ge(q["s2"], (g + 1) * K)
                    sp.sem_inc(v.tick, 1)
                    s2_rows = v.s2_d[bass.ds(node_rows(g), T), :].rearrange("(p k) d -> p (k d)", k=K)
                    sp.dma_start(s2_rows[at:P], s2[at:P, s, :]).then_inc(s_out[s], 16)
                g = i
                if live(g):
                    s = par
                    wait(sp, q["rest"], g - 3)
                    wait(sp, q["h"], g - 3)
                    sp.dma_start(x[:, s, :, :], group(v.x_d, g)).then_inc(x_in[s], 16)
                    wait(sp, got[s], (g - s) * (4 * K))
                    sp.sem_inc(v.tick, 1)
                    sp.dma_start(place[:, s, :], v.place_d[bass.ds(node_rows(g), T), :]
                                 .rearrange("(p k) a -> p (k a)", k=K)).then_inc(place_in[s], 16)
                g = i - 5
                if live(g):
                    s = half(par, 5)
                    at = FRESH if isinstance(g, int) and g == NG - 1 else 0
                    sp.wait_ge(q["h1"], g + 1)
                    sp.sem_inc(v.tick, 1)
                    sp.dma_start(group(v.x1_d, g)[at:P], x1[at:P, s, :, :]).then_inc(x_out[s], 16)
                    sp.dma_start(group(v.h1_d, g)[at:P], h1[at:P, s, :, :]).then_inc(h_out[s], 16)

            staged4(sp, 7, body)
            for s in range(2):
                sp.wait_ge(x_out[s], NG // 2 * 16)
                sp.wait_ge(h_out[s], NG // 2 * 16)
                sp.wait_ge(s_out[s], NG // 2 * 16)

        @block.gpsimd
        def _(pool):
            bound = pool.to_reg(EMPTY)

            def body(i, par):
                g = i - 1
                if live(g):
                    s4 = (par - 1) % 4
                    wait(pool, q["w"], g - 3)
                    wait(pool, q["fe"], g - 3)
                    pool.wait_ge(place_in[s4], (g - s4) * 4 + 16)
                    pool.sem_inc(v.tick, 1)
                    for k in range(K):
                        pool.indirect_dma_start(out=sums[:, s4, k, :], out_offset=None, in_=v.sums0[:, :],
                                                in_offset=bass.IndirectOffsetOnAxis(ap=place[:, s4, k:k + 1], axis=0),
                                                bounds_check=bound, oob_is_err=False).then_inc(got[s4], 16)
                g = i - 3
                if live(g):
                    s, s4 = half(par, 3), (par - 3) % 4
                    pool.wait_ge(q["w"], g + 1)
                    wait(pool, q["rest"], g)
                    pool.tensor_tensor(by_head(fe[:, :, :]), by_head(sums[:, s4, :, 0:P]), spread(w[:, s, 0, :, :]),
                                       ALU.mult).then_inc(q["fe"], 1)
                    wait(pool, q["x1"], g - 1)
                    pool.wait_ge(x_in[s4], (g - s4) * 4 + 16)
                    pool.wait_ge(q["fe"], g + 1)
                    pool.tensor_tensor(rest[:, s, :, :], fe[:, :, :], x[:, s4, :, :], ALU.add).then_inc(q["rest"], 1)

            staged4(pool, 3, body)

        @block.scalar
        def _(act):
            act.preload_act_table_set("natural_log_exp_and_others")

            def body(i, par):
                g = i - 2
                if live(g):
                    act.wait_ge(q["zT"], g + 1)
                    wait(act, q["xw"], g)
                    act.activation(hT[:, :], ps_z[:, :], ACT.Copy).then_inc(q["relu"], 1)
                g = i - 5
                if live(g):
                    s = half(par, 5)
                    act.wait_ge(q["aggr1"], (g + 1) * K)
                    act.activation(lnv1[:, :], mv1[:, s, :, 1], ACT.Ln, bias=v.eps[:, :]).then_inc(q["ln1"], 1)
                    act.wait_ge(q["ln1"], g + 1)
                    act.activation(rstd1[:, s, :], lnv1[:, :], ACT.Exp, scale=-0.5).then_inc(q["rstd1"], 1)
                g = i - 1
                if live(g):
                    act.wait_ge(q["aggr"], (g + 1) * K)
                    wait(act, q["off"], g)
                    act.activation(lnv[:, :], mv[:, :, 1], ACT.Ln, bias=v.eps[:, :]).then_inc(q["ln"], 1)
                    wait(act, q["h"], g)
                    act.wait_ge(q["ln"], g + 1)
                    act.activation(rstd[:, :], lnv[:, :], ACT.Exp, scale=-0.5).then_inc(q["rstd"], 1)
                g = i - 3
                if live(g):
                    act.wait_ge(q["arg"], g + 1)
                    wait(act, q["w"], g)
                    act.activation(ex[:, :, :, :], arg[:, :, :, :], ACT.Exp).then_inc(q["ex"], 1)
                g = i - 1
                if live(g):
                    s4 = (par - 1) % 4
                    act.wait_ge(q["off"], g + 1)
                    wait(act, q["zT"], g)
                    for k in range(K):
                        last = act.activation(h[:, k, :], x[:, s4, k, :], ACT.Relu, bias=off[:, k:k + 1],
                                              scale=rstd[:, k:k + 1])
                    last.then_inc(q["h"], 1)
                g = i - 5
                if live(g):
                    s = half(par, 5)
                    act.wait_ge(q["off1"], g + 1)
                    wait(act, h_out[s], (g - s) * 8)
                    wait(act, q["s2"], (g - 1) * K)
                    for k in range(K):
                        last = act.activation(h1[:, s, k, :], x1[:, s, k, :], ACT.Relu, bias=off1[:, s, k:k + 1],
                                              scale=rstd1[:, s, k:k + 1])
                    last.then_inc(q["h1"], 1)
                g = i - 2
                if live(g):
                    s = half(par, 2)
                    act.wait_ge(q["xw"], g + 1)
                    wait(act, q["L"], g)
                    act.activation(raw_l[:, :, :], ps_x[:, s, :, P:P + H], ACT.Copy).then_inc(q["raw"], 1)
            staged4(act, 5, body)

        @block.vector
        def _(dve):
            def body(i, par):
                stats_g, weigh_g, sum_g, s2_g = i - 1, i - 3, i - 5, i - 6
                if live(sum_g):
                    g, s = sum_g, half(par, 5)
                    dve.wait_ge(q["rest"], g + 1)
                    wait(dve, x_out[s], (g - s) * 8)
                    wait(dve, q["h1"], g - 1)
                    dve.wait_ge(q["own"], g + 1)
                    dve.tensor_tensor(x1[:, s, :, :], own[:, s, :, :], rest[:, s, :, :], ALU.add).then_inc(q["x1"], 1)
                if live(stats_g):
                    g, s4 = stats_g, (par - 1) % 4
                    dve.wait_ge(x_in[s4], (g - s4) * 4 + 16)
                    for k in range(K):
                        dve.bn_stats(bst[:, k, :], x[:, s4, k, :]).then_inc(q["stats"], 1)
                if live(weigh_g):
                    g, s4 = weigh_g, (par - 3) % 4
                    dve.wait_ge(got[s4], (g - s4) * (4 * K) + 16 * K)
                    dve.tensor_scalar(empty[:, :, :], sums[:, s4, :, P:P + H], 0.0, -BIG, ALU.is_equal, ALU.mult)\
                       .then_inc(q["soft"], 1)
                    dve.wait_ge(q["raw"], g + 1)
                    dve.scalar_tensor_tensor(out=L[:, :, :], in0=raw_l[:, :, :], scalar=SLOPE, in1=raw_l[:, :, :],
                                             op0=ALU.mult, op1=ALU.max).then_inc(q["L"], 1)
                if live(sum_g):
                    g, s = sum_g, half(par, 5)
                    dve.wait_ge(q["x1"], g + 1)
                    for k in range(K):
                        dve.bn_stats(bst1[:, k, :], x1[:, s, k, :]).then_inc(q["stats1"], 1)
                if live(weigh_g):
                    g, s4 = weigh_g, (par - 3) % 4
                    dve.wait_ge(q["soft"], g * 5 + 1)
                    dve.tensor_tensor(me[:, :, :], sums[:, s4, :, P + H:ROW], empty[:, :, :], ALU.add)\
                       .then_inc(q["soft"], 1)
                if live(stats_g):
                    g = stats_g
                    dve.wait_ge(q["stats"], (g + 1) * K)
                    dve.sem_inc(v.tick, 1)
                    for k in range(K):
                        dve.bn_aggr(mv[:, k, :], bst[:, k, :]).then_inc(q["aggr"], 1)
                if live(weigh_g):
                    g = weigh_g
                    dve.wait_ge(q["soft"], g * 5 + 2)
                    dve.wait_ge(q["L"], g + 1)
                    dve.tensor_tensor(top[:, :, :], me[:, :, :], L[:, :, :], ALU.max).then_inc(q["top"], 1)
                if live(sum_g):
                    g, s = sum_g, half(par, 5)
                    dve.wait_ge(q["stats1"], (g + 1) * K)
                    dve.sem_inc(v.tick, 1)
                    for k in range(K):
                        dve.bn_aggr(mv1[:, s, k, :], bst1[:, k, :]).then_inc(q["aggr1"], 1)
                if live(weigh_g):
                    g = weigh_g
                    dve.wait_ge(q["top"], g + 1)
                    dve.tensor_tensor(arg[:, 0, :, :], me[:, :, :], top[:, :, :], ALU.subtract)
                    dve.tensor_tensor(arg[:, 1, :, :], L[:, :, :], top[:, :, :], ALU.subtract).then_inc(q["arg"], 1)

                def score_row(k):
                    if live(s2_g):
                        g, s = s2_g, half(par, 6)
                        if k == 0:
                            dve.wait_ge(q["h1"], g + 1)
                            wait(dve, s_out[s], (g - s) * 8)
                        wait(dve, q["s2"], (g - 1) * K + (k + 1))
                        dve.tensor_tensor_reduce(prod[:, k, :], h1[:, s, k, :], v.w_att2_all[:, :], 1.0, 0.0, ALU.mult,
                                                 ALU.add, s2[:, s, k:k + 1]).then_inc(q["s2"], 1)

                score_row(0)
                score_row(1)
                if live(weigh_g):
                    g, s4 = weigh_g, (par - 3) % 4
                    dve.wait_ge(q["ex"], g + 1)
                    dve.tensor_tensor(den[:, :, :], ex[:, 0, :, :], sums[:, s4, :, P:P + H], ALU.mult)\
                       .then_inc(q["soft"], 1)
                if live(sum_g):
                    g, s = sum_g, half(par, 5)
                    dve.wait_ge(q["rstd1"], g + 1)
                    dve.scalar_tensor_tensor(out=off1[:, s, :], in0=mv1[:, s, :, 0], scalar=-1.0, in1=rstd1[:, s, :],
                                             op0=ALU.mult, op1=ALU.mult).then_inc(q["off1"], 1)
                if live(weigh_g):
                    g = weigh_g
                    dve.wait_ge(q["soft"], g * 5 + 3)
                    dve.tensor_tensor(den[:, :, :], den[:, :, :], ex[:, 1, :, :], ALU.add).then_inc(q["soft"], 1)
                if live(stats_g):
                    g = stats_g
                    dve.wait_ge(q["rstd"], g + 1)
                    wait(dve, q["h"], g)
                    dve.scalar_tensor_tensor(out=off[:, :], in0=mv[:, :, 0], scalar=-1.0, in1=rstd[:, :],
                                             op0=ALU.mult, op1=ALU.mult).then_inc(q["off"], 1)
                if live(weigh_g):
                    g = weigh_g
                    dve.wait_ge(q["soft"], g * 5 + 4)
                    dve.reciprocal(rden[:, :, :], den[:, :, :]).then_inc(q["soft"], 1)
                score_row(2)
                if live(weigh_g):
                    g, s = weigh_g, half(par, 3)
                    dve.wait_ge(q["soft"], g * 5 + 5)
                    wait(dve, q["fe"], g - 1)
                    dve.tensor_tensor(w[:, s, :, :, :].rearrange("p a k h -> p a (k h)"),
                                      ex[:, :, :, :].rearrange("p a k h -> p a (k h)"),
                                      rden[:, :, :].rearrange("p (a k) h -> p a (k h)", a=1).broadcast_to([P, 2, K * H]),
                                      ALU.mult).then_inc(q["w"], 1)
                score_row(3)
                if live(weigh_g):
                    g, s = weigh_g, half(par, 3)
                    dve.wait_ge(q["w"], g + 1)
                    dve.tensor_tensor(by_head(own[:, s, :, :]), by_head(ps_x[:, s, :, 0:P]), spread(w[:, s, 1, :, :]),
                                      ALU.mult).then_inc(q["own"], 1)

            staged4(dve, 6, body)

        @block.tensor
        def _(pe):
            def body(i, par):
                g = i - 2
                if live(g):
                    s = half(par, 2)
                    pe.wait_ge(q["h"], g + 1)
                    wait(pe, q["relu"], g)
                    for k in range(K):
                        last = pe.transpose(ps_z[:, k * P:(k + 1) * P], h[:, k, :], v.ident[:, :])
                    last.then_inc(q["zT"], 1)
                    pe.wait_ge(q["relu"], g + 1)
                    wait(pe, q["own"], g - 1)
                    wait(pe, q["raw"], g - 1)
                    for k in range(K):
                        pe.matmul(ps_x[:, s, k, 0:P + H], hT[:, k * P:(k + 1) * P], v.w_ext[:, :], start=True, stop=False)
                        last = pe.matmul(ps_x[:, s, k, 0:P + H], v.ones[:, :], v.b_ext[:, :], start=False, stop=True)
                    last.then_inc(q["xw"], 1)

            staged4(pe, 2, body)


def edges1(nc, v):
    f32, i32, ALU, ACT = v.f32, v.i32, v.ALU, v.ACT
    with ExitStack() as ctx:
        def sb(name, shape, dt=f32):
            return ctx.enter_context(nc.sbuf_tensor(name, shape, dt))

        def pb(name, shape):
            return ctx.enter_context(nc.psum_tensor(name, shape, f32))

        def sem(name):
            v.used.append(nc.alloc_semaphore(name))
            return v.used[-1]

        gi = sb("e1_gi", [P, 2, K, 2], i32)
        hg = sb("e1_hg", [P, 2, K, P])
        sg = sb("e1_sg", [P, 2, K])
        hT = sb("e1_hT", [P, 2, T])
        lin = sb("e1_lin", [P, 2, T])
        arg = sb("e1_arg", [P, K])
        ex = sb("e1_ex", [P, K])
        ex1 = sb("e1_ex1", [P, K])
        att = sb("e1_att", [P, 2, K])
        same = sb("e1_same", [1, 2, T], v.bf16)
        y = sb("e1_y", [P, T])
        S = sb("e1_S", [P, 2, T])
        row = sb("e1_row", [P, 2, K, P])
        ps_h, ps_m, ps_s, ps_c, ps_t, ps_r = (pb(f"e1_ps{n}", [P, T]) for n in "hmsctr")

        names = ("idx", "hT", "hTs", "s1", "msg", "lin", "arg", "ex", "ex1", "att", "bc", "y", "S", "back", "row")
        q = {n: sem(f"e1_{n}") for n in names}
        got = [sem("e1_got0"), sem("e1_got1")]
        same_in = [sem("e1_same_in0"), sem("e1_same_in1")]
        row_out = [sem("e1_row_out0"), sem("e1_row_out1")]
        block = ctx.enter_context(nc.Block())

        @block.gpsimd
        def _(pool):
            bound = pool.to_reg(N - 1)

            def body(i, par):
                g = i
                if live(g):
                    s = par
                    wait(pool, q["hT"], g - 1)
                    wait(pool, q["arg"], g - 1)
                    pool.tensor_copy(gi[:, s, :, :], v.ends_idx[:, bass.ds(g * K, K), :]).then_inc(q["idx"], 1)
                    pool.wait_ge(q["idx"], g + 1)
                    pool.sem_inc(v.tick, 1)
                    for k in range(K):
                        for a, (out, table) in enumerate(((hg[:, s, k, :], v.h1_d), (sg[:, s, k:k + 1], v.s2_d))):
                            pool.indirect_dma_start(out=out, out_offset=None, in_=table[:, :],
                                                    in_offset=bass.IndirectOffsetOnAxis(ap=gi[:, s, k, a:a + 1], axis=0),
                                                    bounds_check=bound, oob_is_err=False).then_inc(got[s], 16)

            staged(pool, 0, body)

        @block.sync
        def _(sp):
            def body(i, par):
                g = i
                if live(g):
                    s = par
                    wait(sp, q["bc"], g - 1)
                    sp.dma_start(same[:, s, :], v.same_d[bass.ds(g * T, T)].rearrange("(a n) -> a n", a=1))\
                      .then_inc(same_in[s], 16)
                g = i - 3
                if live(g):
                    s = (par - 3) % 2
                    sp.wait_ge(q["row"], g + 1)
                    sp.dma_start(v.sums1[bass.ds(g * T, T), :].rearrange("(p k) d -> p k d", k=K), row[:, s, :, :])\
                      .then_inc(row_out[s], 16)

            staged(sp, 3, body)
            for s in range(2):
                sp.wait_ge(row_out[s], NG // 2 * 16)

        @block.vector
        def _(dve):
            dve.memset(S[:, 1, T - 1:T], 0.0)
            dve.drain()

            def body(i, par):
                g = i - 1
                if live(g):
                    s = (par - 1) % 2
                    dve.wait_ge(q["s1"], g + 1)
                    wait(dve, q["ex"], g)
                    dve.tensor_tensor(arg[:, :], ps_s[:, 0:K], sg[:, s, :], ALU.add).then_inc(q["arg"], 1)
                    dve.wait_ge(q["ex"], g + 1)
                    dve.tensor_scalar(ex1[:, :], ex[:, :], 1.0, None, ALU.add).then_inc(q["ex1"], 1)
                    wait(dve, q["bc"], g - 1)
                    dve.wait_ge(q["ex1"], g + 1)
                    dve.reciprocal(att[:, s, :], ex1[:, :]).then_inc(q["att"], 1)
                    dve.wait_ge(q["att"], g + 1)
                g = i - 2
                if live(g):
                    s = (par - 2) % 2
                    dve.wait_ge(q["bc"], g + 1)
                    dve.wait_ge(q["lin"], g + 1)
                    dve.tensor_tensor(y[:, :], lin[:, s, :], ps_t[:, :], ALU.mult).then_inc(q["y"], 1)
                    wait(dve, q["back"], g - 1)
                    dve.wait_ge(q["y"], g + 1)
                    dve.tensor_tensor_scan(S[:, s, :], ps_c[:, :], y[:, :], S[:, 1 - s, T - 1:T],
                                           ALU.mult, ALU.add).then_inc(q["S"], 1)
                    dve.wait_ge(q["S"], g + 1)

            staged(dve, 2, body)

        @block.scalar
        def _(act):
            act.preload_act_table_set("natural_log_exp_and_others")
            def body(i, par):
                g = i - 1
                if live(g):
                    s = (par - 1) % 2
                    act.wait_ge(q["hT"], g + 1)
                    wait(act, q["msg"], g - 1)
                    act.activation(hT[:, s, :], ps_h[:, :], ACT.Copy).then_inc(q["hTs"], 1)
                    act.wait_ge(q["arg"], g + 1)
                    wait(act, q["ex1"], g)
                    act.activation(ex[:, :], arg[:, :], ACT.Exp, scale=-1.0, bias=v.minus_b_att[:, :]).then_inc(q["ex"], 1)
                    act.wait_ge(q["msg"], g + 1)
                    wait(act, q["y"], g - 1)
                    act.activation(lin[:, s, :], ps_m[:, :], ACT.Identity, bias=v.b_msg[:, :]).then_inc(q["lin"], 1)
                g = i - 2
                if live(g):
                    s = (par - 2) % 2
                    act.wait_ge(q["back"], g + 1)
                    wait(act, row_out[s], (g - s) * 8)
                    act.activation(row[:, s, :, :].rearrange("p k d -> p (k d)"), ps_r[:, :], ACT.Copy).then_inc(q["row"], 1)

            staged(act, 2, body)

        @block.tensor
        def _(pe):
            def body(i, par):
                g = i - 1
                if live(g):
                    s = (par - 1) % 2
                    pe.wait_ge(got[s], (g - s) * (16 * K) + 32 * K)
                    wait(pe, q["hTs"], g)
                    for k in range(K):
                        last = pe.transpose(ps_h[:, k * P:(k + 1) * P], hg[:, s, k, :], v.ident[:, :])
                    last.then_inc(q["hT"], 1)
                g = i - 2
                if live(g):
                    s = (par - 2) % 2
                    pe.wait_ge(q["att"], g + 1)
                    pe.wait_ge(same_in[s], (g - s) * 8 + 16)
                    wait(pe, q["S"], g)
                    pe.matmul(ps_c[:, :], v.ones16[:, :], same[:, s, :], start=True, stop=True)
                    for k in range(K):
                        last = pe.matmul(ps_t[:, k * P:(k + 1) * P], att[:, s, k:k + 1].broadcast_to([P, P]),
                                         v.ident[:, :], start=True, stop=True)
                    last.then_inc(q["bc"], 1)
                g = i - 1
                if live(g):
                    s = (par - 1) % 2
                    pe.wait_ge(q["hTs"], g + 1)
                    wait(pe, q["arg"], g)
                    for k in range(K):
                        last = pe.matmul(ps_s[:, k:k + 1], hT[:, s, k * P:(k + 1) * P], v.w_att1[:, :], start=True, stop=True)
                    last.then_inc(q["s1"], 1)
                    wait(pe, q["lin"], g)
                    pe.matmul(ps_m[:, :], v.w_msg[:, :], hT[:, s, :], start=True, stop=True).then_inc(q["msg"], 1)
                g = i - 2
                if live(g):
                    s = (par - 2) % 2
                    pe.wait_ge(q["S"], g + 1)
                    wait(pe, q["row"], g)
                    for k in range(K):
                        last = pe.transpose(ps_r[:, k * P:(k + 1) * P], S[:, s, k * P:(k + 1) * P], v.ident[:, :])
                    last.then_inc(q["back"], 1)

            staged(pe, 2, body)


def nodes1(nc, v):
    f32, ALU, ACT = v.f32, v.ALU, v.ACT
    with ExitStack() as ctx:
        def sb(name, shape, dt=f32):
            return ctx.enter_context(nc.sbuf_tensor(name, shape, dt))

        def pb(name, shape):
            return ctx.enter_context(nc.psum_tensor(name, shape, f32))

        def sem(name):
            v.used.append(nc.alloc_semaphore(name))
            return v.used[-1]

        place = sb("n1_place", [P, 4, K], v.i32)
        h = sb("n1_h", [P, 4, K, P])
        a = sb("n1_a", [P, 4, K, P])
        hT = sb("n1_hT", [P, 2, T])
        aT = sb("n1_aT", [P, 2, T])
        r = sb("n1_r", [P, T])
        zg = sb("n1_zg", [P, 2, T])
        t1 = sb("n1_t1", [P, T])
        t2 = sb("n1_t2", [P, T])
        n = sb("n1_n", [P, 2, T])
        d = sb("n1_d", [P, T])
        e = sb("n1_e", [P, 2, T])
        hn = sb("n1_hn", [P, 2, T])
        ps_h, ps_a = pb("n1_psh", [P, T]), pb("n1_psa", [P, T])
        ps_r, ps_z, ps_i, ps_n = (pb(f"n1_ps{c}", [P, T]) for c in "rzin")
        names = ("T", "hT", "aT", "gr", "gz", "gn", "r", "z", "t1", "t2", "n", "d", "e", "hn", "st")
        q = {c: sem(f"n1_{c}") for c in names}
        rows_in = [sem(f"n1_in{s}") for s in range(4)]
        got = [sem(f"n1_got{s}") for s in range(4)]
        place_in = [sem(f"n1_place_in{s}") for s in range(4)]
        out = [sem("n1_out0"), sem("n1_out1")]
        block = ctx.enter_context(nc.Block())

        def group(dram, g):
            return dram[bass.ds(node_rows(g), T), :].rearrange("(p k) d -> p k d", k=K)

        @block.sync
        def _(sp):
            def body(i, par):
                g = i
                if live(g):
                    s = par
                    wait(sp, got[s], (g - s) * (4 * K))
                    sp.sem_inc(v.tick, 1)
                    sp.dma_start(place[:, s, :], v.place_d[bass.ds(node_rows(g), T), :]
                                 .rearrange("(p k) a -> p (k a)", k=K)).then_inc(place_in[s], 16)
                    wait(sp, q["T"], g - 3)
                    sp.dma_start(h[:, s, :, :], group(v.h1_d, g)).then_inc(rows_in[s], 16)
                g = i - 5
                if live(g):
                    s = half(par, 5)
                    sp.wait_ge(q["hn"], g + 1)
                    sp.dma_start(v.hn_d[:, bass.ds(g * T, T)], hn[:, s, :]).then_inc(out[s], 16)

            staged4(sp, 5, body)
            for s in range(2):
                sp.wait_ge(out[s], NG // 2 * 16)

        @block.tensor
        def _(pe):
            def body(i, par):
                g = i - 3
                if live(g):
                    s = (par - 3) % 4
                    pe.wait_ge(rows_in[s], (g - s) * 4 + 16)
                    pe.wait_ge(got[s], (g - s) * (4 * K) + 16 * K)
                    wait(pe, q["aT"], g)
                    for k in range(K):
                        pe.transpose(ps_h[:, k * P:(k + 1) * P], h[:, s, k, :], v.ident[:, :])
                    for k in range(K):
                        last = pe.transpose(ps_a[:, k * P:(k + 1) * P], a[:, s, k, :], v.ident[:, :])
                    last.then_inc(q["T"], 1)
                g = i - 4
                if live(g):
                    s = half(par, 4)
                    pe.wait_ge(q["aT"], g + 1)
                    wait(pe, q["r"], g)
                    pe.matmul(ps_r[:, :], v.w_hhT[:, 0:P], hT[:, s, :], start=True, stop=False)
                    pe.matmul(ps_r[:, :], v.w_ihT[:, 0:P], aT[:, s, :], start=False, stop=True).then_inc(q["gr"], 1)
                    wait(pe, q["t2"], g)
                    pe.matmul(ps_n[:, :], v.w_hhT[:, 2 * P:3 * P], hT[:, s, :], start=True, stop=True)
                    pe.matmul(ps_i[:, :], v.w_ihT[:, 2 * P:3 * P], aT[:, s, :], start=True, stop=True).then_inc(q["gn"], 1)
                    wait(pe, q["z"], g)
                    pe.matmul(ps_z[:, :], v.w_hhT[:, P:2 * P], hT[:, s, :], start=True, stop=False)
                    pe.matmul(ps_z[:, :], v.w_ihT[:, P:2 * P], aT[:, s, :], start=False, stop=True).then_inc(q["gz"], 1)

            staged4(pe, 4, body)

        @block.scalar
        def _(act):
            act.preload_act_table_set("sigmoid_and_others")
            def body(i, par):
                g = i - 3
                if live(g):
                    s = half(par, 3)
                    act.wait_ge(q["T"], g + 1)
                    wait(act, q["gz"], g - 1)
                    wait(act, q["d"], g - 1)
                    act.activation(hT[:, s, :], ps_h[:, :], ACT.Copy)
                    act.activation(aT[:, s, :], ps_a[:, :], ACT.Copy).then_inc(q["aT"], 1)
                g = i - 4
                if live(g):
                    s = half(par, 4)
                    act.wait_ge(q["gr"], g + 1)
                    wait(act, q["t1"], g)
                    act.activation(r[:, :], ps_r[:, :], ACT.Sigmoid, bias=v.b_gate[:, 0:1]).then_inc(q["r"], 1)
                    act.wait_ge(q["gz"], g + 1)
                    wait(act, q["e"], g - 1)
                    act.activation(zg[:, s, :], ps_z[:, :], ACT.Sigmoid, bias=v.b_gate[:, 1:2]).then_inc(q["z"], 1)
                    act.wait_ge(q["t2"], g + 1)
                    wait(act, q["hn"], g - 1)
                    act.activation(n[:, s, :], t2[:, :], ACT.Tanh, bias=v.b_ih[:, 2:3]).then_inc(q["n"], 1)

            staged4(act, 4, body)

        @block.vector
        def _(dve):
            def body(i, par):
                g = i - 4
                if live(g):
                    dve.wait_ge(q["gn"], g + 1)
                    dve.wait_ge(q["r"], g + 1)
                    dve.scalar_tensor_tensor(out=t1[:, :], in0=ps_n[:, :], scalar=v.b_hh[:, 2:3], in1=r[:, :],
                                             op0=ALU.add, op1=ALU.mult).then_inc(q["t1"], 1)
                    dve.wait_ge(q["t1"], g + 1)
                    wait(dve, q["n"], g)
                    dve.tensor_tensor(t2[:, :], t1[:, :], ps_i[:, :], ALU.add).then_inc(q["t2"], 1)
                g = i - 5
                if live(g):
                    s = half(par, 5)
                    dve.wait_ge(q["hn"], g + 1)
                    lo = FRESH if isinstance(g, int) and g == NG - 1 else 0
                    part = hn[:, s, :].rearrange("p (k n) -> p k n", k=K)[:, :, lo:P]
                    dve.bn_stats(v.stats[:, bass.ds(g, 1), :], part).then_inc(q["st"], 1)
                g = i - 4
                if live(g):
                    s = half(par, 4)
                    dve.wait_ge(q["n"], g + 1)
                    dve.tensor_tensor(d[:, :], hT[:, s, :], n[:, s, :], ALU.subtract).then_inc(q["d"], 1)
                    wait(dve, q["hn"], g - 1)
                    dve.wait_ge(q["z"], g + 1)
                    dve.wait_ge(q["d"], g + 1)
                    dve.tensor_tensor(e[:, s, :], d[:, :], zg[:, s, :], ALU.mult).then_inc(q["e"], 1)
                    dve.wait_ge(q["e"], g + 1)

            staged4(dve, 5, body)

        @block.gpsimd
        def _(pool):
            bound = pool.to_reg(EMPTY)

            def body(i, par):
                g = i - 1
                if live(g):
                    s = (par - 1) % 4
                    wait(pool, q["T"], g - 3)
                    pool.wait_ge(place_in[s], (g - s) * 4 + 16)
                    pool.sem_inc(v.tick, 1)
                    for k in range(K):
                        pool.indirect_dma_start(out=a[:, s, k, :], out_offset=None, in_=v.sums1[:, :],
                                                in_offset=bass.IndirectOffsetOnAxis(ap=place[:, s, k:k + 1], axis=0),
                                                bounds_check=bound, oob_is_err=False).then_inc(got[s], 16)
                g = i - 4
                if live(g):
                    s = half(par, 4)
                    wait(pool, out[s], (g - s) * 8)
                    wait(pool, q["st"], g - 1)
                    pool.wait_ge(q["e"], g + 1)
                    pool.tensor_tensor(hn[:, s, :], e[:, s, :], n[:, s, :], ALU.add).then_inc(q["hn"], 1)

            staged4(pool, 4, body)


def finish(nc, v):
    f32, ALU, ACT = v.f32, v.ALU, v.ACT
    with ExitStack() as ctx:
        def sb(name, shape, dt=f32):
            return ctx.enter_context(nc.sbuf_tensor(name, shape, dt))

        def sem(name):
            v.used.append(nc.alloc_semaphore(name))
            return v.used[-1]

        mv = sb("f_mv", [P, 2])
        sd = sb("f_sd", [P, 1])
        rs = sb("f_rs", [P, 1])
        scale = sb("f_scale", [P, 1])
        ms = sb("f_ms", [P, 1])
        shift = sb("f_shift", [P, 1])
        hn = sb("f_hn", [P, 4, T])
        x1 = sb("f_x1", [P, 4, K, P])
        bn = sb("f_bn", [P, 2, T])
        o = sb("f_o", [P, 2, K, P])
        ps = [ctx.enter_context(nc.psum_tensor(f"f_ps{s}", [P, T], f32)) for s in range(2)]
        chain, ready = sem("f_chain"), sem("f_ready")
        bn_done, T_done, o_done, sd_done, sd_in = sem("f_bn_done"), sem("f_T_done"), sem("f_o_done"), sem("f_sd_done"), sem("f_sd_in")
        rows_in = [sem(f"f_in{s}") for s in range(4)]
        out = [sem("f_out0"), sem("f_out1")]
        block = ctx.enter_context(nc.Block())

        def group(dram, g):
            return dram[bass.ds(node_rows(g), T), :].rearrange("(p k) d -> p k d", k=K)

        @block.sync
        def _(sp):
            def body(i, par):
                g = i
                if live(g):
                    s = par
                    wait(sp, bn_done, g - 3)
                    wait(sp, o_done, g - 3)
                    sp.dma_start(hn[:, s, :], v.hn_d[:, bass.ds(g * T, T)]).then_inc(rows_in[s], 16)
                    sp.dma_start(x1[:, s, :, :], group(v.x1_d, g)).then_inc(rows_in[s], 16)

            staged4(sp, 0, body)

        @block.scalar
        def _(act):
            act.wait_ge(sd_in, 1)
            act.activation(sd[:, :], mv[:, 1:2], ACT.Sqrt, bias=v.eps[:, :]).then_inc(sd_done, 1)
            act.wait_ge(ready, 1)

            def body(i, par):
                g = i - 1
                if live(g):
                    s = (par - 1) % 2
                    s4 = (par - 1) % 4
                    act.wait_ge(rows_in[s4], (g - s4) * 8 + 32)
                    wait(act, T_done, g - 1)
                    act.activation(bn[:, s, :], hn[:, s4, :], ACT.Identity, bias=shift[:, :], scale=scale[:, :])\
                       .then_inc(bn_done, 1)
                g = i - 2
                if live(g):
                    s = (par - 2) % 2
                    at = FRESH if isinstance(g, int) and g == NG - 1 else 0
                    act.wait_ge(o_done, g + 1)
                    act.dma_start(group(v.out_d, g)[at:P], o[at:P, s, :, :]).then_inc(out[s], 16)

            staged4(act, 2, body)
            for s in range(2):
                act.wait_ge(out[s], NG // 2 * 16)

        @block.vector
        def _(dve):
            links = [0]

            def link(ins):
                links[0] += 1
                ins.then_inc(chain, 1)
                dve.wait_ge(chain, links[0])

            dve.bn_aggr(mv[:, :], v.stats[:, :, :].rearrange("p g s -> p (g s)")).then_inc(sd_in, 1)
            dve.wait_ge(sd_in, 1)
            dve.wait_ge(sd_done, 1)
            link(dve.reciprocal(rs[:, :], sd[:, :]))
            link(dve.tensor_tensor(scale[:, :], rs[:, :], v.gamma[:, :], ALU.mult))
            link(dve.tensor_tensor(ms[:, :], mv[:, 0:1], scale[:, :], ALU.mult))
            dve.tensor_tensor(shift[:, :], v.beta[:, :], ms[:, :], ALU.subtract).then_inc(ready, 1)

            def body(i, par):
                g = i - 2
                if live(g):
                    s = (par - 2) % 2
                    dve.wait_ge(T_done, g + 1)
                    wait(dve, out[s], (g - s) * 8)
                    dve.tensor_tensor(o[:, s, :, :].rearrange("p k d -> p (k d)"), ps[s][:, :],
                                      x1[:, (par - 2) % 4, :, :].rearrange("p k d -> p (k d)"), ALU.add).then_inc(o_done, 1)

            staged4(dve, 2, body)

        @block.tensor
        def _(pe):
            def body(i, par):
                g = i - 2
                if live(g):
                    s = (par - 2) % 2
                    pe.wait_ge(bn_done, g + 1)
                    wait(pe, o_done, g - 1)
                    for k in range(K):
                        last = pe.transpose(ps[s][:, k * P:(k + 1) * P], bn[:, s, k * P:(k + 1) * P], v.ident[:, :])
                    last.then_inc(T_done, 1)

            staged4(pe, 2, body)


_INS = ["x", "src", "dst", "L0_gnn_W", "L0_gnn_b_lin", "L0_gnn_alpha", "L0_gnn_bias", "L1_gnn_W_msg", "L1_gnn_b_msg",
        "L1_gnn_W_att", "L1_gnn_b_att", "L1_gnn_W_ih", "L1_gnn_b_ih", "L1_gnn_W_hh", "L1_gnn_b_hh", "L1_gnn_gamma",
        "L1_gnn_beta"]
_SCRATCH = {"sums0": (EMPTY + 1, ROW), "sums1": (EMPTY + 1, P), "x1": (N, P), "h1": (N, P), "s2": (N, 1), "same": (NT * P,),
            "start": (NT * P,), "hnew": (P, NG * T)}
DEBUG = False


def kernel(**inputs):
    import numpy as np
    import concourse.bacc as bacc
    from concourse.bass_utils import run_bass_kernel_spmd

    nc = bacc.Bacc("TRN2", target_bir_lowering=False, num_devices=1)
    arrays, io = {}, {}
    for name in _INS:
        a = np.ascontiguousarray(inputs[name])
        arrays[f"in_{name}"] = a
        io[name] = nc.dram_tensor(f"in_{name}", a.shape, mybir.dt.from_np(a.dtype), kind="ExternalInput").ap()
    io["out"] = nc.dram_tensor("out", (N, P), mybir.dt.float32, kind="ExternalOutput").ap()
    kind = "ExternalOutput" if DEBUG else "Internal"
    scratch = {n: nc.dram_tensor(f"scratch_{n}", (E, 1), mybir.dt.int32, kind="Internal").ap() for n in ("src_s", "dst_s", "place")}
    scratch |= {n: nc.dram_tensor(f"scratch_{n}", s, mybir.dt.bfloat16 if n in ("same", "start") else mybir.dt.float32,
                                  kind=kind).ap() for n, s in _SCRATCH.items()}
    build(nc, io, scratch)
    r = run_bass_kernel_spmd(nc, [arrays], core_ids=[0])
    return r.results[0]["out"]
```

```python
import concourse.bass as bass
from concourse import mybir
from contextlib import ExitStack

P = 128
N = 50000
E = 50000
T = 512
K = T // P
NG = -(-E // T)
NT = NG * K
CH = 4
CT = NT // CH
H = 4
ROW = P + 2 * H
EMPTY = NG * T
LAST = N - T
FRESH = (NG * T - N) // K
KEPT = 60
PAD = 70000.0
NOWHERE = 60000.0
BIG = 1e30
EPS = 1e-5
SLOPE = 0.2


def wait(eng, sem, count):
    if not (isinstance(count, int) and count <= 0):
        eng.wait_ge(sem, count)


def staged(eng, depth, body):
    head = depth + 2 + depth % 2
    for i in range(head):
        body(i, i % 2)
    end = NG - 2
    with eng.Fori(0, (end - head) // 2) as turn:
        body(turn * 2 + head, 0)
        body(turn * 2 + (head + 1), 1)
    for i in range(end, NG + depth):
        body(i, i % 2)


def staged4(eng, depth, body):
    head = -(-(depth + 3) // 4) * 4
    for i in range(head):
        body(i, i % 4)
    end = head + (NG - 1 - head) // 4 * 4
    with eng.Fori(0, (end - head) // 4) as turn:
        for j in range(4):
            body(turn * 4 + (head + j), j)
    for i in range(end, NG + depth):
        body(i, i % 4)


def staged_kept(eng, depth, body):
    head = -(-(depth + 3) // 4) * 4
    mixed = head + (KEPT - head) // 4 * 4
    after = -(-(KEPT + depth) // 4) * 4
    end = after + (NG - 1 - after) // 4 * 4
    for i in range(head):
        body(i, i % 4, None)
    with eng.Fori(0, (mixed - head) // 4) as turn:
        for j in range(4):
            body(turn * 4 + (head + j), j, True)
    for i in range(mixed, after):
        body(i, i % 4, None)
    with eng.Fori(0, (end - after) // 4) as turn:
        for j in range(4):
            body(turn * 4 + (after + j), j, False)
    for i in range(end, NG + depth):
        body(i, i % 4, None)


def is_kept(g, all_kept):
    return g < KEPT if isinstance(g, int) else all_kept


def half(par, off):
    return (par - off) % 2


def live(g):
    return not isinstance(g, int) or 0 <= g < NG


def node_rows(g):
    if isinstance(g, int):
        return min(g * T, LAST)
    return g * T


class Shared:
    pass


def build(nc, io, scratch):
    v = Shared()
    v.io = io
    v.used = []
    v.f32, v.i32, v.bf16 = mybir.dt.float32, mybir.dt.int32, mybir.dt.bfloat16
    v.ACT, v.ALU, v.AX = mybir.ActivationFunctionType, mybir.AluOpType, mybir.AxisListType
    v.sums0, v.sums1, v.x1_d, v.h1_d, v.hT_d, v.s2_d, v.same_d, v.start_d, v.hn_d = (
        scratch[n] for n in ("sums0", "sums1", "x1", "h1", "h1T", "s2", "same", "start", "hnew"))
    v.x_d, v.out_d = io["x"], io["out"]
    v.src_s, v.dst_s, v.place_d = scratch["src_s"], scratch["dst_s"], scratch["place"]
    v.src_sorted, v.dst_sorted = (a[:, :].rearrange("n a -> (n a)") for a in (v.src_s, v.dst_s))

    with ExitStack() as whole:
        def keep(name, shape, dt=v.f32):
            return whole.enter_context(nc.sbuf_tensor(name, shape, dt))

        v.ident = keep("ident", [P, P])
        v.ones16 = keep("ones16", [1, P], v.bf16)
        v.w_ext = keep("w_ext", [P, P + H])
        v.b_ext = keep("b_ext", [1, P + H])
        v.b_parts = keep("b_parts", [1, 3, P + H], v.bf16)
        v.alpha = keep("alpha", [P, H])
        v.alpha_all = keep("alpha_all", [P, P])
        v.b_lin = keep("b_lin", [P, 1])
        v.bias = keep("bias", [P, 1])
        v.w_msg = keep("w_msg", [P, P])
        v.b_msg = keep("b_msg", [P, 1])
        v.w_att1 = keep("w_att1", [P, 1])
        v.w_att2_all = keep("w_att2_all", [P, P])
        v.b_att = keep("b_att", [P, 1])
        v.minus_b_att = keep("minus_b_att", [P, 1])
        v.w_ihT = keep("w_ihT", [P, 3 * P])
        v.w_hhT = keep("w_hhT", [P, 3 * P])
        v.b_ih = keep("b_ih", [P, 3])
        v.b_hh = keep("b_hh", [P, 3])
        v.b_gate = keep("b_gate", [P, 2])
        v.gamma = keep("gamma", [P, 1])
        v.beta = keep("beta", [P, 1])
        v.eps = keep("eps", [P, 1])
        v.ends_idx = keep("ends_idx", [P, NT, 2], v.i32)
        v.place_idx = keep("place_idx", [P, NT, 3], v.i32)
        v.stats = keep("stats", [P, NG, 6])

        v.tick = whole.enter_context(nc.semaphore("tick"))

        order(nc, v)
        prepare(nc, v)
        edges0(nc, v)
        nc.clear_and_free_semaphores(v.used)
        nc.all_engine_barrier()
        v.used = []
        nodes0(nc, v)
        v.kept = keep("kept", [P, KEPT * T])
        edges1(nc, v)
        nodes1(nc, v)
        finish(nc, v)


def order(nc, v):
    f32, i32, ALU, AX = v.f32, v.i32, v.ALU, v.AX
    src, dst = v.io["src"], v.io["dst"]
    with ExitStack() as ctx:
        def sb(name, shape, dt=f32):
            return ctx.enter_context(nc.sbuf_tensor(name, shape, dt))

        def sem(name):
            v.used.append(nc.alloc_semaphore(name))
            return v.used[-1]

        W = 390
        B = NT * P // 8
        near = sb("o_near", [P, 2, 2, W], i32)
        falls = sb("o_falls", [P, 2, W])
        fell = sb("o_fell", [P, 1])
        fell_all = sb("o_fell_all", [1, 1], i32)
        ones_col = sb("o_ones", [P, 1])
        ps = ctx.enter_context(nc.psum_tensor("o_ps", [1, 512], f32))
        cols = sb("o_cols", [P, 2, NT], i32)
        key = sb("o_key", [P, 2, NT])
        one = sb("o_one", [P, 2])
        number = sb("o_number", [P, NT], i32)
        along = sb("o_along", [P, B], i32)
        alongf = sb("o_alongf", [P, B])
        rowi = sb("o_rowi", [P, B], i32)
        rowf = sb("o_rowf", [P, B])
        before = sb("o_before", [P, B])
        count = sb("o_count", [P, 1])
        rank = sb("o_rank", [P, NT])
        ranki = sb("o_ranki", [P, NT], i32)
        at = sb("o_at", [P, 3], i32)
        copied, near_in, fell_done, summed, told = (sem(f"o_{n}") for n in (
            "copied", "near_in", "fell_done", "summed", "told"))
        blank, cols_in, numbers, row_in, row_used, ranked, picked, placed = (sem(f"o_{n}") for n in (
            "blank", "cols_in", "numbers", "row_in", "row_used", "ranked", "picked", "placed"))
        block = ctx.enter_context(nc.Block())

        @block.sync
        def _(sp):
            for first in (0, E - 1 - P * W):
                for shift in range(2):
                    a = first + shift
                    sp.dma_start(near[:, min(first, 1), shift, :], dst[a:a + P * W].rearrange("(p w) -> p w", p=P))\
                      .then_inc(near_in, 16)
            for out, array in ((v.src_s, src), (v.dst_s, dst)):
                sp.dma_start(out[:, :].rearrange("(p w) a -> p (w a)", p=80), array.rearrange("(p w) -> p w", p=80))\
                  .then_inc(copied, 16)
            sp.wait_ge(copied, 32)
            sp.wait_ge(told, 1)
            wrong = sp.value_load(fell_all[0:1, 0:1], min_val=0, max_val=E)
            with sp.If(wrong > 0):
                sp.wait_ge(blank, 1)
                for a, array in enumerate((dst, src)):
                    whole = E // P
                    with nc.allow_non_contiguous_dma(reason="only for edges that come unordered"):
                        sp.dma_start(cols[:, a, 0:whole], array[0:whole * P].rearrange("(t p) -> p t", p=P))\
                          .then_inc(cols_in, 16)
                        sp.dma_start(cols[0:E % P, a, whole:whole + 1],
                                     array[whole * P:E].rearrange("(p t) -> p t", t=1)).then_inc(cols_in, 16)

                def row(b, width):
                    sp.dma_start(rowi[:, 0:width], dst[bass.ds(b * B, width)].rearrange("(a n) -> a n", a=1)
                                 .broadcast_to([P, width])).then_inc(row_in, 16)

                row(0, B)
                with sp.Fori(0, 6) as b:
                    sp.wait_ge(row_used, b + 1)
                    row(b + 1, B)
                sp.wait_ge(row_used, 8)
                row(7, E - 7 * B)

        @block.vector
        def _(dve):
            dve.memset(ones_col[:, :], 1.0).then_inc(fell_done, 1)
            dve.wait_ge(near_in, 64)
            dve.tensor_tensor(falls[:, :, :], near[:, :, 0, :], near[:, :, 1, :], ALU.is_gt)
            dve.drain()
            dve.tensor_reduce(out=fell[:, :], in_=falls[:, :, :].rearrange("p a w -> p (a w)"), axis=AX.X, op=ALU.add)\
               .then_inc(fell_done, 1)
            dve.wait_ge(summed, 1)
            dve.tensor_scalar(fell_all[0:1, 0:1], ps[0:1, 0:1], float(E), None, ALU.min).then_inc(told, 1)
            dve.wait_ge(told, 1)
            wrong = dve.value_load(fell_all[0:1, 0:1], min_val=0, max_val=E)
            with dve.If(wrong > 0):
                dve.memset(cols[:, 0, :], int(PAD))
                dve.memset(cols[:, 1, :], 0).then_inc(blank, 1)
                dve.memset(rank[:, :], 0.0)
                dve.wait_ge(numbers, 2)
                dve.wait_ge(cols_in, 64)
                dve.tensor_copy(alongf[:, :], along[:, :])
                dve.tensor_copy(key[:, 1, :], number[:, :])
                dve.tensor_scalar(key[:, 0, :], cols[:, 0, :], 65536.0, None, ALU.mult)

                def block_of_edges(b):
                    dve.wait_ge(row_in, b * 16 + 16)
                    dve.tensor_scalar(rowf[:, :], rowi[:, :], 65536.0, None, ALU.mult)
                    dve.drain()
                    dve.sem_inc(row_used, 1)
                    with dve.Fori(0, NT) as t:
                        dve.tensor_copy(one[:, :], key[:, :, bass.ds(t, 1)].rearrange("p a t -> p (a t)"))
                        dve.drain()
                        dve.scalar_tensor_tensor(out=before[:, :], in0=rowf[:, :], scalar=one[:, 0:1], in1=alongf[:, :],
                                                 op0=ALU.subtract, op1=ALU.add)
                        dve.drain()
                        dve.tensor_scalar(before[:, :], before[:, :], one[:, 1:2], 0.0, ALU.is_lt, ALU.add,
                                          accum_out=count[:, :])
                        dve.drain()
                        dve.tensor_tensor(rank[:, bass.ds(t, 1)], rank[:, bass.ds(t, 1)], count[:, :], ALU.add)
                    dve.drain()
                    dve.tensor_scalar(key[:, 1, :], key[:, 1, :], float(B), None, ALU.subtract)
                    dve.drain()

                dve.drain()
                with dve.Fori(0, 7) as b:
                    block_of_edges(b)
                dve.memset(rowi[:, E - 7 * B:B], int(PAD)).then_inc(row_used, 1)
                dve.wait_ge(row_used, 8)
                block_of_edges(7)
                dve.tensor_copy(ranki[:, :], rank[:, :]).then_inc(ranked, 1)

        @block.tensor
        def _(pe):
            pe.wait_ge(fell_done, 2)
            pe.matmul(ps[0:1, 0:1], fell[:, :], ones_col[:, :], start=True, stop=True).then_inc(summed, 1)

        @block.gpsimd
        def _(pool):
            pool.wait_ge(told, 1)
            wrong = pool.value_load(fell_all[0:1, 0:1], min_val=0, max_val=E)
            with pool.If(wrong > 0):
                pool.iota(along[:, :], pattern=[[1, B]], base=0, channel_multiplier=0).then_inc(numbers, 1)
                pool.iota(number[:, :], pattern=[[P, NT]], base=0, channel_multiplier=1).then_inc(numbers, 1)
                bound = pool.to_reg(E - 1)
                pool.wait_ge(copied, 32)
                pool.wait_ge(cols_in, 64)
                pool.wait_ge(ranked, 1)
                pool.sem_inc(v.tick, 1)
                with pool.Fori(0, NT) as t:
                    pool.tensor_copy(at[:, 0:1], ranki[:, bass.ds(t, 1)])
                    pool.tensor_copy(at[:, 1:3], cols[:, :, bass.ds(t, 1)].rearrange("p a t -> p (a t)"))\
                        .then_inc(picked, 1)
                    pool.wait_ge(picked, t + 1)
                    pool.sem_inc(v.tick, 1)
                    for a, out in ((1, v.dst_s), (2, v.src_s)):
                        pool.indirect_dma_start(out=out[:, :], out_offset=bass.IndirectOffsetOnAxis(ap=at[:, 0:1], axis=0),
                                                in_=at[:, a:a + 1], in_offset=None, bounds_check=bound, oob_is_err=False)\
                            .then_inc(placed, 16)
                    pool.wait_ge(placed, t * 32 + 32)
                    pool.sem_inc(v.tick, 1)


def prepare(nc, v):
    f32, i32, ALU = v.f32, v.i32, v.ALU
    io = v.io
    with ExitStack() as ctx:
        def sb(name, shape, dt=f32):
            return ctx.enter_context(nc.sbuf_tensor(name, shape, dt))

        def sem(name):
            v.used.append(nc.alloc_semaphore(name))
            return v.used[-1]

        raw = [sb(f"raw_{n}", [CT, CH, P], i32) for n in ("src", "dst", "prev", "next")]
        flt = [sb(f"flt_{n}", [CT, CH, P]) for n in ("src", "dst", "prev", "next")]
        same = sb("same", [CT, CH, P])
        same16 = sb("same16", [CT, CH, P], v.bf16)
        start = sb("start", [CT, CH, P], v.bf16)
        ends = sb("ends", [CT, CH, P])
        put = sb("put", [CT, CH, P])
        place = sb("place", [P, NT], i32)
        inside = sb("inside", [CT, CH, P])
        w_ih = sb("w_ih", [P, 3, P])
        w_hh = sb("w_hh", [P, 3, P])
        wT = sb("wT", [P, P])
        zeros = sb("zeros", [1, ROW])
        bias_row = sb("bias_row", [1, P])
        left = sb("left", [1, P + H])
        nowhere = sb("nowhere", [80, N // 80], i32)
        ps_t = ctx.enter_context(nc.psum_tensor("ps_t", [P, 3, 512], f32))
        ps_w = ctx.enter_context(nc.psum_tensor("ps_w", [P, 2, 512], f32))
        ps_a = ctx.enter_context(nc.psum_tensor("ps_a", [P, 3, 512], f32))

        weights_in, edges_in, filled, cleared = sem("weights_in"), sem("edges_in"), sem("filled"), sem("cleared")
        zeros_set, raw_set, consts, consts2, flt_ready = sem("zeros_set"), sem("raw_set"), sem("consts"), sem("consts2"), sem("flt_ready")
        chain, tables, tables_out = sem("chain"), sem("tables"), sem("tables_out")
        edges_T, weights_T, wT_ready, folded, bfold = (sem(n) for n in ("edges_T", "weights_T", "wT_ready", "folded", "bfold"))
        idx_done, alpha_zero, alpha_in, w_in, gates = (sem(n) for n in ("idx_done", "alpha_zero", "alpha_in", "w_in", "gates"))
        block = ctx.enter_context(nc.Block())
        full = (E // P) - (CH - 1) * CT
        rest = E % P
        weight_loads = [0]

        @block.sync
        def _(sp):
            sp.wait_ge(raw_set, 1)
            n = 0

            def load(dst, src):
                sp.dma_start(dst, src).then_inc(edges_in, 16)

            def rows(a, lo, count):
                return a[lo:lo + count * P].rearrange("(t p) -> t p", p=P)

            for a, (buf, array) in enumerate(((raw[0], v.src_sorted), (raw[1], v.dst_sorted))):
                for c in range(CH - 1):
                    load(buf[:, c, :], rows(array, c * CT * P, CT))
                load(buf[0:full, CH - 1, :], rows(array, (CH - 1) * CT * P, full))
                load(buf[full:full + 1, CH - 1, 0:rest], array[E - rest:E].rearrange("(a n) -> a n", a=1))
            load(raw[2][0:1, 0, 1:P], v.dst_sorted[0:P - 1].rearrange("(a n) -> a n", a=1))
            load(raw[2][1:CT, 0, :], rows(v.dst_sorted, P - 1, CT - 1))
            for c in range(1, CH - 1):
                load(raw[2][:, c, :], rows(v.dst_sorted, c * CT * P - 1, CT))
            load(raw[2][0:full, CH - 1, :], rows(v.dst_sorted, (CH - 1) * CT * P - 1, full))
            load(raw[2][full:full + 1, CH - 1, 0:rest], v.dst_sorted[E - rest - 1:E - 1].rearrange("(a n) -> a n", a=1))
            for c in range(CH - 1):
                load(raw[3][:, c, :], rows(v.dst_sorted, c * CT * P + 1, CT))
            load(raw[3][0:full, CH - 1, :], rows(v.dst_sorted, (CH - 1) * CT * P + 1, full))
            load(raw[3][full:full + 1, CH - 1, 0:rest - 1], v.dst_sorted[E - rest + 1:E].rearrange("(a n) -> a n", a=1))
            sp.wait_ge(tables, 2)
            for table, t in ((v.same_d, same16), (v.start_d, start)):
                sp.dma_start(table[:].rearrange("(c t p) -> t c p", c=CH, t=CT), t[:, :, :]).then_inc(tables_out, 16)
            sp.wait_ge(tables_out, 32)

        @block.scalar
        def _(act):
            def load(dst, src):
                weight_loads[0] += 1
                act.dma_start(dst, src).then_inc(weights_in, 16)

            def column(a):
                return a.rearrange("(p a) -> p a", a=1)

            load(v.w_ext[:, 0:P], io["L0_gnn_W"])
            load(v.b_lin[:, :], column(io["L0_gnn_b_lin"]))
            load(v.b_ext[:, 0:P], io["L0_gnn_b_lin"].rearrange("(a n) -> a n", a=1))
            load(v.bias[:, :], column(io["L0_gnn_bias"]))
            load(bias_row[:, :], io["L0_gnn_bias"].rearrange("(a n) -> a n", a=1))
            load(v.w_msg[:, :], io["L1_gnn_W_msg"])
            load(v.b_msg[:, :], column(io["L1_gnn_b_msg"]))
            load(v.w_att1[:, :], io["L1_gnn_W_att"][0:P, :])
            load(v.w_att2_all[:, :], io["L1_gnn_W_att"][P:2 * P, :].rearrange("n a -> a n").broadcast_to([P, P]))
            load(v.b_att[:, :], io["L1_gnn_b_att"].rearrange("(a n) -> a n", a=1).broadcast_to([P, 1]))
            load(w_ih[:, :, :], io["L1_gnn_W_ih"].rearrange("(c r) k -> r c k", c=3))
            load(w_hh[:, :, :], io["L1_gnn_W_hh"].rearrange("(c r) k -> r c k", c=3))
            for c in range(3):
                load(v.b_ih[:, c:c + 1], column(io["L1_gnn_b_ih"][c * P:(c + 1) * P]))
                load(v.b_hh[:, c:c + 1], column(io["L1_gnn_b_hh"][c * P:(c + 1) * P]))
            load(v.gamma[:, :], column(io["L1_gnn_gamma"]))
            load(v.beta[:, :], column(io["L1_gnn_beta"]))
            act.wait_ge(alpha_zero, 1)
            for h in range(2):
                load(v.alpha[64 * h:64 * h + 64, h:h + 1], io["L0_gnn_alpha"][0, h, :].rearrange("(p a) -> p a", a=1))
            act.wait_ge(zeros_set, 1)
            act.dma_start(v.sums0[EMPTY:EMPTY + 1, :], zeros[:, 0:ROW]).then_inc(cleared, 16)
            act.dma_start(v.sums1[EMPTY:EMPTY + 1, :], zeros[:, 0:P]).then_inc(cleared, 16)
            act.dma_start(v.place_d.rearrange("(p w) a -> p (w a)", p=80), nowhere[:, :]).then_inc(cleared, 16)
            act.wait_ge(cleared, 48)

        @block.gpsimd
        def _(pool):
            pool.memset(v.ident[:, :], 0.0).then_inc(consts, 1)
            pool.wait_ge(consts, 1)
            pool.affine_select(out=v.ident[:, :], in_=v.ident[:, :], compare_op=ALU.not_equal, fill=1.0, base=0,
                               pattern=[[-1, P]], channel_multiplier=1).then_inc(consts2, 1)
            pool.iota(place[:, :], pattern=[[T, NG], [1, K]], base=0, channel_multiplier=K).then_inc(consts2, 1)

        @block.vector
        def _(dve):
            links = [0]

            def link(ins):
                links[0] += 1
                ins.then_inc(chain, 1)
                dve.wait_ge(chain, links[0])

            dve.memset(raw[0][:, :, :], 0)
            dve.memset(raw[1][:, :, :], int(PAD))
            dve.memset(raw[3][:, :, :], int(PAD))
            link(dve.memset(raw[2][:, :, :], int(PAD)))
            dve.memset(raw[2][0:1, 0, 0:1], -1).then_inc(raw_set, 1)
            dve.memset(v.alpha[:, :], 0.0).then_inc(alpha_zero, 1)
            dve.memset(nowhere[:, :], EMPTY)
            dve.memset(zeros[:, :], 0.0).then_inc(zeros_set, 1)
            dve.memset(v.ones16[:, :], 1.0)
            dve.memset(v.alpha_all[:, :], 0.0)
            dve.memset(v.eps[:, :], EPS)
            dve.wait_ge(edges_in, 16 * (2 * (CH + 1) + (CH + 2) + (CH + 1)))
            dve.tensor_copy(flt[3][:, :, :], raw[3][:, :, :])
            dve.tensor_copy(flt[2][:, :, :], raw[2][:, :, :])
            dve.tensor_copy(flt[0][:, :, :], raw[0][:, :, :])
            link(dve.tensor_copy(flt[1][:, :, :], raw[1][:, :, :]))
            link(dve.tensor_tensor(same[:, :, :], flt[1][:, :, :], flt[2][:, :, :], ALU.is_equal))
            dve.tensor_copy(same16[:, :, :], same[:, :, :])
            dve.tensor_scalar(start[:, :, :], same[:, :, :], 1.0, BIG, ALU.subtract, ALU.mult).then_inc(tables, 2)
            dve.tensor_tensor(ends[:, :, :], flt[1][:, :, :], flt[3][:, :, :], ALU.not_equal)
            link(dve.tensor_scalar(put[:, :, :], flt[1][:, :, :], NOWHERE, None, ALU.subtract))
            link(dve.tensor_tensor(put[:, :, :], put[:, :, :], ends[:, :, :], ALU.mult))
            dve.tensor_scalar(put[:, :, :], put[:, :, :], NOWHERE, None, ALU.add)
            dve.tensor_scalar(inside[:, :, :], flt[1][:, :, :], float(N - 1), None, ALU.min).then_inc(flt_ready, 1)
            dve.wait_ge(weights_in, 16 * weight_loads[0])
            dve.tensor_tensor(v.b_gate[:, :], v.b_ih[:, 0:2], v.b_hh[:, 0:2], ALU.add)
            dve.tensor_tensor(v.b_ext[:, 0:P], v.b_ext[:, 0:P], bias_row[:, :], ALU.add)
            dve.tensor_scalar(v.minus_b_att[:, :], v.b_att[:, :], -1.0, None, ALU.mult)
            for h in range(2):
                dve.tensor_copy(v.alpha_all[:, h * (P // H):(h + 1) * (P // H)],
                                v.alpha[:, h:h + 1].broadcast_to([P, P // H]))
            dve.wait_ge(edges_T, 1)
            for a, t in enumerate((v.ends_idx[:, :, 0], v.ends_idx[:, :, 1], v.place_idx[:, :, 1])):
                dve.tensor_copy(t, ps_t[:, a, 0:NT])
            dve.tensor_copy(v.place_idx[:, :, 0], ps_t[:, 0, 0:NT])
            dve.wait_ge(consts2, 2)
            dve.tensor_copy(v.place_idx[:, :, 2], place[:, :])
            dve.wait_ge(weights_T, 1)
            dve.tensor_copy(v.w_ihT[:, :], ps_w[:, 0, 0:3 * P])
            dve.tensor_copy(v.w_hhT[:, :], ps_w[:, 1, 0:3 * P])
            dve.tensor_copy(wT[:, :], ps_a[:, 0, 0:P]).then_inc(wT_ready, 1)
            dve.wait_ge(folded, 1)
            dve.tensor_copy(v.w_ext[:, P:P + H], ps_a[:, 1, 0:H])
            link(dve.tensor_copy(v.b_ext[:, P:P + H], ps_a[0:1, 2, 0:H]))
            link(dve.tensor_copy(v.b_parts[:, 0, :], v.b_ext[:, :]))
            link(dve.tensor_tensor(left[:, :], v.b_ext[:, :], v.b_parts[:, 0, :], ALU.subtract))
            link(dve.tensor_copy(v.b_parts[:, 1, :], left[:, :]))
            link(dve.tensor_tensor(left[:, :], left[:, :], v.b_parts[:, 1, :], ALU.subtract))
            dve.tensor_copy(v.b_parts[:, 2, :], left[:, :])

        @block.tensor
        def _(pe):
            pe.wait_ge(consts2, 1)
            pe.wait_ge(flt_ready, 1)
            for a, t in enumerate((flt[0], inside, put)):
                for c in range(CH):
                    last = pe.transpose(ps_t[:, a, c * CT:(c + 1) * CT], t[:, c, :], v.ident[0:CT, 0:CT])
            last.then_inc(edges_T, 1)
            pe.wait_ge(weights_in, 16 * weight_loads[0])
            for c in range(3):
                pe.transpose(ps_w[:, 0, c * P:(c + 1) * P], w_ih[:, c, :], v.ident[:, :])
                pe.transpose(ps_w[:, 1, c * P:(c + 1) * P], w_hh[:, c, :], v.ident[:, :])
            pe.transpose(ps_a[:, 0, 0:P], v.w_ext[:, 0:P], v.ident[:, :]).then_inc(weights_T, 1)
            pe.wait_ge(wT_ready, 1)
            pe.matmul(ps_a[:, 1, 0:H], wT[:, :], v.alpha[:, :], start=True, stop=True)
            pe.matmul(ps_a[0:1, 2, 0:H], v.b_lin[:, :], v.alpha[:, :], start=True, stop=True).then_inc(folded, 1)


def edges0(nc, v):
    f32, i32, ALU, ACT = v.f32, v.i32, v.ALU, v.ACT
    with ExitStack() as ctx:
        def sb(name, shape, dt=f32):
            return ctx.enter_context(nc.sbuf_tensor(name, shape, dt))

        def pb(name, shape):
            return ctx.enter_context(nc.psum_tensor(name, shape, f32))

        def sem(name):
            v.used.append(nc.alloc_semaphore(name))
            return v.used[-1]

        gi = sb("e0_gi", [P, 4, K, 3], i32)
        xg = sb("e0_xg", [P, 4, K, P])
        bst = sb("e0_bst", [P, K, 6])
        mv = sb("e0_mv", [P, K, 2])
        lnv = sb("e0_lnv", [P, K])
        rstd = sb("e0_rstd", [P, K])
        z = sb("e0_z", [P, 2, K, P])
        hT = sb("e0_hT", [P, T])
        xw = sb("e0_xw", [P, 2, T])
        raw_l = sb("e0_raw_l", [P, T])
        L = sb("e0_L", [P, T])
        start = sb("e0_start", [1, 2, T], v.bf16)
        M = sb("e0_M", [P, 2, T + 1])
        keepf = sb("e0_keepf", [P, T])
        y = sb("e0_y", [P, T])
        S = sb("e0_S", [P, 2, T])
        D = sb("e0_D", [P, 2, T])
        row = sb("e0_row", [P, 2, K, ROW])
        ps_z, ps_x, ps_l, ps_a, ps_b = (pb(f"e0_ps{n}", [P, T]) for n in "zxlab")
        ps_S, ps_D, ps_M = (pb(f"e0_ps{n}", [P, K, P]) for n in "SDM")

        idx_copied = sem("e0_idx_copied")
        got = [sem(f"e0_got{s}") for s in range(4)]
        start_in = [sem("e0_start_in0"), sem("e0_start_in1")]
        put = [sem("e0_put0"), sem("e0_put1")]
        stats_done, aggr_done, ln_done, rstd_done, z_done = (sem(f"e0_{n}") for n in ("stats", "aggr", "ln", "rstd", "z"))
        zT_done, relu_done, w_done, xw_done, l_done, L_done, M_done = (sem(f"e0_{n}") for n in ("zT", "relu", "w", "xw", "l", "L", "M"))
        arg_done, exp_done, y_done, S_done, D_done, back_done, row_done = (sem(f"e0_{n}") for n in ("arg", "exp", "y", "S", "D", "back", "row"))
        raw_done = sem("e0_raw")
        row_out = [sem("e0_row_out0"), sem("e0_row_out1")]
        start_done, u_done = sem("e0_start"), sem("e0_u")
        block = ctx.enter_context(nc.Block())

        @block.gpsimd
        def _(pool):
            bound = pool.to_reg(N - 1)

            def body(i, par):
                g = i
                if live(g):
                    s = par % 2
                    wait(pool, z_done, g - 3)
                    pool.wait_ge(idx_copied, g + 1)
                    pool.sem_inc(v.tick, 1)
                    for k in range(K):
                        pool.indirect_dma_start(out=xg[:, par, k, :], out_offset=None, in_=v.x_d[:, :],
                                                in_offset=bass.IndirectOffsetOnAxis(ap=gi[:, par, k, 0:1], axis=0),
                                                bounds_check=bound, oob_is_err=False).then_inc(got[par], 16)
                    for k in range(K):
                        pool.indirect_dma_start(out=v.place_d[:, :],
                                                out_offset=bass.IndirectOffsetOnAxis(ap=gi[:, par, k, 1:2], axis=0),
                                                in_=gi[:, par, k, 2:3], in_offset=None,
                                                bounds_check=bound, oob_is_err=False).then_inc(put[s], 16)

            staged4(pool, 0, body)
            for s in range(2):
                pool.wait_ge(put[s], NG // 2 * 16 * K)

        @block.sync
        def _(sp):
            def body(i, par):
                g = i - 2
                if live(g):
                    s = par
                    wait(sp, start_done, g - 1)
                    src = v.start_d[bass.ds(g * T, T)].rearrange("(a n) -> a n", a=1)
                    sp.dma_start(start[:, s, :], src).then_inc(start_in[s], 16)
                g = i - 4
                if live(g):
                    s = par
                    sp.wait_ge(row_done, g + 1)
                    sp.dma_start(v.sums0[bass.ds(g * T, T), :].rearrange("(p k) d -> p k d", k=K), row[:, s, :, :])\
                      .then_inc(row_out[s], 16)

            staged(sp, 4, body)
            for s in range(2):
                sp.wait_ge(row_out[s], NG // 2 * 16)

        @block.vector
        def _(dve):
            dve.memset(M[:, 1, T:T + 1], -BIG)
            dve.memset(S[:, 1, T - 1:T], 0.0)
            dve.memset(D[:, 1, T - 1:T], 0.0)
            dve.drain()

            def lay_indices(g, s4):
                if live(g):
                    wait(dve, put[s4 % 2], (g - s4 % 2 - 2) * (8 * K))
                    dve.tensor_copy(gi[:, s4, :, :], v.place_idx[:, bass.ds(g * K, K), :]).then_inc(idx_copied, 1)

            lay_indices(0, 0)

            def body(i, par):
                lay_indices(i + 1, (par + 1) % 4)
                g = i - 1
                if live(g):
                    s = (par - 1) % 2
                    s4 = (par - 1) % 4
                    dve.wait_ge(got[s4], (g - s4) * (4 * K) + 16 * K)
                    for k in range(K):
                        dve.bn_stats(bst[:, k, :], xg[:, s4, k, :]).then_inc(stats_done, 1)
                    dve.wait_ge(stats_done, (g + 1) * K)
                    wait(dve, z_done, g)
                    dve.sem_inc(v.tick, 1)
                    for k in range(K):
                        dve.bn_aggr(mv[:, k, :], bst[:, k, :]).then_inc(aggr_done, 1)
                g = i - 3
                if live(g):
                    s = (par - 3) % 2
                    dve.wait_ge(exp_done, g + 1)
                    dve.scalar_tensor_tensor(out=y[:, :], in0=xw[:, s, :], scalar=v.bias[:, :], in1=ps_b[:, :],
                                             op0=ALU.add, op1=ALU.mult).then_inc(y_done, 1)
                    wait(dve, back_done, g - 1)
                    dve.wait_ge(y_done, g + 1)
                    dve.tensor_tensor_scan(S[:, s, :], keepf[:, :], y[:, :], S[:, 1 - s, T - 1:T],
                                           ALU.mult, ALU.add).then_inc(S_done, 1)
                    dve.tensor_tensor_scan(D[:, s, :], keepf[:, :], ps_b[:, :], D[:, 1 - s, T - 1:T],
                                           ALU.mult, ALU.add).then_inc(D_done, 1)
                g = i - 1
                if live(g):
                    s = (par - 1) % 2
                    dve.wait_ge(rstd_done, g + 1)
                    wait(dve, zT_done, g - 1)
                    for k in range(K):
                        last = dve.tensor_scalar(z[:, s, k, :], xg[:, (par - 1) % 4, k, :], mv[:, k, 0:1], rstd[:, k:k + 1],
                                                 ALU.subtract, ALU.mult)
                    last.then_inc(z_done, 1)
                g = i - 2
                if live(g):
                    s = (par - 2) % 2
                    dve.wait_ge(raw_done, g + 1)
                    dve.scalar_tensor_tensor(out=L[:, :], in0=ps_l[:, :], scalar=SLOPE, in1=raw_l[:, :],
                                             op0=ALU.mult, op1=ALU.max).then_inc(L_done, 1)
                    wait(dve, back_done, g - 1)
                    dve.tensor_copy(M[:, s, 0:1], M[:, 1 - s, T:T + 1])
                    dve.wait_ge(start_done, g + 1)
                    dve.wait_ge(L_done, g + 1)
                    dve.tensor_tensor_scan(M[:, s, 1:T + 1], ps_a[:, :], L[:, :], M[:, 1 - s, T:T + 1],
                                           ALU.add, ALU.max).then_inc(M_done, 1)
                    dve.wait_ge(M_done, g + 1)
                    dve.tensor_tensor(ps_a[:, :], M[:, s, 0:T], ps_a[:, :], ALU.add).then_inc(u_done, 1)
                    wait(dve, exp_done, g)
                    dve.tensor_tensor(ps_b[:, :], L[:, :], M[:, s, 1:T + 1], ALU.subtract)
                    dve.wait_ge(u_done, g + 1)
                    dve.tensor_tensor(ps_a[:, :], ps_a[:, :], M[:, s, 1:T + 1], ALU.subtract).then_inc(arg_done, 1)

            staged4(dve, 3, body)

        @block.scalar
        def _(act):
            act.preload_act_table_set("natural_log_exp_and_others")
            def body(i, par):
                g = i - 2
                if live(g):
                    act.wait_ge(zT_done, g + 1)
                    wait(act, w_done, g)
                    act.activation(hT[:, :], ps_z[:, :], ACT.Relu).then_inc(relu_done, 1)
                g = i - 3
                if live(g):
                    act.wait_ge(arg_done, g + 1)
                    wait(act, D_done, g)
                    act.activation(ps_b[:, :], ps_b[:, :], ACT.Exp)
                    act.activation(keepf[:, :], ps_a[:, :], ACT.Exp).then_inc(exp_done, 1)
                g = i - 1
                if live(g):
                    act.wait_ge(aggr_done, (g + 1) * K)
                    wait(act, z_done, g)
                    act.activation(lnv[:, :], mv[:, :, 1], ACT.Ln, bias=v.eps[:, :]).then_inc(ln_done, 1)
                    act.wait_ge(ln_done, g + 1)
                    act.activation(rstd[:, :], lnv[:, :], ACT.Exp, scale=-0.5).then_inc(rstd_done, 1)
                g = i - 2
                if live(g):
                    s = (par - 2) % 2
                    act.wait_ge(w_done, g + 1)
                    wait(act, y_done, g - 1)
                    act.activation(xw[:, s, :], ps_x[:, :], ACT.Identity, bias=v.b_lin[:, :]).then_inc(xw_done, 1)
                    act.wait_ge(l_done, g + 1)
                    wait(act, L_done, g)
                    act.activation(raw_l[:, :], ps_l[:, :], ACT.Copy).then_inc(raw_done, 1)
                g = i - 3
                if live(g):
                    s = (par - 3) % 2
                    act.wait_ge(back_done, g + 1)
                    wait(act, row_out[s], (g - s) * 8)
                    act.activation(row[:, s, :, 0:P], ps_S[:, :, :], ACT.Copy)
                    act.activation(row[:, s, :, P:P + H], ps_D[:, :, 0:P:P // H], ACT.Copy)
                    act.activation(row[:, s, :, P + H:ROW], ps_M[:, :, 0:P:P // H], ACT.Copy).then_inc(row_done, 1)

            staged(act, 3, body)

        @block.tensor
        def _(pe):
            def body(i, par):
                g = i - 2
                if live(g):
                    s = (par - 2) % 2
                    pe.wait_ge(z_done, g + 1)
                    wait(pe, relu_done, g)
                    for k in range(K):
                        last = pe.transpose(ps_z[:, k * P:(k + 1) * P], z[:, s, k, :], v.ident[:, :])
                    last.then_inc(zT_done, 1)
                g = i - 2
                if live(g):
                    s = (par - 2) % 2
                    pe.wait_ge(relu_done, g + 1)
                    wait(pe, xw_done, g)
                    pe.matmul(ps_x[:, :], v.w_ext[:, 0:P], hT[:, :], start=True, stop=True).then_inc(w_done, 1)
                    pe.wait_ge(start_in[s], (g - s) * 8 + 16)
                    wait(pe, exp_done, g)
                    pe.matmul(ps_a[:, :], v.ones16[:, :], start[:, s, :], start=True, stop=True).then_inc(start_done, 1)
                    pe.wait_ge(xw_done, g + 1)
                    wait(pe, L_done, g)
                    pe.matmul(ps_l[:, :], v.alpha_all[:, :], xw[:, s, :], start=True, stop=True).then_inc(l_done, 1)
                g = i - 3
                if live(g):
                    s = (par - 3) % 2
                    pe.wait_ge(S_done, g + 1)
                    wait(pe, row_done, g)
                    for k in range(K):
                        pe.transpose(ps_S[:, k, :], S[:, s, k * P:(k + 1) * P], v.ident[:, :])
                        pe.transpose(ps_M[:, k, :], M[:, s, k * P + 1:(k + 1) * P + 1], v.ident[:, :])
                    pe.wait_ge(D_done, g + 1)
                    for k in range(K):
                        last = pe.transpose(ps_D[:, k, :], D[:, s, k * P:(k + 1) * P], v.ident[:, :])
                    last.then_inc(back_done, 1)

            staged(pe, 3, body)


def nodes0(nc, v):
    f32, ALU, ACT, AX = v.f32, v.ALU, v.ACT, v.AX
    with ExitStack() as ctx:
        def sb(name, shape, dt=f32):
            return ctx.enter_context(nc.sbuf_tensor(name, shape, dt))

        def pb(name, shape):
            return ctx.enter_context(nc.psum_tensor(name, shape, f32))

        def sem(name):
            v.used.append(nc.alloc_semaphore(name))
            return v.used[-1]

        x = sb("n0_x", [P, 4, K, P])
        place = sb("n0_place", [P, 4, K], v.i32)
        sums = sb("n0_sums", [P, 4, K, ROW])
        bst = sb("n0_bst", [P, K, 6])
        mv = sb("n0_mv", [P, K, 2])
        lnv = sb("n0_lnv", [P, K])
        rstd = sb("n0_rstd", [P, K])
        off = sb("n0_off", [P, K])
        h = sb("n0_h", [P, K, P])
        hT = sb("n0_hT", [P, T])
        raw_l = sb("n0_raw_l", [P, K, H])
        L = sb("n0_L", [P, K, H])
        empty = sb("n0_empty", [P, K, H])
        me = sb("n0_me", [P, K, H])
        top = sb("n0_top", [P, K, H])
        arg = sb("n0_arg", [P, 2, K, H])
        ex = sb("n0_ex", [P, 2, K, H])
        den = sb("n0_den", [P, K, H])
        rden = sb("n0_rden", [P, K, H])
        w = sb("n0_w", [P, 2, 2, K, H])
        own = sb("n0_own", [P, 2, K, P])
        fe = sb("n0_fe", [P, 2, K, P])
        x1 = sb("n0_x1", [P, 2, K, P])
        bst1 = sb("n0_bst1", [P, K, 6])
        mv1 = sb("n0_mv1", [P, 2, K, 2])
        lnv1 = sb("n0_lnv1", [P, K])
        rstd1 = sb("n0_rstd1", [P, 2, K])
        off1 = sb("n0_off1", [P, 2, K])
        h1 = sb("n0_h1", [P, 2, K, P])
        prod = sb("n0_prod", [P, K, P])
        s2 = sb("n0_s2", [P, 2, K])
        ps_z = pb("n0_psz", [P, T])
        ps_x = pb("n0_psx", [P, 2, K, 256])
        ps_rest = [pb(f"n0_psr{s}", [P, T]) for s in range(2)]

        names = ("stats", "aggr", "ln", "rstd", "off", "h", "zT", "relu", "xw", "raw", "L", "soft", "top", "arg", "ex",
                 "w", "own", "fe", "rest", "x1", "stats1", "aggr1", "ln1", "rstd1", "off1", "h1", "prod", "s2")
        q = {n: sem(f"n0_{n}") for n in names}
        x_in = [sem(f"n0_x_in{s}") for s in range(4)]
        got = [sem(f"n0_got{s}") for s in range(4)]
        place_in = [sem(f"n0_place_in{s}") for s in range(4)]
        x_out = [sem("n0_x_out0"), sem("n0_x_out1")]
        h_out = [sem("n0_h_out0"), sem("n0_h_out1")]
        s_out = [sem("n0_s_out0"), sem("n0_s_out1")]
        block = ctx.enter_context(nc.Block())

        def group(dram, g):
            return dram[bass.ds(node_rows(g), T), :].rearrange("(p k) d -> p k d", k=K)

        def by_head(a):
            return a.rearrange("p k (h c) -> p k h c", h=H)

        def spread(a):
            return a.rearrange("p k (h a) -> p k h a", a=1).broadcast_to([P, K, H, P // H])

        @block.sync
        def _(sp):
            def body(i, par):
                g = i - 7
                if live(g):
                    s = half(par, 7)
                    at = FRESH if isinstance(g, int) and g == NG - 1 else 0
                    sp.wait_ge(q["s2"], (g + 1) * K)
                    sp.sem_inc(v.tick, 1)
                    s2_rows = v.s2_d[bass.ds(node_rows(g), T), :].rearrange("(p k) d -> p (k d)", k=K)
                    sp.dma_start(s2_rows[at:P], s2[at:P, s, :]).then_inc(s_out[s], 16)
                g = i
                if live(g):
                    s = par
                    wait(sp, q["rest"], g - 3)
                    wait(sp, q["h"], g - 3)
                    sp.dma_start(x[:, s, :, :], group(v.x_d, g)).then_inc(x_in[s], 16)
                    wait(sp, got[s], (g - s) * (4 * K))
                    sp.sem_inc(v.tick, 1)
                    sp.dma_start(place[:, s, :], v.place_d[bass.ds(node_rows(g), T), :]
                                 .rearrange("(p k) a -> p (k a)", k=K)).then_inc(place_in[s], 16)
                g = i - 5
                if live(g):
                    s = half(par, 5)
                    at = FRESH if isinstance(g, int) and g == NG - 1 else 0
                    sp.wait_ge(q["h1"], g + 1)
                    sp.sem_inc(v.tick, 1)
                    sp.dma_start(group(v.x1_d, g)[at:P], x1[at:P, s, :, :]).then_inc(x_out[s], 16)
                    sp.dma_start(group(v.h1_d, g)[at:P], h1[at:P, s, :, :]).then_inc(h_out[s], 16)

            staged4(sp, 7, body)
            for s in range(2):
                sp.wait_ge(x_out[s], NG // 2 * 16)
                sp.wait_ge(h_out[s], NG // 2 * 16)
                sp.wait_ge(s_out[s], NG // 2 * 16)

        @block.gpsimd
        def _(pool):
            bound = pool.to_reg(EMPTY)

            def body(i, par):
                g = i - 1
                if live(g):
                    s4 = (par - 1) % 4
                    wait(pool, q["w"], g - 3)
                    wait(pool, q["fe"], g - 3)
                    pool.wait_ge(place_in[s4], (g - s4) * 4 + 16)
                    pool.sem_inc(v.tick, 1)
                    for k in range(K):
                        pool.indirect_dma_start(out=sums[:, s4, k, :], out_offset=None, in_=v.sums0[:, :],
                                                in_offset=bass.IndirectOffsetOnAxis(ap=place[:, s4, k:k + 1], axis=0),
                                                bounds_check=bound, oob_is_err=False).then_inc(got[s4], 16)
                g = i - 3
                if live(g):
                    s, s4 = half(par, 3), (par - 3) % 4
                    pool.wait_ge(q["w"], g + 1)
                    wait(pool, q["rest"], g - 1)
                    pool.tensor_tensor(by_head(fe[:, s, :, :]), by_head(sums[:, s4, :, 0:P]), spread(w[:, s, 0, :, :]),
                                       ALU.mult).then_inc(q["fe"], 1)

            staged4(pool, 3, body)

        @block.scalar
        def _(act):
            act.preload_act_table_set("natural_log_exp_and_others")

            def body(i, par):
                g = i - 2
                if live(g):
                    act.wait_ge(q["zT"], g + 1)
                    wait(act, q["xw"], g)
                    act.activation(hT[:, :], ps_z[:, :], ACT.Copy).then_inc(q["relu"], 1)
                g = i - 1
                if live(g):
                    act.wait_ge(q["aggr"], (g + 1) * K)
                    wait(act, q["off"], g)
                    act.activation(lnv[:, :], mv[:, :, 1], ACT.Ln, bias=v.eps[:, :]).then_inc(q["ln"], 1)
                    wait(act, q["h"], g)
                    act.wait_ge(q["ln"], g + 1)
                    act.activation(rstd[:, :], lnv[:, :], ACT.Exp, scale=-0.5).then_inc(q["rstd"], 1)
                g = i - 3
                if live(g):
                    act.wait_ge(q["arg"], g + 1)
                    wait(act, q["w"], g)
                    act.activation(ex[:, :, :, :], arg[:, :, :, :], ACT.Exp).then_inc(q["ex"], 1)
                g = i - 5
                if live(g):
                    s = half(par, 5)
                    act.wait_ge(q["aggr1"], (g + 1) * K)
                    act.activation(lnv1[:, :], mv1[:, s, :, 1], ACT.Ln, bias=v.eps[:, :]).then_inc(q["ln1"], 1)
                    act.wait_ge(q["ln1"], g + 1)
                    act.activation(rstd1[:, s, :], lnv1[:, :], ACT.Exp, scale=-0.5).then_inc(q["rstd1"], 1)
                g = i - 1
                if live(g):
                    s4 = (par - 1) % 4
                    act.wait_ge(q["off"], g + 1)
                    wait(act, q["zT"], g)
                    for k in range(K):
                        last = act.activation(h[:, k, :], x[:, s4, k, :], ACT.Relu, bias=off[:, k:k + 1],
                                              scale=rstd[:, k:k + 1])
                    last.then_inc(q["h"], 1)
                g = i - 5
                if live(g):
                    s = half(par, 5)
                    act.wait_ge(q["off1"], g + 1)
                    wait(act, h_out[s], (g - s) * 8)
                    wait(act, q["s2"], (g - 1) * K)
                    for k in range(K):
                        last = act.activation(h1[:, s, k, :], x1[:, s, k, :], ACT.Relu, bias=off1[:, s, k:k + 1],
                                              scale=rstd1[:, s, k:k + 1])
                    last.then_inc(q["h1"], 1)
                g = i - 2
                if live(g):
                    s = half(par, 2)
                    act.wait_ge(q["xw"], g + 1)
                    wait(act, q["L"], g)
                    act.activation(raw_l[:, :, :], ps_x[:, s, :, P:P + H], ACT.Copy).then_inc(q["raw"], 1)

            staged4(act, 5, body)

        @block.vector
        def _(dve):
            def body(i, par):
                stats_g, weigh_g, sum_g, s2_g = i - 1, i - 3, i - 5, i - 6
                def score_row(k):
                    if live(s2_g):
                        g, s = s2_g, half(par, 6)
                        if k == 0:
                            dve.wait_ge(q["h1"], g + 1)
                            wait(dve, s_out[s], (g - s) * 8)
                        wait(dve, q["s2"], (g - 1) * K + (k + 1))
                        dve.tensor_tensor_reduce(prod[:, k, :], h1[:, s, k, :], v.w_att2_all[:, :], 1.0, 0.0, ALU.mult,
                                                 ALU.add, s2[:, s, k:k + 1]).then_inc(q["s2"], 1)

                if live(sum_g):
                    g, s = sum_g, half(par, 5)
                    dve.wait_ge(q["rest"], g + 1)
                    wait(dve, x_out[s], (g - s) * 8)
                    wait(dve, q["h1"], g - 1)
                    dve.wait_ge(q["own"], g + 1)
                    dve.tensor_tensor(x1[:, s, :, :], own[:, s, :, :], ps_rest[s][:, :].rearrange("p (k d) -> p k d", k=K),
                                      ALU.add).then_inc(q["x1"], 1)
                if live(stats_g):
                    g, s4 = stats_g, (par - 1) % 4
                    dve.wait_ge(x_in[s4], (g - s4) * 4 + 16)
                    for k in range(K):
                        dve.bn_stats(bst[:, k, :], x[:, s4, k, :]).then_inc(q["stats"], 1)
                if live(weigh_g):
                    g, s4 = weigh_g, (par - 3) % 4
                    dve.wait_ge(got[s4], (g - s4) * (4 * K) + 16 * K)
                    dve.tensor_scalar(empty[:, :, :], sums[:, s4, :, P:P + H], 0.0, -BIG, ALU.is_equal, ALU.mult)\
                       .then_inc(q["soft"], 1)
                    dve.wait_ge(q["raw"], g + 1)
                    dve.scalar_tensor_tensor(out=L[:, :, :], in0=raw_l[:, :, :], scalar=SLOPE, in1=raw_l[:, :, :],
                                             op0=ALU.mult, op1=ALU.max).then_inc(q["L"], 1)
                if live(weigh_g):
                    g, s4 = weigh_g, (par - 3) % 4
                    dve.wait_ge(q["soft"], g * 5 + 1)
                    dve.tensor_tensor(me[:, :, :], sums[:, s4, :, P + H:ROW], empty[:, :, :], ALU.add)\
                       .then_inc(q["soft"], 1)
                if live(stats_g):
                    g = stats_g
                    dve.wait_ge(q["stats"], (g + 1) * K)
                    dve.sem_inc(v.tick, 1)
                    for k in range(K):
                        dve.bn_aggr(mv[:, k, :], bst[:, k, :]).then_inc(q["aggr"], 1)
                if live(weigh_g):
                    g = weigh_g
                    dve.wait_ge(q["soft"], g * 5 + 2)
                    dve.wait_ge(q["L"], g + 1)
                    dve.tensor_tensor(top[:, :, :], me[:, :, :], L[:, :, :], ALU.max).then_inc(q["top"], 1)
                if live(weigh_g):
                    g = weigh_g
                    dve.wait_ge(q["top"], g + 1)
                    dve.tensor_tensor(arg[:, 0, :, :], me[:, :, :], top[:, :, :], ALU.subtract)
                    dve.tensor_tensor(arg[:, 1, :, :], L[:, :, :], top[:, :, :], ALU.subtract).then_inc(q["arg"], 1)
                if live(sum_g):
                    g, s = sum_g, half(par, 5)
                    dve.wait_ge(q["x1"], g + 1)
                    for k in range(K):
                        dve.bn_stats(bst1[:, k, :], x1[:, s, k, :]).then_inc(q["stats1"], 1)
                score_row(0)
                if live(weigh_g):
                    g, s4 = weigh_g, (par - 3) % 4
                    dve.wait_ge(q["ex"], g + 1)
                    dve.tensor_tensor(den[:, :, :], ex[:, 0, :, :], sums[:, s4, :, P:P + H], ALU.mult)\
                       .then_inc(q["soft"], 1)
                if live(sum_g):
                    g, s = sum_g, half(par, 5)
                    dve.wait_ge(q["stats1"], (g + 1) * K)
                    dve.sem_inc(v.tick, 1)
                    for k in range(K):
                        dve.bn_aggr(mv1[:, s, k, :], bst1[:, k, :]).then_inc(q["aggr1"], 1)
                if live(weigh_g):
                    g = weigh_g
                    dve.wait_ge(q["soft"], g * 5 + 3)
                    dve.tensor_tensor(den[:, :, :], den[:, :, :], ex[:, 1, :, :], ALU.add).then_inc(q["soft"], 1)
                if live(stats_g):
                    g = stats_g
                    dve.wait_ge(q["rstd"], g + 1)
                    wait(dve, q["h"], g)
                    dve.scalar_tensor_tensor(out=off[:, :], in0=mv[:, :, 0], scalar=-1.0, in1=rstd[:, :],
                                             op0=ALU.mult, op1=ALU.mult).then_inc(q["off"], 1)
                if live(weigh_g):
                    g = weigh_g
                    dve.wait_ge(q["soft"], g * 5 + 4)
                    dve.reciprocal(rden[:, :, :], den[:, :, :]).then_inc(q["soft"], 1)
                score_row(1)
                if live(weigh_g):
                    g, s = weigh_g, half(par, 3)
                    dve.wait_ge(q["soft"], g * 5 + 5)
                    wait(dve, q["fe"], g - 1)
                    dve.tensor_tensor(w[:, s, :, :, :].rearrange("p a k h -> p a (k h)"),
                                      ex[:, :, :, :].rearrange("p a k h -> p a (k h)"),
                                      rden[:, :, :].rearrange("p (a k) h -> p a (k h)", a=1).broadcast_to([P, 2, K * H]),
                                      ALU.mult).then_inc(q["w"], 1)
                if live(sum_g):
                    g, s = sum_g, half(par, 5)
                    dve.wait_ge(q["rstd1"], g + 1)
                    dve.scalar_tensor_tensor(out=off1[:, s, :], in0=mv1[:, s, :, 0], scalar=-1.0, in1=rstd1[:, s, :],
                                             op0=ALU.mult, op1=ALU.mult).then_inc(q["off1"], 1)
                if live(weigh_g):
                    g, s = weigh_g, half(par, 3)
                    dve.wait_ge(q["w"], g + 1)
                    dve.tensor_tensor(by_head(own[:, s, :, :]), by_head(ps_x[:, s, :, 0:P]), spread(w[:, s, 1, :, :]),
                                      ALU.mult).then_inc(q["own"], 1)
                score_row(2)
                score_row(3)

            staged4(dve, 6, body)

        @block.tensor
        def _(pe):
            def body(i, par):
                g = i - 2
                if live(g):
                    s = half(par, 2)
                    pe.wait_ge(q["h"], g + 1)
                    wait(pe, q["relu"], g)
                    for k in range(K):
                        last = pe.transpose(ps_z[:, k * P:(k + 1) * P], h[:, k, :], v.ident[:, :])
                    last.then_inc(q["zT"], 1)
                g = i - 4
                if live(g):
                    s, s4 = half(par, 4), par % 4
                    pe.wait_ge(x_in[s4], (g - s4) * 4 + 16)
                    wait(pe, q["x1"], g - 1)
                    pe.matmul(ps_rest[s][:, :], v.ident[:, :], x[:, s4, :, :].rearrange("p k d -> p (k d)"),
                              start=True, stop=False)
                    pe.wait_ge(q["fe"], g + 1)
                    pe.matmul(ps_rest[s][:, :], v.ident[:, :], fe[:, s, :, :].rearrange("p k d -> p (k d)"),
                              start=False, stop=True).then_inc(q["rest"], 1)
                g = i - 2
                if live(g):
                    s = half(par, 2)
                    pe.wait_ge(q["relu"], g + 1)
                    wait(pe, q["own"], g - 1)
                    wait(pe, q["raw"], g - 1)
                    for k in range(K):
                        for c in range(3):
                            pe.matmul(ps_x[:, s, k, 0:P + H], v.ones16[:, :], v.b_parts[:, c, :], start=c == 0, stop=False)
                        last = pe.matmul(ps_x[:, s, k, 0:P + H], hT[:, k * P:(k + 1) * P], v.w_ext[:, :],
                                         start=False, stop=True)
                    last.then_inc(q["xw"], 1)

            staged4(pe, 4, body)


def edges1(nc, v):
    f32, i32, ALU, ACT = v.f32, v.i32, v.ALU, v.ACT
    with ExitStack() as ctx:
        def sb(name, shape, dt=f32):
            return ctx.enter_context(nc.sbuf_tensor(name, shape, dt))

        def pb(name, shape):
            return ctx.enter_context(nc.psum_tensor(name, shape, f32))

        def sem(name):
            v.used.append(nc.alloc_semaphore(name))
            return v.used[-1]

        gi = sb("e1_gi", [P, 4, K, 2], i32)
        hg = sb("e1_hg", [P, 4, K, P])
        sg = sb("e1_sg", [P, 4, K])
        hT = sb("e1_hT", [P, 2, T])
        lin = sb("e1_lin", [P, 2, T])
        arg = sb("e1_arg", [P, K])
        ex = sb("e1_ex", [P, K])
        ex1 = sb("e1_ex1", [P, K])
        att = sb("e1_att", [P, 2, K])
        same = sb("e1_same", [1, 2, T], v.bf16)
        y = sb("e1_y", [P, T])
        S = sb("e1_S", [P, 2, T])
        row = sb("e1_row", [P, 2, K, P])
        node_h = sb("e1_node_h", [P, 2, K, P])
        node_hT = sb("e1_node_hT", [P, 2, T])
        ps_h, ps_m, ps_s, ps_c, ps_t, ps_r, ps_n = (pb(f"e1_ps{n}", [P, T]) for n in "hmsctrn")

        names = ("idx", "hT", "hTs", "s1", "msg", "lin", "arg", "ex", "ex1", "att", "bc", "y", "S", "back", "row", "nT", "nTs")
        q = {n: sem(f"e1_{n}") for n in names}
        got = [sem(f"e1_got{s}") for s in range(4)]
        same_in = [sem("e1_same_in0"), sem("e1_same_in1")]
        row_out = [sem("e1_row_out0"), sem("e1_row_out1")]
        node_in = [sem("e1_node_in0"), sem("e1_node_in1")]
        node_out = [sem("e1_node_out0"), sem("e1_node_out1")]
        block = ctx.enter_context(nc.Block())

        @block.gpsimd
        def _(pool):
            bound = pool.to_reg(N - 1)

            def body(i, par):
                g = i
                if live(g):
                    s = par
                    wait(pool, q["hT"], g - 3)
                    wait(pool, q["arg"], g - 3)
                    pool.wait_ge(q["idx"], g + 1)
                    pool.sem_inc(v.tick, 1)
                    for k in range(K):
                        for a, (out, table) in enumerate(((hg[:, s, k, :], v.h1_d), (sg[:, s, k:k + 1], v.s2_d))):
                            pool.indirect_dma_start(out=out, out_offset=None, in_=table[:, :],
                                                    in_offset=bass.IndirectOffsetOnAxis(ap=gi[:, s, k, a:a + 1], axis=0),
                                                    bounds_check=bound, oob_is_err=False).then_inc(got[s], 16)

            staged4(pool, 0, body)

        @block.sync
        def _(sp):
            def body(i, par, all_kept):
                g = i
                if live(g):
                    s = par % 2
                    wait(sp, q["bc"], g - 1)
                    sp.dma_start(same[:, s, :], v.same_d[bass.ds(g * T, T)].rearrange("(a n) -> a n", a=1))\
                      .then_inc(same_in[s], 16)
                    wait(sp, q["nT"], g - 1)
                    sp.dma_start(node_h[:, s, :, :], v.h1_d[bass.ds(node_rows(g), T), :]
                                 .rearrange("(p k) d -> p k d", k=K)).then_inc(node_in[s], 16)
                g = i - 2
                if live(g) and not is_kept(g, all_kept):
                    s = half(par, 2)
                    sp.wait_ge(q["nTs"], g + 1)
                    sp.sem_inc(v.tick, 1)
                    sp.dma_start(v.hT_d[:, bass.ds(g * T, T)], node_hT[:, s, :]).then_inc(node_out[s], 16)
                g = i - 3
                if live(g):
                    s = half(par, 3)
                    sp.wait_ge(q["row"], g + 1)
                    sp.dma_start(v.sums1[bass.ds(g * T, T), :].rearrange("(p k) d -> p k d", k=K), row[:, s, :, :])\
                      .then_inc(row_out[s], 16)

            staged_kept(sp, 3, body)
            for s in range(2):
                sp.wait_ge(row_out[s], NG // 2 * 16)
                sp.wait_ge(node_out[s], (NG - KEPT) // 2 * 16)

        @block.vector
        def _(dve):
            dve.memset(S[:, 1, T - 1:T], 0.0)
            dve.drain()

            def lay_indices(g, s4):
                if live(g):
                    wait(dve, got[s4], (g - s4) * (8 * K))
                    dve.tensor_copy(gi[:, s4, :, :], v.ends_idx[:, bass.ds(g * K, K), :]).then_inc(q["idx"], 1)

            lay_indices(0, 0)

            def body(i, par, all_kept):
                lay_indices(i + 1, (par + 1) % 4)
                g = i - 1
                if live(g):
                    s = half(par, 1)
                    dve.wait_ge(q["s1"], g + 1)
                    wait(dve, q["ex"], g)
                    dve.tensor_tensor(arg[:, :], ps_s[:, 0:K], sg[:, (par - 1) % 4, :], ALU.add).then_inc(q["arg"], 1)
                    dve.wait_ge(q["ex"], g + 1)
                    dve.tensor_scalar(ex1[:, :], ex[:, :], 1.0, None, ALU.add).then_inc(q["ex1"], 1)
                    wait(dve, q["bc"], g - 1)
                    dve.wait_ge(q["ex1"], g + 1)
                    dve.reciprocal(att[:, s, :], ex1[:, :]).then_inc(q["att"], 1)
                    dve.wait_ge(q["att"], g + 1)
                g = i - 2
                if live(g):
                    s = half(par, 2)
                    dve.wait_ge(q["bc"], g + 1)
                    dve.wait_ge(q["lin"], g + 1)
                    dve.tensor_tensor(y[:, :], lin[:, s, :], ps_t[:, :], ALU.mult).then_inc(q["y"], 1)
                    wait(dve, q["back"], g - 1)
                    dve.wait_ge(q["y"], g + 1)
                    dve.tensor_tensor_scan(S[:, s, :], ps_c[:, :], y[:, :], S[:, 1 - s, T - 1:T],
                                           ALU.mult, ALU.add).then_inc(q["S"], 1)
                    dve.wait_ge(q["S"], g + 1)
                g = i - 1
                if live(g):
                    s = half(par, 1)
                    dve.wait_ge(q["nT"], g + 1)
                    if is_kept(g, all_kept):
                        to = v.kept[:, bass.ds(g * T, T)]
                    else:
                        to = node_hT[:, s, :]
                        wait(dve, node_out[s], (g - KEPT - s) * 8)
                    dve.tensor_copy(to, ps_n[:, :]).then_inc(q["nTs"], 1)

            staged_kept(dve, 2, body)

        @block.scalar
        def _(act):
            act.preload_act_table_set("natural_log_exp_and_others")
            def body(i, par):
                g = i - 1
                if live(g):
                    s = half(par, 1)
                    act.wait_ge(q["hT"], g + 1)
                    wait(act, q["msg"], g - 1)
                    act.activation(hT[:, s, :], ps_h[:, :], ACT.Copy).then_inc(q["hTs"], 1)
                    act.wait_ge(q["arg"], g + 1)
                    wait(act, q["ex1"], g)
                    act.activation(ex[:, :], arg[:, :], ACT.Exp, scale=-1.0, bias=v.minus_b_att[:, :]).then_inc(q["ex"], 1)
                    act.wait_ge(q["msg"], g + 1)
                    wait(act, q["y"], g - 1)
                    act.activation(lin[:, s, :], ps_m[:, :], ACT.Identity, bias=v.b_msg[:, :]).then_inc(q["lin"], 1)
                g = i - 2
                if live(g):
                    s = half(par, 2)
                    act.wait_ge(q["back"], g + 1)
                    wait(act, row_out[s], (g - s) * 8)
                    act.activation(row[:, s, :, :].rearrange("p k d -> p (k d)"), ps_r[:, :], ACT.Copy).then_inc(q["row"], 1)

            staged4(act, 2, body)

        @block.tensor
        def _(pe):
            def body(i, par):
                g = i - 1
                if live(g):
                    s4 = (par - 1) % 4
                    pe.wait_ge(got[s4], (g - s4) * (8 * K) + 32 * K)
                    wait(pe, q["hTs"], g)
                    for k in range(K):
                        last = pe.transpose(ps_h[:, k * P:(k + 1) * P], hg[:, s4, k, :], v.ident[:, :])
                    last.then_inc(q["hT"], 1)
                g = i - 2
                if live(g):
                    s = half(par, 2)
                    pe.wait_ge(q["att"], g + 1)
                    pe.wait_ge(same_in[s], (g - s) * 8 + 16)
                    wait(pe, q["S"], g)
                    pe.matmul(ps_c[:, :], v.ones16[:, :], same[:, s, :], start=True, stop=True)
                    for k in range(K):
                        last = pe.matmul(ps_t[:, k * P:(k + 1) * P], att[:, s, k:k + 1].broadcast_to([P, P]),
                                         v.ident[:, :], start=True, stop=True)
                    last.then_inc(q["bc"], 1)
                g = i - 1
                if live(g):
                    s = half(par, 1)
                    pe.wait_ge(q["hTs"], g + 1)
                    wait(pe, q["arg"], g)
                    for k in range(K):
                        last = pe.matmul(ps_s[:, k:k + 1], hT[:, s, k * P:(k + 1) * P], v.w_att1[:, :], start=True, stop=True)
                    last.then_inc(q["s1"], 1)
                    wait(pe, q["lin"], g)
                    pe.matmul(ps_m[:, :], v.w_msg[:, :], hT[:, s, :], start=True, stop=True).then_inc(q["msg"], 1)
                    pe.wait_ge(node_in[s], (g - s) * 8 + 16)
                    wait(pe, q["nTs"], g)
                    for k in range(K):
                        last = pe.transpose(ps_n[:, k * P:(k + 1) * P], node_h[:, s, k, :], v.ident[:, :])
                    last.then_inc(q["nT"], 1)
                g = i - 2
                if live(g):
                    s = half(par, 2)
                    pe.wait_ge(q["S"], g + 1)
                    wait(pe, q["row"], g)
                    for k in range(K):
                        last = pe.transpose(ps_r[:, k * P:(k + 1) * P], S[:, s, k * P:(k + 1) * P], v.ident[:, :])
                    last.then_inc(q["back"], 1)

            staged4(pe, 2, body)


def nodes1(nc, v):
    f32, ALU, ACT = v.f32, v.ALU, v.ACT
    with ExitStack() as ctx:
        def sb(name, shape, dt=f32):
            return ctx.enter_context(nc.sbuf_tensor(name, shape, dt))

        def pb(name, shape):
            return ctx.enter_context(nc.psum_tensor(name, shape, f32))

        def sem(name):
            v.used.append(nc.alloc_semaphore(name))
            return v.used[-1]

        place = sb("n1_place", [P, 4, K], v.i32)
        a = sb("n1_a", [P, 4, K, P])
        hT = sb("n1_hT", [P, 4, T])
        aT = sb("n1_aT", [P, 2, T])
        r = sb("n1_r", [P, T])
        zg = sb("n1_zg", [P, 2, T])
        t1 = sb("n1_t1", [P, T])
        t2 = sb("n1_t2", [P, T])
        n = sb("n1_n", [P, 2, T])
        d = sb("n1_d", [P, T])
        e = sb("n1_e", [P, T])
        hn = sb("n1_hn", [P, 2, T])
        ps_a, ps_r, ps_z, ps_i, ps_n = (pb(f"n1_ps{c}", [P, T]) for c in "arzin")
        names = ("T", "aT", "gr", "gz", "gn", "r", "z", "t1", "t2", "n", "d", "e", "hn", "st")
        q = {c: sem(f"n1_{c}") for c in names}
        rows_in = [sem(f"n1_in{s}") for s in range(4)]
        got = [sem(f"n1_got{s}") for s in range(4)]
        place_in = [sem(f"n1_place_in{s}") for s in range(4)]
        out = [sem("n1_out0"), sem("n1_out1")]
        block = ctx.enter_context(nc.Block())
        def hT_of(g, s4, all_kept):
            return v.kept[:, bass.ds(g * T, T)] if is_kept(g, all_kept) else hT[:, s4, :]

        def hn_of(g, s, all_kept):
            return v.kept[:, bass.ds(g * T, T)] if is_kept(g, all_kept) else hn[:, s, :]


        @block.sync
        def _(sp):
            def body(i, par, all_kept):
                g = i
                if live(g):
                    s = par
                    wait(sp, got[s], (g - s) * (4 * K))
                    sp.sem_inc(v.tick, 1)
                    sp.dma_start(place[:, s, :], v.place_d[bass.ds(node_rows(g), T), :]
                                 .rearrange("(p k) a -> p (k a)", k=K)).then_inc(place_in[s], 16)
                    if not is_kept(g, all_kept):
                        wait(sp, q["gz"], g - 3)
                        wait(sp, q["d"], g - 3)
                        sp.sem_inc(v.tick, 1)
                        sp.dma_start(hT[:, s, :], v.hT_d[:, bass.ds(g * T, T)]).then_inc(rows_in[s], 16)
                g = i - 5
                if live(g) and not is_kept(g, all_kept):
                    s = half(par, 5)
                    sp.wait_ge(q["hn"], g + 1)
                    sp.dma_start(v.hn_d[:, bass.ds(g * T, T)], hn[:, s, :]).then_inc(out[s], 16)

            staged_kept(sp, 5, body)
            for s in range(2):
                sp.wait_ge(out[s], (NG - KEPT) // 2 * 16)

        @block.tensor
        def _(pe):
            def body(i, par, all_kept):
                g = i - 3
                if live(g):
                    s = (par - 3) % 4
                    pe.wait_ge(got[s], (g - s) * (4 * K) + 16 * K)
                    wait(pe, q["aT"], g)
                    for k in range(K):
                        last = pe.transpose(ps_a[:, k * P:(k + 1) * P], a[:, s, k, :], v.ident[:, :])
                    last.then_inc(q["T"], 1)
                g = i - 4
                if live(g):
                    s, s4 = half(par, 4), (par - 4) % 4
                    pe.wait_ge(q["aT"], g + 1)
                    if not is_kept(g, all_kept):
                        pe.wait_ge(rows_in[s4], (g - KEPT - s4) * 4 + 16)
                    h = hT_of(g, s4, all_kept)
                    wait(pe, q["r"], g)
                    pe.matmul(ps_r[:, :], v.w_hhT[:, 0:P], h, start=True, stop=False)
                    pe.matmul(ps_r[:, :], v.w_ihT[:, 0:P], aT[:, s, :], start=False, stop=True).then_inc(q["gr"], 1)
                    wait(pe, q["t2"], g)
                    pe.matmul(ps_n[:, :], v.w_hhT[:, 2 * P:3 * P], h, start=True, stop=True)
                    pe.matmul(ps_i[:, :], v.w_ihT[:, 2 * P:3 * P], aT[:, s, :], start=True, stop=True).then_inc(q["gn"], 1)
                    wait(pe, q["z"], g)
                    pe.matmul(ps_z[:, :], v.w_hhT[:, P:2 * P], h, start=True, stop=False)
                    pe.matmul(ps_z[:, :], v.w_ihT[:, P:2 * P], aT[:, s, :], start=False, stop=True).then_inc(q["gz"], 1)

            staged_kept(pe, 4, body)

        @block.scalar
        def _(act):
            act.preload_act_table_set("sigmoid_and_others")
            def body(i, par):
                g = i - 3
                if live(g):
                    s = half(par, 3)
                    act.wait_ge(q["T"], g + 1)
                    wait(act, q["gz"], g - 1)
                    act.activation(aT[:, s, :], ps_a[:, :], ACT.Copy).then_inc(q["aT"], 1)
                g = i - 4
                if live(g):
                    s = half(par, 4)
                    act.wait_ge(q["gr"], g + 1)
                    wait(act, q["t1"], g)
                    act.activation(r[:, :], ps_r[:, :], ACT.Sigmoid, bias=v.b_gate[:, 0:1]).then_inc(q["r"], 1)
                    act.wait_ge(q["gz"], g + 1)
                    wait(act, q["e"], g - 1)
                    act.activation(zg[:, s, :], ps_z[:, :], ACT.Sigmoid, bias=v.b_gate[:, 1:2]).then_inc(q["z"], 1)
                    act.wait_ge(q["t2"], g + 1)
                    wait(act, q["hn"], g - 1)
                    act.activation(n[:, s, :], t2[:, :], ACT.Tanh, bias=v.b_ih[:, 2:3]).then_inc(q["n"], 1)

            staged4(act, 4, body)

        @block.vector
        def _(dve):
            def body(i, par, all_kept):
                g = i - 4
                if live(g):
                    dve.wait_ge(q["gn"], g + 1)
                    dve.wait_ge(q["r"], g + 1)
                    dve.scalar_tensor_tensor(out=t1[:, :], in0=ps_n[:, :], scalar=v.b_hh[:, 2:3], in1=r[:, :],
                                             op0=ALU.add, op1=ALU.mult).then_inc(q["t1"], 1)
                    dve.wait_ge(q["t1"], g + 1)
                    wait(dve, q["n"], g)
                    dve.tensor_tensor(t2[:, :], t1[:, :], ps_i[:, :], ALU.add).then_inc(q["t2"], 1)
                g = i - 5
                if live(g):
                    s = half(par, 5)
                    dve.wait_ge(q["e"], g + 1)
                    if not is_kept(g, all_kept):
                        wait(dve, out[s], (g - KEPT - s) * 8)
                    dve.tensor_tensor(hn_of(g, s, all_kept), e[:, :], n[:, s, :], ALU.add).then_inc(q["hn"], 1)
                g = i - 4
                if live(g):
                    s, s4 = half(par, 4), (par - 4) % 4
                    dve.wait_ge(q["n"], g + 1)
                    dve.tensor_tensor(d[:, :], hT_of(g, s4, all_kept), n[:, s, :], ALU.subtract).then_inc(q["d"], 1)
                g = i - 5
                if live(g):
                    s = half(par, 5)
                    dve.wait_ge(q["hn"], g + 1)
                    lo = FRESH if isinstance(g, int) and g == NG - 1 else 0
                    part = hn_of(g, s, all_kept).rearrange("p (k n) -> p k n", k=K)[:, :, lo:P]
                    dve.bn_stats(v.stats[:, bass.ds(g, 1), :], part).then_inc(q["st"], 1)
                g = i - 4
                if live(g):
                    s = half(par, 4)
                    dve.wait_ge(q["z"], g + 1)
                    dve.wait_ge(q["d"], g + 1)
                    wait(dve, q["hn"], g)
                    dve.tensor_tensor(e[:, :], d[:, :], zg[:, s, :], ALU.mult).then_inc(q["e"], 1)

            staged_kept(dve, 5, body)

        @block.gpsimd
        def _(pool):
            bound = pool.to_reg(EMPTY)

            def body(i, par):
                g = i - 1
                if live(g):
                    s = (par - 1) % 4
                    wait(pool, q["T"], g - 3)
                    pool.wait_ge(place_in[s], (g - s) * 4 + 16)
                    pool.sem_inc(v.tick, 1)
                    for k in range(K):
                        pool.indirect_dma_start(out=a[:, s, k, :], out_offset=None, in_=v.sums1[:, :],
                                                in_offset=bass.IndirectOffsetOnAxis(ap=place[:, s, k:k + 1], axis=0),
                                                bounds_check=bound, oob_is_err=False).then_inc(got[s], 16)

            staged4(pool, 1, body)


def finish(nc, v):
    f32, ALU, ACT = v.f32, v.ALU, v.ACT
    with ExitStack() as ctx:
        def sb(name, shape, dt=f32):
            return ctx.enter_context(nc.sbuf_tensor(name, shape, dt))

        def sem(name):
            v.used.append(nc.alloc_semaphore(name))
            return v.used[-1]

        mv = sb("f_mv", [P, 2])
        sd = sb("f_sd", [P, 1])
        rs = sb("f_rs", [P, 1])
        scale = sb("f_scale", [P, 1])
        ms = sb("f_ms", [P, 1])
        shift = sb("f_shift", [P, 1])
        hn = sb("f_hn", [P, 4, T])
        x1 = sb("f_x1", [P, 4, K, P])
        bn = sb("f_bn", [P, 4, T])
        o = sb("f_o", [P, 4, K, P])
        ps = [ctx.enter_context(nc.psum_tensor(f"f_ps{s}", [P, T], f32)) for s in range(4)]
        chain, ready = sem("f_chain"), sem("f_ready")
        bn_done, T_done, o_done, sd_done, sd_in = sem("f_bn_done"), sem("f_T_done"), sem("f_o_done"), sem("f_sd_done"), sem("f_sd_in")
        hn_in = [sem(f"f_hn_in{s}") for s in range(4)]
        x1_in = [sem(f"f_x1_in{s}") for s in range(4)]
        out = [sem(f"f_out{s}") for s in range(4)]
        block = ctx.enter_context(nc.Block())

        def group(dram, g):
            return dram[bass.ds(node_rows(g), T), :].rearrange("(p k) d -> p k d", k=K)

        @block.sync
        def _(sp):
            def body(i, par, all_kept):
                g = i - 4
                if live(g):
                    s = par
                    at = FRESH if isinstance(g, int) and g == NG - 1 else 0
                    sp.wait_ge(o_done, g + 1)
                    sp.sem_inc(v.tick, 1)
                    sp.dma_start(group(v.out_d, g)[at:P], o[at:P, s, :, :]).then_inc(out[s], 16)
                g = i
                if live(g):
                    s = par
                    wait(sp, bn_done, g - 3)
                    wait(sp, o_done, g - 3)
                    sp.sem_inc(v.tick, 1)
                    if not is_kept(g, all_kept):
                        sp.dma_start(hn[:, s, :], v.hn_d[:, bass.ds(g * T, T)]).then_inc(hn_in[s], 16)
                    sp.dma_start(x1[:, s, :, :], group(v.x1_d, g)).then_inc(x1_in[s], 16)

            staged_kept(sp, 4, body)
            for s in range(4):
                sp.wait_ge(out[s], (NG - s + 3) // 4 * 16)

        @block.scalar
        def _(act):
            act.wait_ge(sd_in, 1)
            act.activation(sd[:, :], mv[:, 1:2], ACT.Sqrt, bias=v.eps[:, :]).then_inc(sd_done, 1)
            act.wait_ge(ready, 1)

            def body(i, par, all_kept):
                g = i - 2
                if live(g):
                    s = (par - 2) % 4
                    if is_kept(g, all_kept):
                        new = v.kept[:, bass.ds(g * T, T)]
                    else:
                        new = hn[:, s, :]
                        act.wait_ge(hn_in[s], (g - KEPT - s) * 4 + 16)
                    wait(act, T_done, g - 3)
                    act.activation(bn[:, s, :], new, ACT.Identity, bias=shift[:, :], scale=scale[:, :])\
                       .then_inc(bn_done, 1)

            staged_kept(act, 2, body)

        @block.vector
        def _(dve):
            links = [0]

            def link(ins):
                links[0] += 1
                ins.then_inc(chain, 1)
                dve.wait_ge(chain, links[0])

            dve.bn_aggr(mv[:, :], v.stats[:, :, :].rearrange("p g s -> p (g s)")).then_inc(sd_in, 1)
            dve.wait_ge(sd_in, 1)
            dve.wait_ge(sd_done, 1)
            link(dve.reciprocal(rs[:, :], sd[:, :]))
            link(dve.tensor_tensor(scale[:, :], rs[:, :], v.gamma[:, :], ALU.mult))
            link(dve.tensor_tensor(ms[:, :], mv[:, 0:1], scale[:, :], ALU.mult))
            dve.tensor_tensor(shift[:, :], v.beta[:, :], ms[:, :], ALU.subtract).then_inc(ready, 1)

            def body(i, par):
                g = i - 3
                if live(g):
                    s = (par - 3) % 4
                    dve.wait_ge(T_done, g + 1)
                    dve.wait_ge(x1_in[s], (g - s) * 4 + 16)
                    wait(dve, out[s], (g - s) * 4)
                    dve.tensor_tensor(o[:, s, :, :].rearrange("p k d -> p (k d)"), ps[s][:, :],
                                      x1[:, s, :, :].rearrange("p k d -> p (k d)"), ALU.add).then_inc(o_done, 1)

            staged4(dve, 3, body)

        @block.tensor
        def _(pe):
            def body(i, par):
                g = i - 3
                if live(g):
                    s = (par - 3) % 4
                    pe.wait_ge(bn_done, g + 1)
                    wait(pe, o_done, g - 3)
                    for k in range(K):
                        last = pe.transpose(ps[s][:, k * P:(k + 1) * P], bn[:, s, k * P:(k + 1) * P], v.ident[:, :])
                    last.then_inc(T_done, 1)

            staged4(pe, 3, body)


_INS = ["x", "src", "dst", "L0_gnn_W", "L0_gnn_b_lin", "L0_gnn_alpha", "L0_gnn_bias", "L1_gnn_W_msg", "L1_gnn_b_msg",
        "L1_gnn_W_att", "L1_gnn_b_att", "L1_gnn_W_ih", "L1_gnn_b_ih", "L1_gnn_W_hh", "L1_gnn_b_hh", "L1_gnn_gamma",
        "L1_gnn_beta"]
_SCRATCH = {"sums0": (EMPTY + 1, ROW), "sums1": (EMPTY + 1, P), "x1": (N, P), "h1": (N, P), "s2": (N, 1), "same": (NT * P,),
            "start": (NT * P,), "hnew": (P, NG * T),
            "h1T": (P, NG * T)}
DEBUG = False


def kernel(**inputs):
    import numpy as np
    import concourse.bacc as bacc
    from concourse.bass_utils import run_bass_kernel_spmd

    nc = bacc.Bacc("TRN2", target_bir_lowering=False, num_devices=1)
    arrays, io = {}, {}
    for name in _INS:
        a = np.ascontiguousarray(inputs[name])
        arrays[f"in_{name}"] = a
        io[name] = nc.dram_tensor(f"in_{name}", a.shape, mybir.dt.from_np(a.dtype), kind="ExternalInput").ap()
    io["out"] = nc.dram_tensor("out", (N, P), mybir.dt.float32, kind="ExternalOutput").ap()
    kind = "ExternalOutput" if DEBUG else "Internal"
    scratch = {n: nc.dram_tensor(f"scratch_{n}", (E, 1), mybir.dt.int32, kind="Internal").ap() for n in ("src_s", "dst_s", "place")}
    scratch |= {n: nc.dram_tensor(f"scratch_{n}", s, mybir.dt.bfloat16 if n in ("same", "start") else mybir.dt.float32,
                                  kind=kind).ap() for n, s in _SCRATCH.items()}
    build(nc, io, scratch)
    r = run_bass_kernel_spmd(nc, [arrays], core_ids=[0])
    return r.results[0]["out"]
```
